# Optimizing a Trainium2 kernel written in Bass

```python
import numpy as np
import jax
import jax.numpy as jnp

def _softmax(x, axis=-1):
    return jax.nn.softmax(x, axis=axis)

def _gelu(x):
    return jax.nn.gelu(x, approximate=True)

def _silu(x):
    return jax.nn.silu(x)

def _sigmoid(x):
    return jax.nn.sigmoid(x)

def _layernorm(x, axis=-1, eps=1e-05):
    m = jnp.mean(x, axis=axis, keepdims=True)
    v = jnp.var(x, axis=axis, keepdims=True)
    return (x - m) / jnp.sqrt(v + eps)

def _scatter_add(tgt, idx, src, axis=0):
    return tgt.at[idx].add(src)

def _segment_sum(src, seg, n):
    return jax.ops.segment_sum(src, seg, n)
kernel_name = 'mk_flamingo_gated_d2_seqx_r8_7586e9'

def setup_inputs(seed: int=0):
    np.random.seed(seed)
    _w = jnp.asarray

    def _rec_inputs():
        import jax
        import jax.numpy as jnp
        _rk = jax.random.key(seed)
        x = 7.22e-05 + 1 * jax.random.normal(jax.random.fold_in(_rk, 1), (64, 64, 256), jnp.float32)
        _lenS = 64 - jax.random.randint(jax.random.fold_in(_rk, 7), (64,), 0, max(1, 64 // 4) + 1, jnp.int32)
        _lenS2 = 64 - jax.random.randint(jax.random.fold_in(_rk, 8), (64,), 0, max(1, 64 // 4) + 1, jnp.int32)
        _ctx_512P = jax.random.normal(jax.random.fold_in(_rk, 11), (64, 16, 64), jnp.float32)
        _ctx_512c = jax.random.dirichlet(jax.random.fold_in(_rk, 511), 0.3 * jnp.ones((16,), jnp.float32), (64, 64))
        _ctx_512t = jnp.einsum('bsk,bkd->bsd', _ctx_512c, _ctx_512P)
        _ctx_512t = _ctx_512t * jax.lax.rsqrt(jnp.mean(jnp.square(_ctx_512t)) + 1e-12) * 0.953939
        ctx_512 = -0.000514642 + 1.00011 * (_ctx_512t + 0.3 * jax.random.normal(jax.random.fold_in(_rk, 611), (64, 64, 64), jnp.float32))
        _g = jax.random.normal(jax.random.fold_in(_rk, 9001), (2, 2), jnp.float32)
        _g = jnp.sign(_g) * jnp.maximum(jnp.abs(_g), 1.0) + (_g == 0) * 1.0
        g_xattn = _g[0]
        g_ffn = _g[1]
        return (x, ctx_512, g_xattn, g_ffn)
    x, ctx_512, g_xattn, g_ffn = _rec_inputs()

    def _L0_xattn_setup():
        import jax, jax.numpy as jnp
        import numpy as np
        import math
        NUM_Q_HEADS = 32
        NUM_KV_HEADS = 8
        key = jax.random.key(seed)
        k1, k2, k3 = jax.random.split(key, 3)
        B, S, E = (2, 256, 256)
        kv_E = NUM_KV_HEADS * (E // NUM_Q_HEADS)
        q = jax.random.normal(k1, (B, S, E), dtype=jnp.float32)
        k = jax.random.normal(k2, (B, S, kv_E), dtype=jnp.float32)
        v = jax.random.normal(k3, (B, S, kv_E), dtype=jnp.float32)
        return {'q': q, 'k': k, 'v': v}
    _L0_xattn_all = _L0_xattn_setup()
    _L0_xattn_in = {k: v for k, v in _L0_xattn_all.items() if k in ()}
    del _L0_xattn_all

    def _L0_ffn_setup():
        import jax, jax.numpy as jnp
        import numpy as np
        D_MODEL = 256
        HIDDEN = 4 * D_MODEL
        B, S = (2, 512)

        def bit_linear(x, w, b):
            gamma_x = jnp.clip(jnp.max(jnp.abs(x), axis=-1, keepdims=True), 1e-05, None)
            scale_x = 127.0 / gamma_x
            x_dq = jnp.clip(jnp.round(x * scale_x), -128.0, 127.0) / scale_x
            x_ste = x + jax.lax.stop_gradient(x_dq - x)
            gamma_w = jnp.clip(jnp.mean(jnp.abs(w)), 1e-05, None)
            w_dq = jnp.clip(jnp.round(w / gamma_w), -1.0, 1.0) * gamma_w
            w_ste = w + jax.lax.stop_gradient(w_dq - w)
            return jnp.einsum('bsd,hd->bsh', x_ste, w_ste) + b
        key = jax.random.key(seed)
        ks = jax.random.split(key, 7)
        std = 0.02
        return {'x': jax.random.normal(ks[0], (B, S, D_MODEL), dtype=jnp.float32), 'gate_w': jax.random.normal(ks[1], (HIDDEN, D_MODEL), dtype=jnp.float32) * std, 'gate_b': jnp.zeros((HIDDEN,), dtype=jnp.float32), 'val_w': jax.random.normal(ks[2], (HIDDEN, D_MODEL), dtype=jnp.float32) * std, 'val_b': jnp.zeros((HIDDEN,), dtype=jnp.float32), 'out_w': jax.random.normal(ks[3], (D_MODEL, HIDDEN), dtype=jnp.float32) * std, 'out_b': jnp.zeros((D_MODEL,), dtype=jnp.float32)}
    _L0_ffn_all = _L0_ffn_setup()
    _L0_ffn_in = {k: v for k, v in _L0_ffn_all.items() if k in ('gate_w', 'gate_b', 'val_w', 'val_b', 'out_w', 'out_b')}
    del _L0_ffn_all

    def _L1_xattn_setup():
        import jax, jax.numpy as jnp
        import numpy as np
        B, S, L = (2, 128, 128)
        DIM_Q, H, K, D_C, D_CQ, R = (256, 16, 128, 64, 192, 64)

        def _rope_tables(seq_len, dim, dtype):
            inv_freq = 1.0 / 10000.0 ** (jnp.arange(0, dim, 2, dtype=dtype) / dim)
            t = jnp.arange(seq_len, dtype=dtype)
            freqs = t[:, None] * inv_freq[None, :]
            sin = jnp.repeat(jnp.sin(freqs), 2, axis=-1)
            cos = jnp.repeat(jnp.cos(freqs), 2, axis=-1)
            return (sin, cos)

        def _rotate_half(x):
            h = x.shape[-1] // 2
            return jnp.concatenate([-x[..., h:], x[..., :h]], axis=-1)
        key = jax.random.key(seed)
        ks = jax.random.split(key, 8)
        s_in = 1.0 / np.sqrt(DIM_Q)
        s_k = 1.0 / np.sqrt(K)
        s_cq = 1.0 / np.sqrt(D_CQ)
        s_c = 1.0 / np.sqrt(D_C)
        return {'hidden_q': jax.random.normal(ks[0], (B, S, DIM_Q), jnp.float32), 'kv_c': jax.random.normal(ks[1], (B, L, D_C), jnp.float32), 'Wq': jax.random.normal(ks[2], (H * K, DIM_Q), jnp.float32) * s_in, 'w_kc_q': jax.random.normal(ks[3], (H, K, D_CQ), jnp.float32) * s_k, 'w_kc_kv': jax.random.normal(ks[4], (H, K, D_C), jnp.float32) * s_k, 'W_qr': jax.random.normal(ks[5], (H, D_CQ, R), jnp.float32) * s_cq / np.sqrt(R), 'W_kr': jax.random.normal(ks[6], (H, D_C, R), jnp.float32) * s_c, 'Wo': jax.random.normal(ks[7], (DIM_Q, H * K), jnp.float32) * s_k}
    _L1_xattn_all = _L1_xattn_setup()
    _L1_xattn_in = {k: v for k, v in _L1_xattn_all.items() if k in ('Wq', 'w_kc_q', 'w_kc_kv', 'W_qr', 'W_kr', 'Wo')}
    del _L1_xattn_all

    def _L1_ffn_setup():
        import jax, jax.numpy as jnp
        import numpy as np
        E, TOP_K, D, H = (8, 2, 256, 176)
        B, S = (2, 256)
        key = jax.random.key(seed)
        ks = jax.random.split(key, 8)
        x = jax.random.normal(ks[0], (B, S, D), dtype=jnp.float32)
        gate_w = jax.random.normal(ks[1], (E, D), dtype=jnp.float32) * (1.0 / np.sqrt(D))
        gate_b = jax.random.normal(ks[2], (E,), dtype=jnp.float32) * 0.01
        bias = jnp.zeros((E,), dtype=jnp.float32)
        w1 = jax.random.normal(ks[3], (E, H, D), dtype=jnp.float32) * (1.0 / np.sqrt(D))
        b1 = jax.random.normal(ks[4], (E, H), dtype=jnp.float32) * 0.01
        w2 = jax.random.normal(ks[5], (E, D, H), dtype=jnp.float32) * (1.0 / np.sqrt(H))
        b2 = jax.random.normal(ks[6], (E, D), dtype=jnp.float32) * 0.01
        return {'x': x, 'gate_w': gate_w, 'gate_b': gate_b, 'bias': bias, 'w1': w1, 'b1': b1, 'w2': w2, 'b2': b2}
    _L1_ffn_all = _L1_ffn_setup()
    _L1_ffn_in = {k: v for k, v in _L1_ffn_all.items() if k in ('gate_w', 'gate_b', 'bias', 'w1', 'b1', 'w2', 'b2')}
    del _L1_ffn_all
    return {'x': x, 'ctx_512': ctx_512, 'g_xattn': g_xattn, 'g_ffn': g_ffn, 'L0_ffn_gate_w': _L0_ffn_in['gate_w'], 'L0_ffn_gate_b': _L0_ffn_in['gate_b'], 'L0_ffn_val_w': _L0_ffn_in['val_w'], 'L0_ffn_val_b': _L0_ffn_in['val_b'], 'L0_ffn_out_w': _L0_ffn_in['out_w'], 'L0_ffn_out_b': _L0_ffn_in['out_b'], 'L1_xattn_Wq': _L1_xattn_in['Wq'], 'L1_xattn_w_kc_q': _L1_xattn_in['w_kc_q'], 'L1_xattn_w_kc_kv': _L1_xattn_in['w_kc_kv'], 'L1_xattn_W_qr': _L1_xattn_in['W_qr'], 'L1_xattn_W_kr': _L1_xattn_in['W_kr'], 'L1_xattn_Wo': _L1_xattn_in['Wo'], 'L1_ffn_gate_w': _L1_ffn_in['gate_w'], 'L1_ffn_gate_b': _L1_ffn_in['gate_b'], 'L1_ffn_bias': _L1_ffn_in['bias'], 'L1_ffn_w1': _L1_ffn_in['w1'], 'L1_ffn_b1': _L1_ffn_in['b1'], 'L1_ffn_w2': _L1_ffn_in['w2'], 'L1_ffn_b2': _L1_ffn_in['b2']}

def reference(x, ctx_512, g_xattn, g_ffn, L0_ffn_gate_w, L0_ffn_gate_b, L0_ffn_val_w, L0_ffn_val_b, L0_ffn_out_w, L0_ffn_out_b, L1_xattn_Wq, L1_xattn_w_kc_q, L1_xattn_w_kc_kv, L1_xattn_W_qr, L1_xattn_W_kr, L1_xattn_Wo, L1_ffn_gate_w, L1_ffn_gate_b, L1_ffn_bias, L1_ffn_w1, L1_ffn_b1, L1_ffn_w2, L1_ffn_b2):
    import jax
    import jax.numpy as jnp

    def _L0_xattn_ref(q, k, v):
        import jax, jax.numpy as jnp
        import numpy as np
        import math
        NUM_Q_HEADS = 32
        NUM_KV_HEADS = 8
        B, S, E = q.shape
        H, KV = (NUM_Q_HEADS, NUM_KV_HEADS)
        D = E // H
        G = H // KV
        scale = math.sqrt(D)
        qh = q.reshape(B, S, KV, G, D).transpose(0, 2, 3, 1, 4)
        kh = k.reshape(B, S, KV, D).transpose(0, 2, 1, 3)
        vh = v.reshape(B, S, KV, D).transpose(0, 2, 1, 3)
        scores = jnp.einsum('bkgsd,bktd->bkgst', qh, kh) / scale
        weights = jax.nn.softmax(scores, axis=-1)
        out = jnp.einsum('bkgst,bktd->bkgsd', weights, vh)
        return out.transpose(0, 3, 1, 2, 4).reshape(B, S, E)

    def _L0_ffn_ref(x, gate_w, gate_b, val_w, val_b, out_w, out_b):
        import jax, jax.numpy as jnp
        import numpy as np
        D_MODEL = 256
        HIDDEN = 4 * D_MODEL
        B, S = (2, 512)

        def bit_linear(x, w, b):
            gamma_x = jnp.clip(jnp.max(jnp.abs(x), axis=-1, keepdims=True), 1e-05, None)
            scale_x = 127.0 / gamma_x
            x_dq = jnp.clip(jnp.round(x * scale_x), -128.0, 127.0) / scale_x
            x_ste = x + jax.lax.stop_gradient(x_dq - x)
            gamma_w = jnp.clip(jnp.mean(jnp.abs(w)), 1e-05, None)
            w_dq = jnp.clip(jnp.round(w / gamma_w), -1.0, 1.0) * gamma_w
            w_ste = w + jax.lax.stop_gradient(w_dq - w)
            return jnp.einsum('bsd,hd->bsh', x_ste, w_ste) + b
        gate = jax.nn.silu(bit_linear(x, gate_w, gate_b))
        val = bit_linear(x, val_w, val_b)
        return bit_linear(gate * val, out_w, out_b)

    def _L1_xattn_ref(hidden_q, kv_c, Wq, w_kc_q, w_kc_kv, W_qr, W_kr, Wo):
        import jax, jax.numpy as jnp
        import numpy as np
        B, S, L = (2, 128, 128)
        DIM_Q, H, K, D_C, D_CQ, R = (256, 16, 128, 64, 192, 64)

        def _rope_tables(seq_len, dim, dtype):
            inv_freq = 1.0 / 10000.0 ** (jnp.arange(0, dim, 2, dtype=dtype) / dim)
            t = jnp.arange(seq_len, dtype=dtype)
            freqs = t[:, None] * inv_freq[None, :]
            sin = jnp.repeat(jnp.sin(freqs), 2, axis=-1)
            cos = jnp.repeat(jnp.cos(freqs), 2, axis=-1)
            return (sin, cos)

        def _rotate_half(x):
            h = x.shape[-1] // 2
            return jnp.concatenate([-x[..., h:], x[..., :h]], axis=-1)
        b, s, _ = hidden_q.shape
        l = kv_c.shape[1]
        q_hk = (hidden_q @ Wq.T).reshape(b, s, H, K)
        q_big = jnp.einsum('bshk,hkq->bshq', q_hk, w_kc_q)
        sin, cos = _rope_tables(l, D_C, kv_c.dtype)
        kv_rope = kv_c * cos[None] + _rotate_half(kv_c) * sin[None]
        q_r = jnp.einsum('bshq,hqr->bhsr', q_big, W_qr)
        k_r = jnp.einsum('bld,hdr->bhlr', kv_rope, W_kr)
        scores = jnp.einsum('bhsr,bhlr->bhsl', q_r, k_r)
        attn = jax.nn.softmax(scores, axis=-1)
        ctx_c = jnp.einsum('bhsl,bld->bhsd', attn, kv_rope)
        ctx_lat = jnp.einsum('bhsd,hkd->bshk', ctx_c, w_kc_kv)
        out = ctx_lat.reshape(b, s, H * K) @ Wo.T
        return out

    def _L1_ffn_ref(x, gate_w, gate_b, bias, w1, b1, w2, b2):
        import jax, jax.numpy as jnp
        import numpy as np
        E, TOP_K, D, H = (8, 2, 256, 176)
        B, S = (2, 256)
        b, s, d = x.shape
        xf = x.reshape(-1, d)
        scores = xf @ gate_w.T + gate_b + bias
        top_scores, top_idx = jax.lax.top_k(scores, TOP_K)
        gates = jax.nn.softmax(top_scores, axis=-1)
        comb = jnp.sum(jax.nn.one_hot(top_idx, E, dtype=gates.dtype) * gates[..., None], axis=1)
        h = jax.nn.silu(jnp.einsum('td,ehd->teh', xf, w1) + b1)
        y = jnp.einsum('teh,edh->ted', h, w2) + b2
        out = jnp.einsum('ted,te->td', y, comb)
        return out.reshape(b, s, d)
    x = x + jnp.tanh(g_xattn[0]) * _L0_xattn_ref(_layernorm(x, axis=-1), ctx_512, ctx_512)
    x = x + jnp.tanh(g_ffn[0]) * _L0_ffn_ref(_layernorm(x, axis=-1), L0_ffn_gate_w, L0_ffn_gate_b, L0_ffn_val_w, L0_ffn_val_b, L0_ffn_out_w, L0_ffn_out_b)
    x = x + jnp.tanh(g_xattn[1]) * _L1_xattn_ref(_layernorm(x, axis=-1), ctx_512, L1_xattn_Wq, L1_xattn_w_kc_q, L1_xattn_w_kc_kv, L1_xattn_W_qr, L1_xattn_W_kr, L1_xattn_Wo)
    x = x + jnp.tanh(g_ffn[1]) * _L1_ffn_ref(_layernorm(x, axis=-1), L1_ffn_gate_w, L1_ffn_gate_b, L1_ffn_bias, L1_ffn_w1, L1_ffn_b1, L1_ffn_w2, L1_ffn_b2)
    return x

_drawn_inputs = setup_inputs


def setup_inputs(seed=0):
    import zlib

    import numpy as np

    out = dict(_drawn_inputs(seed))
    spreads = {'g_ffn': (-1.0, 0.6),
     'L0_ffn_gate_b': (0.0, 0.8),
     'L0_ffn_val_b': (0.0, 0.8),
     'L0_ffn_out_b': (0.0, 0.1),
     'L1_ffn_bias': (0.0, 0.278)}
    factors = {'L0_ffn_gate_w': 5.409,
     'L0_ffn_val_w': 5.097,
     'L0_ffn_out_w': 5.278,
     'L1_ffn_gate_b': 5.128,
     'L1_ffn_b1': 36.009,
     'L1_ffn_b2': 22.073}
    for name, (base, spread) in spreads.items():
        noise = np.random.default_rng([zlib.crc32(name.encode()), seed]).standard_normal(out[name].shape)
        drawn = base * np.exp(spread * noise) if base else spread * noise
        out[name] = jnp.asarray(drawn.astype(out[name].dtype))
    for name, factor in factors.items():
        out[name] = (out[name] * factor).astype(out[name].dtype)
    return out
```

```python
from contextlib import ExitStack

import numpy as np

import concourse.bass as bass
from concourse import mybir

ALU = mybir.AluOpType
ACT = mybir.ActivationFunctionType
AX = mybir.AxisListType
F32 = mybir.dt.float32
F16 = mybir.dt.float16
BF16 = mybir.dt.bfloat16

P = 128
BATCH, SEQ, D = 64, 64, 256
TILES = BATCH * SEQ // P
CD = 64
EPS = 1e-5
HID = 1024
HEADS1 = 16
KD, CQ, RR = 128, 192, 64
PAIRS1 = HEADS1 // 2
EXPERTS, EH = 8, 176
EB = EXPERTS * EH // P
ROUND0 = 1536.0
MAGIC = float(2 ** 23 + 0x6600)
BIG = float(1.5 * 2 ** 23)


def tiles_loop(eng, depth, stages):
    def iteration(n, parity, static):
        for lag, stage in stages:
            t = n - lag
            if static and not 0 <= t < TILES:
                continue
            stage(t, (parity - lag) % 2, (not static) or t >= 2)

    first = depth + 2 + depth % 2
    for n in range(first):
        iteration(n, n % 2, True)
    with eng.Fori(first, TILES - 1, 2) as n:
        iteration(n, 0, False)
        iteration(n + 1, 1, False)
    for n in range(TILES, TILES + depth):
        iteration(n, n % 2, True)


def build(nc, d, out, last_phase=4):
    with ExitStack() as ctx:
        def sb(name, shape, dt=F32):
            return ctx.enter_context(nc.sbuf_tensor(name, shape, dt))

        def sem(name):
            return ctx.enter_context(nc.semaphore(name))

        xs = sb("xs", [P, TILES, D])
        ctx2 = sb("ctx2", [P, BATCH, CD])
        kTp = sb("kTp", [P, TILES, SEQ])
        gT = sb("gT", [P, 4])
        graw = sb("graw", [P, 4])
        idf = sb("idf", [P, P])
        id16 = sb("id16", [P, P], F16)
        idb = sb("idb", [P, P], BF16)
        half = sb("half", [P, 1])
        kvmask = sb("kvmask", [P, 8])
        rowhalf = sb("rowhalf", [P, 2])
        sel0f = sb("sel0f", [16, 8, P])
        sel0 = sb("sel0", [16, 8, P], BF16)
        wgv = sb("wgv", [P, 2, 2 * HID], BF16)
        wow = sb("wow", [P, 8, D], BF16)
        gam = sb("gam", [P, 4])
        bgv = sb("bgv", [P, 2, HID])
        bo = sb("bo", [P, D])
        wA = sb("wA", [P, 2, HEADS1 * CD])
        wB = sb("wB", [P, PAIRS1, D])
        cosT = sb("cosT", [P, 2, SEQ])
        sinT = sb("sinT", [P, 2, SEQ])
        cosN = sb("cosN", [P, 2, CD])
        sinN = sb("sinN", [P, 2, CD])
        sel1f = sb("sel1f", [16, PAIRS1, P])
        sel1 = sb("sel1", [16, PAIRS1, P], BF16)
        ones2 = sb("ones2", [P, P])
        w1T = sb("w1T", [P, 2, EXPERTS * EH])
        w2T = sb("w2T", [P, EB, D])
        b1c = sb("b1c", [P, EB])
        gwT = sb("gwT", [P, 2, EXPERTS])
        gb8 = sb("gb8", [P, 2, EXPERTS])
        before = sb("before", [P, 8, 8])
        b2s = sb("b2s", [EXPERTS, D])
        sel3f = sb("sel3f", [24, EB, P])
        sel3 = sb("sel3", [24, EB, P], BF16)
        ARENA = 16 * 1024 + 768
        arena = sb("arena", [P, ARENA])
        bank = [ctx.enter_context(nc.psum_tensor(f"bank{i}", [P, 512], F32)) for i in range(8)]

        class Arena:
            def __init__(self):
                self.at = 0

            def take(self, shape, dt=F32, rows=P):
                n = int(np.prod(shape))
                words = n if dt == F32 else (n + 1) // 2
                a = arena[0:rows, self.at:self.at + words]
                self.at += words + words % 2
                assert self.at <= ARENA
                if dt != F32:
                    a = a.bitcast(dt)
                names = "abcdef"[:len(shape)]
                if len(shape) > 1:
                    a = a.rearrange(f"p ({' '.join(names)}) -> p {' '.join(names)}",
                                    **dict(zip(names, shape)))
                return a

        class Norm:
            def __init__(self, ph, mem):
                self.bn, self.agg, self.var, self.rstd, self.xn = (
                    sem(f"{ph}_bn"), sem(f"{ph}_agg"), sem(f"{ph}_var"), sem(f"{ph}_rstd"), sem(f"{ph}_xn"))
                self.stat, self.mv, self.ve, self.rs = (
                    mem.take([2, 6]), mem.take([2, 2]), mem.take([2, 1]), mem.take([2, 1]))
                self.out = mem.take([2, D])

        passed = sem("passed")

        def held(eng, s, value):
            eng.wait_ge(s, value)
            eng.sem_inc(passed, 1)

        def stats(v, ln, t, p):
            v.bn_stats(ln.stat[:, p, :], xs[:, t, :]).then_inc(ln.bn, 1)
            held(v, ln.bn, t + 1)
            v.bn_aggr(ln.mv[:, p, :], ln.stat[:, p, :]).then_inc(ln.agg, 1)
            v.wait_ge(ln.agg, t + 1)
            v.tensor_scalar(ln.ve[:, p, :], ln.mv[:, p, 1:2], EPS, None, ALU.add).then_inc(ln.var, 1)

        def rstd(g, ln, t, p):
            g.wait_ge(ln.var, t + 1)
            g.tensor_tensor(ln.rs[:, p, :], ln.ve[:, p, :], half[:, :], ALU.pow).then_inc(ln.rstd, 1)

        def normalise(v, ln, t, p):
            v.wait_ge(ln.rstd, t + 1)
            dst, src = ln.out[:, p, :], xs[:, t, :]
            if ln is ln1:
                dst = dst.rearrange("n (g k i) -> n k g i", k=8, g=4)
                src = src.rearrange("n (k g i) -> n k g i", k=8, g=4)
            v.tensor_scalar(dst, src, ln.mv[:, p, 0:1], ln.rs[:, p, :], ALU.subtract, ALU.mult).then_inc(ln.xn, 1)

        m0 = Arena()
        wq_in = m0.take([2, 2, D])
        cq_in = m0.take([2, 2, CQ])
        dq_in = m0.take([2, 2, 2, RR], rows=96)
        et_in = m0.take([2, 2, CD], rows=RR)
        ckv_in = m0.take([2, 2, CD])
        wo_in = m0.take([2, 2, D])
        ysb = m0.take([2, 2, D], rows=96)
        zsb = m0.take([2, D], rows=RR)
        m0b = Arena()
        wraw = m0b.take([3, 8 * D])
        wabs = m0b.take([3, 1])
        wq01 = m0b.take([8 * D])
        wqb = m0b.take([8 * D], BF16)
        rgam = m0b.take([4])
        ones_sum = m0b.take([P])

        ld_const, ld_x, ld_w0, ld_w1 = sem("ld_const"), sem("ld_x"), sem("ld_w0"), sem("ld_w1")
        consts_done, tanh_done = sem("consts_done"), sem("tanh_done")
        q_abs, q_sum, q_gam, q_rg, q_r1, q_r2, q_bf, q_tr, q_ev = (
            sem(f"q_{n}") for n in ("abs", "sum", "gam", "rg", "r1", "r2", "bf", "tr", "ev"))
        m_ld = [sem("m_ld0"), sem("m_ld1")]
        m_y, m_ye, m_z, m_ze, m_a, m_ae, m_b, m_be = (
            sem(f"m_{n}") for n in ("y", "ye", "z", "ze", "a", "ae", "b", "be"))

        const_loads = [
            (graw[:, :], d["g"]), (idf[:, :], d["ident"]), (kvmask[:, :], d["kvmask"]), (rowhalf[:, :], d["rowhalf"]),
            (sel0f[:, :, :], d["sel0"]), (sel1f[:, :, :], d["sel1"]), (sel3f[:, :, :], d["sel3"]),
            (ones2[:, :], d["ones2"]), (cosT[:, :, :], d["cosT"]), (sinT[:, :, :], d["sinT"]),
            (cosN[:, :, :], d["cosN"]), (sinN[:, :, :], d["sinN"]), (before[:, :, :], d["before"]),
            (bo[:, :], d["bo"].broadcast_to([P, D])), (bgv[:, 0, :], d["bg"].broadcast_to([P, HID])),
            (bgv[:, 1, :], d["bv"].broadcast_to([P, HID])),
            (gb8[:, 0, :], d["gb"].broadcast_to([P, EXPERTS])), (gb8[:, 1, :], d["gbias"].broadcast_to([P, EXPERTS])),
            (b1c[:, :], d["b1"]), (b2s[:, :], d["b2"]), (gwT[:, :, :], d["gwT"]),
        ]
        N_CONST = 16 * len(const_loads)
        N_X = 16 * 6

        m1 = Arena()
        ln1 = Norm("a", m1)
        qT = m1.take([2, 4, SEQ])
        qT16 = m1.take([2, 4, SEQ], BF16)
        kx = m1.take([2, 8, SEQ])
        kx16 = m1.take([2, 8, SEQ], BF16)
        mx1 = m1.take([2, 2, 16])
        nm1 = m1.take([2, 2 * P], BF16, rows=16)
        PT1 = m1.take([2, 4, 512])
        vx = m1.take([2, 8, 18])
        rec1 = m1.take([2, 32, 1])
        att1 = m1.take([2, 32, 8])
        (a_qt, a_qe, a_q16, a_kx, a_k16, a_p1, a_mx, a_mt, a_nm, a_s, a_exp, a_vx, a_pv, a_rec, a_att,
         a_x, a_vz) = (sem(f"a_{n}") for n in (
             "qt", "qe", "q16", "kx", "k16", "p1", "mx", "mt", "nm", "s", "exp", "vx", "pv", "rec", "att",
             "x", "vz"))
        D1 = 4

        m2 = Arena()
        ln2 = Norm("f", m2)
        gx = m2.take([2, 4])
        sg = m2.take([2, 2])
        xm = m2.take([2, D])
        xqT = m2.take([2, 2, P], BF16)
        gate = m2.take([2, HID])
        val = m2.take([2, HID])
        sil = m2.take([2, HID])
        hm = m2.take([2, HID])
        gh = m2.take([2, 4])
        hqT = m2.take([2, 8, P], BF16)
        yb = m2.take([2, D])
        (f_ab, f_c1, f_c2, f_c3, f_sc, f_xm, f_tr, f_xe, f_gp, f_vp, f_g, f_v, f_sil, f_h, f_ha, f_h1, f_h2,
         f_hm, f_ht, f_he, f_o, f_y, f_x) = (sem(f"f_{n}") for n in (
             "ab", "c1", "c2", "c3", "sc", "xm", "tr", "xe", "gp", "vp", "g", "v", "sil", "h", "ha", "h1",
             "h2", "hm", "ht", "he", "o", "y", "x"))
        D2 = 4

        m3 = Arena()
        ln3 = Norm("l", m3)
        xT3 = m3.take([2, 2, P])
        kin = m3.take([2, 2, 2, SEQ])
        kt1 = m3.take([2, 2, 2, SEQ])
        kt2 = m3.take([2, 2, 2, SEQ])
        kbd = m3.take([2, 2, P])
        kbd16 = m3.take([2, 2, P], BF16)
        vt1 = m3.take([2, 2, 2, CD])
        vt2 = m3.take([2, 2, 2, CD])
        vbd = m3.take([2, 2, P])
        qa = m3.take([2, PAIRS1, P])
        qa16 = m3.take([2, PAIRS1, P], BF16)
        mx3 = m3.take([2, HEADS1])
        nm3 = m3.take([2, P], BF16, rows=16)
        PT3 = m3.take([2, 2, 512])
        rec3 = m3.take([2, 512])
        cT = m3.take([2, PAIRS1, P])
        l_kin = [sem("l_kin0"), sem("l_kin1")]
        (l_tr, l_te, l_qa, l_qe, l_q16, l_k1, l_k2, l_kb, l_k16, l_v1, l_v2, l_vb, l_p1, l_mx, l_mt,
         l_nm, l_s, l_exp, l_pv, l_rec, l_c, l_o, l_x, l_z) = (sem(f"l_{n}") for n in (
             "tr", "te", "qa", "qe", "q16", "k1", "k2", "kb", "k16", "v1", "v2", "vb", "p1", "mx",
             "mt", "nm", "s", "exp", "pv", "rec", "c", "o", "x", "z"))
        D3 = 5

        m4 = Arena()
        ln4 = Norm("e", m4)
        xT4 = m4.take([2, 2, P])
        sc4 = m4.take([2, 8])
        tm4 = m4.take([2, 8])
        gt = m4.take([2, 8, 8])
        eq = m4.take([2, 8, 8])
        rank = m4.take([2, 8])
        mxn = m4.take([2, 1])
        ex4 = m4.take([2, 8])
        es4 = m4.take([2, 8])
        z4 = m4.take([2, 2])
        comb = m4.take([2, 8])
        cpart = m4.take([2, 24], BF16)
        cres = m4.take([2, 2, 8])
        cT16 = m4.take([2, P], BF16, rows=24)
        cTf = m4.take([2, P], F32, rows=8)
        hs = m4.take([2, EB * P])
        sh4 = m4.take([2, EB * P])
        xo = m4.take([2, D])
        (e_tr, e_te, e_sc, e_s1, e_s2, e_m, e_ex, e_g1, e_g2, e_g3, e_g4, e_rk, e_es, e_z, e_rz, e_cb, e_c1,
         e_c2, e_c3, e_c4, e_c5, e_ct, e_cte, e_h, e_sl, e_cb2, e_hs, e_y, e_x, e_out) = (
             sem(f"e_{n}") for n in (
                 "tr", "te", "sc", "s1", "s2", "m", "ex", "g1", "g2", "g3", "g4", "rk", "es", "z", "rz",
                 "cb", "c1", "c2", "c3", "c4", "c5", "ct", "cte", "h", "sl", "cb2", "hs", "y", "x", "out"))
        D4 = 4
        CHUNKS4 = [(0, 4), (4, 8), (8, EB)]

        block = ctx.enter_context(nc.Block())

        @block.sync
        def _(sp):
            for dst, src in const_loads:
                sp.dma_start(dst, src).then_inc(ld_const, 16)
            for i, name in enumerate(("gw", "vw")):
                sp.dma_start(wraw[:, i, :], d[name].rearrange("(c p) i -> p c i", p=P)).then_inc(ld_w0, 16)
            sp.dma_start(wraw[:, 2, :], d["ow"].rearrange("(c p) i -> p c i", p=P)).then_inc(ld_w0, 16)
            sp.dma_start(xs[:, :, :], d["x"].rearrange("(t p) i -> p t i", p=P)).then_inc(ld_x, 16)
            for r in range(2):
                sp.dma_start(ctx2[64 * r:64 * r + 64], d["ctx"].rearrange("b t i -> t b i")).then_inc(ld_x, 16)
                sp.dma_start(kTp[64 * r:64 * r + 64],
                             d["ctxT"].rearrange("i (n r) t -> i n r t", r=2)[:, :, r, :]).then_inc(ld_x, 16)
            sp.dma_start(w1T[:, :, :], d["w1T"]).then_inc(ld_x, 16)
            sp.dma_start(w2T[:, :, :], d["w2T"]).then_inc(ld_w1, 16)

            def pair_weights(i, p, used):
                if used:
                    sp.wait_ge(m_be, i - 1)
                    sp.wait_ge(m_ae, i - 1)
                hs2 = bass.ts(i, 2)
                sp.dma_start(wq_in[:, p], d["Wq"][hs2].rearrange("h k i -> k h i")).then_inc(m_ld[p], 16)
                sp.dma_start(cq_in[:, p], d["Cq"][hs2].rearrange("h k q -> k h q")).then_inc(m_ld[p], 16)
                for h in range(2):
                    sp.dma_start(dq_in[:, p, h], d["Dq"][bass.ts(i, 2)][h].rearrange("(c q) r -> q c r", q=96)).then_inc(m_ld[p], 16)
                sp.dma_start(et_in[:, p], d["ET"][hs2].rearrange("h r i -> r h i")).then_inc(m_ld[p], 16)
                sp.dma_start(ckv_in[:, p], d["Ckv"][hs2].rearrange("h k i -> k h i")).then_inc(m_ld[p], 16)
                sp.dma_start(wo_in[:, p], d["WoT"][hs2].rearrange("h k o -> k h o")).then_inc(m_ld[p], 16)

            sp.wait_ge(q_ev, 6)
            pair_weights(0, 0, False)
            pair_weights(1, 1, False)
            with sp.Fori(2, PAIRS1 - 1, 2) as i:
                pair_weights(i, 0, True)
                pair_weights(i + 1, 1, True)

            if last_phase >= 3:
                sp.wait_ge(f_x, TILES)

                def context(t, p, used):
                    if used:
                        sp.wait_ge(l_kb, t - 1)
                    for r in range(2):
                        rows = slice(64 * r, 64 * r + 64)
                        src = d["ctxT"][:, bass.ts(t, 2), :]
                        src2 = d["ctxTs"][:, bass.ts(t, 2), :]
                        sp.dma_start(kin[rows, p, 0], src).then_inc(l_kin[p], 16)
                        sp.dma_start(kin[rows, p, 1], src2).then_inc(l_kin[p], 16)
                tiles_loop(sp, 0, [(0, context)])

            ready = {1: a_x, 2: f_x, 3: l_x, 4: e_x}[last_phase]
            src = xs
            if last_phase < 4:
                for t in range(TILES):
                    sp.wait_ge(ready, t + 1)
                    sp.dma_start(out[bass.ts(t, P), :], src[:, t, :]).then_inc(e_out, 16)
            else:
                def store(t, p, used):
                    sp.wait_ge(e_x, t + 1)
                    sp.dma_start(out[bass.ts(t, P), :], xs[:, t, :]).then_inc(e_out, 16)
                tiles_loop(sp, 0, [(0, store)])
            sp.wait_ge(e_out, 16 * TILES)

        @block.gpsimd
        def _(g):
            g.wait_ge(ld_const, N_CONST)
            g.wait_ge(ld_x, N_X)
            g.wait_ge(consts_done, 1)

            g.wait_ge(m_be, PAIRS1)
            g.wait_ge(m_ae, PAIRS1)
            for p in range(2):
                g.tensor_copy(vx[:, p].rearrange("t n (k i) -> t n k i", k=2)[:, :, :, 8],
                              rowhalf[:, :].unsqueeze(1).broadcast_to([P, 8, 2]))

            def a_keys(t, p, used):
                if used:
                    g.wait_ge(a_s, 4 * t - 4)
                g.tensor_tensor(kx[:, p], kTp[:, t, :].unsqueeze(1).broadcast_to([P, 8, SEQ]),
                                kvmask[:, :].unsqueeze(2).broadcast_to([P, 8, SEQ]), ALU.mult).then_inc(a_kx, 1)
                held(g, a_kx, t + 1)
                g.tensor_copy(kx16[:, p], kx[:, p]).then_inc(a_k16, 1)

            def a_values(t, p, used):
                if used:
                    held(g, a_pv, t - 1)
                g.tensor_tensor(vx[:, p].rearrange("t n (k i) -> t n k i", k=2)[:, :, :, 0:8],
                                ctx2[:, bass.ts(t, 2), :].rearrange("t b (n k i) -> t (b n) k i", n=4, k=2),
                                rowhalf[:, :].unsqueeze(1).unsqueeze(3).broadcast_to([P, 8, 2, 8]),
                                ALU.mult).then_inc(a_vx, 1)

            def a_q16c(t, p, used):
                held(g, a_qe, t + 1)
                g.tensor_copy(qT16[:, p], qT[:, p]).then_inc(a_q16, 1)

            tiles_loop(g, D1, [(0, lambda t, p, u: rstd(g, ln1, t, p)), (1, a_keys), (1, a_q16c), (2, a_values)])

            if last_phase >= 2:
                tiles_loop(g, D2, [(0, lambda t, p, u: rstd(g, ln2, t, p))])
            if last_phase >= 3:
                g.wait_ge(f_x, TILES)
                def twice(x, n):
                    return x.unsqueeze(2).broadcast_to([P, 2, 2, n])

                def table(x, n):
                    return x.unsqueeze(1).broadcast_to([P, 2, 2, n])

                def l_keys(t, p, used):
                    g.wait_ge(l_kin[p], 32 * t + (64 - 32 * p))
                    if used:
                        held(g, l_s, 2 * t - 2)
                    g.tensor_tensor(kt1[:, p], twice(kin[:, p, 0], SEQ), table(cosT[:, :, :], SEQ), ALU.mult).then_inc(l_k1, 1)
                    g.tensor_tensor(kt2[:, p], twice(kin[:, p, 1], SEQ), table(sinT[:, :, :], SEQ), ALU.mult).then_inc(l_k2, 1)
                    g.wait_ge(l_k1, t + 1)
                    g.wait_ge(l_k2, t + 1)
                    g.tensor_tensor(kbd[:, p].rearrange("p b (r n) -> p b r n", r=2), kt1[:, p], kt2[:, p], ALU.add).then_inc(l_kb, 1)
                    held(g, l_kb, t + 1)
                    g.tensor_copy(kbd16[:, p], kbd[:, p]).then_inc(l_k16, 1)

                def l_values(t, p, used):
                    src = ctx2[:, bass.ts(t, 2), :]
                    if used:
                        held(g, l_pv, 2 * t - 2)
                    g.tensor_tensor(vt1[:, p], twice(src, CD), table(cosN[:, :, :], CD), ALU.mult).then_inc(l_v1, 1)
                    for h in range(2):
                        lo = slice(32 * h, 32 * h + 32)
                        hi = slice(32 - 32 * h, 64 - 32 * h)
                        last = g.tensor_tensor(vt2[:, p, :, :, lo], twice(src[:, :, hi], 32), table(sinN[:, :, lo], 32), ALU.mult)
                    last.then_inc(l_v2, 1)
                    g.wait_ge(l_v1, t + 1)
                    g.wait_ge(l_v2, t + 1)
                    g.tensor_tensor(vbd[:, p].rearrange("p b (r n) -> p b r n", r=2), vt1[:, p], vt2[:, p], ALU.add).then_inc(l_vb, 1)

                def l_q16c(t, p, used):
                    held(g, l_qe, 2 * t + 2)
                    g.tensor_copy(qa16[:, p], qa[:, p]).then_inc(l_q16, 1)

                tiles_loop(g, D3, [(0, lambda t, p, u: rstd(g, ln3, t, p)), (2, l_keys), (2, l_q16c), (3, l_values)])
            if last_phase >= 4:
                tiles_loop(g, D4, [(0, lambda t, p, u: rstd(g, ln4, t, p))])

        @block.scalar
        def _(a):
            a.wait_ge(ld_const, N_CONST)
            a.activation(gT[:, :], graw[:, :], ACT.Tanh).then_inc(tanh_done, 1)
            for j in range(6):
                a.wait_ge(q_tr, j + 1)
                src = bank[j % 2][:, :].bitcast(BF16)
                if j < 4:
                    k, m = j // 2, j % 2
                    dst = wgv[:, m, k * HID:(k + 1) * HID]
                else:
                    m = j - 4
                    dst = wow[:, 4 * m:4 * m + 4, :]
                a.activation(dst, src if j < 4 else src.rearrange("p (c i) -> p c i", c=4), ACT.Copy).then_inc(q_ev, 1)

            def pair_evac(i, p, used):
                for h in range(2):
                    a.wait_ge(m_y, 2 * i + h + 1)
                    a.activation(ysb[:, h, :, :], bank[0][0:96, :].rearrange("q (c i) -> q c i", c=2), ACT.Copy).then_inc(m_ye, 1)
                    a.wait_ge(m_z, 2 * i + h + 1)
                    a.activation(zsb[:, h, :], bank[1][0:RR, 0:D], ACT.Copy).then_inc(m_ze, 1)
            pair_evac(0, 0, False)
            pair_evac(1, 1, False)
            with a.Fori(2, PAIRS1 - 1, 2) as i:
                pair_evac(i, 0, True)
                pair_evac(i + 1, 1, True)

            a.wait_ge(m_be, PAIRS1)
            a.wait_ge(m_ae, PAIRS1)

            def a_nmax(t, p, used):
                a.wait_ge(a_mt, t + 1)
                if used:
                    held(a, a_s, 4 * t - 4)
                a.activation(nm1[:, p], bank[3][0:16, 0:2 * P], ACT.Copy, scale=-1.0).then_inc(a_nm, 1)

            def a_exps(t, p, used):
                if used:
                    held(a, a_pv, t - 1)
                for j in range(4):
                    a.wait_ge(a_s, 4 * t + j + 1)
                    a.activation(PT1[:, p, j], bank[4 + j % 2][:, :], ACT.Exp, scale=8.0 ** -0.5).then_inc(a_exp, 1)

            def a_qevac(t, p, used):
                a.wait_ge(a_qt, t + 1)
                if used:
                    held(a, a_s, 4 * t - 4)
                    held(a, a_q16, t - 1)
                for r in range(2):
                    last = a.activation(qT[64 * r:64 * r + 64, p],
                                        bank[0][0:64, :].rearrange("p (g n) -> p g n", g=4)[:, :, 64 * r:64 * r + 64],
                                        ACT.Copy)
                last.then_inc(a_qe, 1)

            tiles_loop(a, D1, [(3, a_nmax), (3, a_exps), (1, a_qevac)])

            if last_phase >= 2:
                a.wait_ge(a_x, TILES)

                def f_xevac(t, p, used):
                    a.wait_ge(f_tr, t + 1)
                    if used:
                        held(a, f_vp, 2 * t - 2)
                    a.activation(xqT[:, p], bank[0][:, 0:P].bitcast(F16).rearrange("p (c n) -> p c n", c=2),
                                 ACT.Copy, bias=-ROUND0).then_inc(f_xe, 1)

                def f_silu(t, p, used):
                    a.wait_ge(f_g, 2 * t + 2)
                    if used:
                        held(a, f_h, t - 1)
                    a.activation(sil[:, p], gate[:, p], ACT.Silu).then_inc(f_sil, 1)

                def f_hevac(t, p, used):
                    a.wait_ge(f_ht, t + 1)
                    if used:
                        held(a, f_o, t - 1)
                    a.activation(hqT[:, p], bank[5][:, :].bitcast(F16).rearrange("p (c n) -> p c n", c=8),
                                 ACT.Copy, bias=-ROUND0).then_inc(f_he, 1)

                tiles_loop(a, D2, [(3, f_hevac), (2, f_silu), (1, f_xevac)])

            if last_phase >= 3:
                a.wait_ge(f_x, TILES)

                def l_tevac(t, p, used):
                    a.wait_ge(l_tr, t + 1)
                    if used:
                        held(a, l_qa, 2 * t - 2)
                    a.activation(xT3[:, p], bank[0][:, 0:2 * P].rearrange("p (c n) -> p c n", c=2), ACT.Copy).then_inc(l_te, 1)

                def l_qevac(t, p, used):
                    if used:
                        held(a, l_s, 2 * t - 2)
                        held(a, l_q16, t - 1)
                    for j in range(2):
                        a.wait_ge(l_qa, 2 * t + j + 1)
                        a.activation(qa[:, p, 4 * j:4 * j + 4], bank[1][:, :].rearrange("p (c n) -> p c n", c=4),
                                     ACT.Copy).then_inc(l_qe, 1)

                def l_nmax(t, p, used):
                    a.wait_ge(l_mt, t + 1)
                    if used:
                        held(a, l_s, 2 * t - 2)
                    a.activation(nm3[:, p], bank[3][0:16, 0:P], ACT.Copy, scale=-1.0).then_inc(l_nm, 1)

                def l_exps(t, p, used):
                    if used:
                        held(a, l_pv, 2 * t - 2)
                    for b in range(2):
                        a.wait_ge(l_s, 2 * t + b + 1)
                        a.activation(PT3[:, p, b], bank[4][:, :], ACT.Exp).then_inc(l_exp, 1)

                tiles_loop(a, D3, [(3, l_nmax), (3, l_exps), (2, l_qevac), (1, l_tevac)])

            if last_phase >= 4:
                a.wait_ge(l_x, TILES)

                def e_tevac(t, p, used):
                    a.wait_ge(e_tr, t + 1)
                    if used:
                        held(a, e_h, 3 * t - 3)
                    a.activation(xT4[:, p], bank[0][:, 0:2 * P].rearrange("p (c n) -> p c n", c=2), ACT.Copy).then_inc(e_te, 1)

                def e_exp(t, p, used):
                    a.wait_ge(e_m, t + 1)
                    if used:
                        held(a, e_es, t - 1)
                    a.activation(ex4[:, p], sc4[:, p], ACT.Exp, bias=mxn[:, p]).then_inc(e_ex, 1)

                def e_ctev(t, p, used):
                    a.wait_ge(e_ct, t + 1)
                    if used:
                        held(a, e_y, t - 1)
                    a.activation(cT16[:, p], bank[2][0:24, 0:P // 2].bitcast(BF16), ACT.Copy)
                    a.activation(cTf[:, p], bank[2][0:8, P:2 * P], ACT.Copy).then_inc(e_cte, 1)

                def e_silu(t, p, used):
                    if used:
                        held(a, e_hs, 3 * t - 3)
                    for c, (j0, j1) in enumerate(CHUNKS4):
                        a.wait_ge(e_h, 3 * t + c + 1)
                        for j in range(j0, j1):
                            last = a.activation(sh4[:, p, j * P:(j + 1) * P], bank[3 + c % 2][:, (j - j0) * P:(j - j0 + 1) * P],
                                                ACT.Silu, bias=b1c[:, j:j + 1])
                        last.then_inc(e_sl, 1)

                tiles_loop(a, D4, [(2, e_exp), (3, e_ctev), (3, e_silu), (1, e_tevac)])

        @block.tensor
        def _(pe):
            pe.wait_ge(ld_const, N_CONST)
            pe.wait_ge(consts_done, 1)
            pe.wait_ge(q_abs, 3)
            pe.matmul(bank[2][:, 0:3], ones_sum, wabs.rearrange("p a b -> p (a b)"), start=True, stop=True).then_inc(q_sum, 1)
            for j in range(6):
                if j >= 2:
                    pe.wait_ge(q_ev, j - 1)
                dst = bank[j % 2][:, :].bitcast(BF16)
                if j < 4:
                    k, m = j // 2, j % 2
                    pe.wait_ge(q_bf, k + 1)
                    for c in range(8):
                        last = pe.transpose(dst[:, c * P:(c + 1) * P], wqb[:, c * D + m * P:c * D + (m + 1) * P], idb[:, :])
                else:
                    m = j - 4
                    pe.wait_ge(q_bf, 3)
                    for c in range(4):
                        for o in range(2):
                            last = pe.transpose(dst[:, c * D + o * P:c * D + (o + 1) * P],
                                                wqb[:, o * HID + (4 * m + c) * P:o * HID + (4 * m + c + 1) * P], idb[:, :])
                last.then_inc(q_tr, 1)

            def pair_products(i, p, used):
                pe.wait_ge(m_ld[p], 56 * i + (112 - 56 * p))
                for h in range(2):
                    if used:
                        held(pe, m_ye, 2 * i + h)
                    elif i + h:
                        pe.wait_ge(m_ye, 2 * i + h)
                    for c in range(2):
                        last = pe.matmul(bank[0][0:96, c * D:(c + 1) * D], cq_in[:, p, h, c * 96:(c + 1) * 96],
                                         wq_in[:, p, h, :], start=True, stop=True)
                    last.then_inc(m_y, 1)
                    held(pe, m_ye, 2 * i + h + 1)
                    for c in range(2):
                        last = pe.matmul(bank[1][0:RR, 0:D], dq_in[:, p, h, c, :], ysb[:, h, c, :], start=(c == 0), stop=(c == 1))
                    last.then_inc(m_z, 1)
                held(pe, m_ze, 2 * i + 2)
                if used:
                    held(pe, m_ae, i)
                elif i:
                    pe.wait_ge(m_ae, i)
                for h in range(2):
                    for m in range(2):
                        last = pe.matmul(bank[2][:, m * P + h * 64:m * P + h * 64 + 64], zsb[:, h, m * P:(m + 1) * P],
                                         et_in[:, p, h, :], start=True, stop=True)
                last.then_inc(m_a, 1)
                if used:
                    held(pe, m_be, i)
                elif i:
                    pe.wait_ge(m_be, i)
                for h in range(2):
                    last = pe.matmul(bank[3][64 * h:64 * h + 64, 0:D], ckv_in[:, p, h, :], wo_in[:, p, h, :], start=True, stop=True)
                last.then_inc(m_b, 1)
            pair_products(0, 0, False)
            pair_products(1, 1, False)
            with pe.Fori(2, PAIRS1 - 1, 2) as i:
                pair_products(i, 0, True)
                pair_products(i + 1, 1, True)

            pe.wait_ge(m_ae, PAIRS1)
            pe.wait_ge(m_be, PAIRS1)

            def a_trans(t, p, used):
                held(pe, ln1.xn, t + 1)
                if used:
                    held(pe, a_qe, t)
                elif t:
                    pe.wait_ge(a_qe, t)
                q = ln1.out[:, p, :].rearrange("n (g c) -> n g c", g=4)
                for g in range(4):
                    last = pe.transpose(bank[0][0:64, g * P:(g + 1) * P], q[:, g], idf[:, :])
                last.then_inc(a_qt, 1)

            def a_pass1(t, p, used):
                held(pe, a_q16, t + 1)
                held(pe, a_k16, t + 1)
                for j in range(4):
                    b, gp = j // 2, j % 2
                    if used:
                        held(pe, a_mx, 4 * t + j - 1)
                    elif 4 * t + j >= 2:
                        pe.wait_ge(a_mx, 4 * t + j - 1)
                    rows = slice(64 * b, 64 * b + 64)
                    pe.matmul(bank[1 + j % 2][:, :], qT16[rows, p, 2 * gp:2 * gp + 2, :].rearrange("p g n -> p (g n)"),
                              kx16[rows, p].rearrange("p k n -> p (k n)"), start=True, stop=True).then_inc(a_p1, 1)

            def a_maxT(t, p, used):
                held(pe, a_mx, 4 * t + 4)
                if used:
                    held(pe, a_nm, t)
                elif t:
                    pe.wait_ge(a_nm, t)
                for gp in range(2):
                    last = pe.transpose(bank[3][0:16, gp * P:(gp + 1) * P], mx1[:, p, gp, :], idf[:, :])
                last.then_inc(a_mt, 1)

            def a_scores(t, p, used):
                held(pe, a_nm, t + 1)
                held(pe, a_kx, t + 1)
                for j in range(4):
                    b = j // 2
                    if used:
                        held(pe, a_exp, 4 * t + j - 1)
                    elif 4 * t + j >= 2:
                        pe.wait_ge(a_exp, 4 * t + j - 1)
                    rows = slice(64 * b, 64 * b + 64)
                    for c in range(2):
                        pair = 2 * (j % 2) + c
                        dst = bank[4 + j % 2][:, c * D:(c + 1) * D]
                        pe.matmul(dst, kx[rows, p, 2 * pair:2 * pair + 2, :].rearrange("p k n -> p (k n)"),
                                  qT[rows, p].rearrange("p g n -> p (g n)"), start=True, stop=False)
                        last = pe.matmul(dst, sel0[:, 4 * b + pair, :], nm1[:, p], start=False, stop=True)
                    last.then_inc(a_s, 1)

            def a_sums(t, p, used):
                held(pe, a_exp, 4 * t + 4)
                held(pe, a_vx, t + 1)
                if used:
                    held(pe, a_att, t)
                elif t:
                    pe.wait_ge(a_att, t)
                for b in range(2):
                    dst = bank[6][64 * b:64 * b + 64, 0:288].rearrange("p (n k g i) -> p n g k i", n=4, k=2, g=4)
                    for pair in range(4):
                        for g in range(4):
                            col = (pair % 2) * D + g * 64
                            last = pe.matmul(dst[:, pair, g], PT1[:, p, 2 * b + pair // 2, col:col + 64],
                                             vx[:, p, 4 * b + pair, :].rearrange("p (k i) -> p k i", k=2), start=True, stop=True)
                last.then_inc(a_pv, 1)

            tiles_loop(pe, D1, [(3, a_maxT), (4, a_sums), (3, a_scores), (2, a_pass1), (1, a_trans)])

            if last_phase >= 2:
                pe.wait_ge(a_x, TILES)

                def f_trans(t, p, used):
                    held(pe, f_xm, t + 1)
                    if used:
                        held(pe, f_xe, t)
                    elif t:
                        pe.wait_ge(f_xe, t)
                    q = xm[:, p, :].bitcast(F16).rearrange("p (n two) -> p n two", two=2)[:, :, 0]
                    dst = bank[0][:, 0:P].bitcast(F16)
                    for c in range(2):
                        last = pe.transpose(dst[:, c * P:(c + 1) * P], q[:, c * P:(c + 1) * P], id16[:, :])
                    last.then_inc(f_tr, 1)

                def f_prod(t, p, used):
                    held(pe, f_xe, t + 1)
                    for j in range(4):
                        done, made = (f_g, f_gp) if j < 2 else (f_v, f_vp)
                        if used:
                            held(pe, done, 2 * t)
                        elif t:
                            pe.wait_ge(done, 2 * t)
                        for c in range(2):
                            last = pe.matmul(bank[1 + j][:, :], xqT[:, p, c, :], wgv[:, c, j * 512:(j + 1) * 512],
                                             start=(c == 0), stop=(c == 1))
                        last.then_inc(made, 1)

                def f_htrans(t, p, used):
                    held(pe, f_hm, t + 1)
                    if used:
                        held(pe, f_he, t)
                    elif t:
                        pe.wait_ge(f_he, t)
                    q = hm[:, p, :].bitcast(F16).rearrange("p (n two) -> p n two", two=2)[:, :, 0]
                    dst = bank[5][:, :].bitcast(F16)
                    for c in range(8):
                        last = pe.transpose(dst[:, c * P:(c + 1) * P], q[:, c * P:(c + 1) * P], id16[:, :])
                    last.then_inc(f_ht, 1)

                def f_outp(t, p, used):
                    held(pe, f_he, t + 1)
                    if used:
                        held(pe, f_y, t)
                    elif t:
                        pe.wait_ge(f_y, t)
                    for c in range(8):
                        last = pe.matmul(bank[6][:, 0:D], hqT[:, p, c, :], wow[:, c, :], start=(c == 0), stop=(c == 7))
                    last.then_inc(f_o, 1)

                tiles_loop(pe, D2, [(4, f_outp), (3, f_htrans), (2, f_prod), (1, f_trans)])

            if last_phase >= 3:
                pe.wait_ge(f_x, TILES)

                def l_trans(t, p, used):
                    held(pe, ln3.xn, t + 1)
                    if used:
                        held(pe, l_te, t)
                    elif t:
                        pe.wait_ge(l_te, t)
                    for c in range(2):
                        last = pe.transpose(bank[0][:, c * P:(c + 1) * P], ln3.out[:, p, c * P:(c + 1) * P], idf[:, :])
                    last.then_inc(l_tr, 1)

                def l_query(t, p, used):
                    held(pe, l_te, t + 1)
                    for j in range(2):
                        if used:
                            held(pe, l_qe, 2 * t + j)
                        elif 2 * t + j:
                            pe.wait_ge(l_qe, 2 * t + j)
                        for k in range(4):
                            pair = 4 * j + k
                            for c in range(2):
                                last = pe.matmul(bank[1][:, k * P:(k + 1) * P], wA[:, c, pair * P:(pair + 1) * P],
                                                 xT3[:, p, c, :], start=(c == 0), stop=(c == 1))
                        last.then_inc(l_qa, 1)

                def l_pass1(t, p, used):
                    held(pe, l_q16, t + 1)
                    held(pe, l_k16, t + 1)
                    for j in range(2):
                        if used:
                            held(pe, l_mx, 2 * t + j)
                        elif 2 * t + j:
                            pe.wait_ge(l_mx, 2 * t + j)
                        for b in range(2):
                            for k in range(4):
                                last = pe.matmul(bank[2][64 * b:64 * b + 64, k * P:(k + 1) * P],
                                                 qa16[:, p, 4 * j + k, 64 * b:64 * b + 64], kbd16[:, p, b], start=True, stop=True)
                        last.then_inc(l_p1, 1)

                def l_maxT(t, p, used):
                    held(pe, l_mx, 2 * t + 2)
                    if used:
                        held(pe, l_nm, t)
                    elif t:
                        pe.wait_ge(l_nm, t)
                    pe.transpose(bank[3][0:16, 0:P], mx3[:, p], idf[:, :]).then_inc(l_mt, 1)

                def l_scores(t, p, used):
                    held(pe, l_nm, t + 1)
                    held(pe, l_kb, t + 1)
                    for b in range(2):
                        if used:
                            held(pe, l_exp, 2 * t + b)
                        elif 2 * t + b:
                            pe.wait_ge(l_exp, 2 * t + b)
                        q = qa[:, p, :, 64 * b:64 * b + 64]
                        pe.matmul(bank[4][:, :].rearrange("p (k n) -> p k n", k=8), kbd[:, p, b], q, start=True, stop=False)
                        for k in range(PAIRS1):
                            last = pe.matmul(bank[4][:, 64 * k:64 * k + 64], sel1[:, k, :], nm3[:, p, 64 * b:64 * b + 64],
                                             start=False, stop=(k == PAIRS1 - 1))
                        last.then_inc(l_s, 1)

                def l_sums(t, p, used):
                    held(pe, l_vb, t + 1)
                    for b in range(2):
                        held(pe, l_exp, 2 * t + b + 1)
                        if used:
                            held(pe, l_c, 2 * t + b)
                        elif 2 * t + b:
                            pe.wait_ge(l_c, 2 * t + b)
                        pe.matmul(bank[6][:, :], ones2[:, :], PT3[:, p, b], start=True, stop=True)
                        pe.matmul(bank[5][:, :], vbd[:, p, b], PT3[:, p, b], start=True, stop=True).then_inc(l_pv, 1)

                def l_outp(t, p, used):
                    held(pe, l_c, 2 * t + 2)
                    if used:
                        held(pe, l_x, t)
                    elif t:
                        pe.wait_ge(l_x, t)
                    for k in range(PAIRS1):
                        last = pe.matmul(bank[7][:, 0:D], cT[:, p, k, :], wB[:, k, :], start=(k == 0), stop=(k == PAIRS1 - 1))
                    last.then_inc(l_o, 1)

                tiles_loop(pe, D3, [(5, l_outp), (3, l_maxT), (4, l_sums), (3, l_scores), (2, l_query), (2, l_pass1), (1, l_trans)])

            if last_phase >= 4:
                pe.wait_ge(l_x, TILES)

                def e_trans(t, p, used):
                    held(pe, ln4.xn, t + 1)
                    if used:
                        held(pe, e_te, t)
                    elif t:
                        pe.wait_ge(e_te, t)
                    for c in range(2):
                        last = pe.transpose(bank[0][:, c * P:(c + 1) * P], ln4.out[:, p, c * P:(c + 1) * P], idf[:, :])
                    last.then_inc(e_tr, 1)

                def e_score(t, p, used):
                    held(pe, e_te, t + 1)
                    if used:
                        held(pe, e_s1, t)
                    elif t:
                        pe.wait_ge(e_s1, t)
                    for c in range(2):
                        last = pe.matmul(bank[1][:, 0:8], xT4[:, p, c, :], gwT[:, c, :], start=(c == 0), stop=(c == 1))
                    last.then_inc(e_sc, 1)

                def e_combT(t, p, used):
                    held(pe, e_c5, t + 1)
                    if used:
                        held(pe, e_cte, t)
                    elif t:
                        pe.wait_ge(e_cte, t)
                    pe.transpose(bank[2][0:24, 0:P // 2].bitcast(BF16), cpart[:, p], idb[:, :])
                    pe.transpose(bank[2][0:8, P:2 * P], comb[:, p], idf[:, :]).then_inc(e_ct, 1)

                def e_hid(t, p, used):
                    for c, (j0, j1) in enumerate(CHUNKS4):
                        if used:
                            held(pe, e_sl, 3 * t + c - 1)
                        elif 3 * t + c >= 2:
                            pe.wait_ge(e_sl, 3 * t + c - 1)
                        for j in range(j0, j1):
                            for k in range(2):
                                last = pe.matmul(bank[3 + c % 2][:, (j - j0) * P:(j - j0 + 1) * P], w1T[:, k, j * P:(j + 1) * P],
                                                 xT4[:, p, k, :], start=(k == 0), stop=(k == 1))
                        last.then_inc(e_h, 1)
                        if c == 0:
                            held(pe, e_cte, t + 1)
                        if used:
                            held(pe, e_hs, 3 * t + c - 1)
                        elif 3 * t + c >= 2:
                            pe.wait_ge(e_hs, 3 * t + c - 1)
                        for j in range(j0, j1):
                            last = pe.matmul(bank[5 + c % 2][:, (j - j0) * P:(j - j0 + 1) * P], sel3[:, j, :], cT16[:, p],
                                             start=True, stop=True)
                        last.then_inc(e_cb2, 1)

                def e_outp(t, p, used):
                    held(pe, e_hs, 3 * t + 3)
                    if used:
                        held(pe, e_x, t)
                    elif t:
                        pe.wait_ge(e_x, t)
                    for j in range(EB):
                        pe.matmul(bank[7][:, 0:D], hs[:, p, j * P:(j + 1) * P], w2T[:, j, :], start=(j == 0), stop=False)
                    pe.matmul(bank[7][:, 0:D], cTf[:, p], b2s[:, :], start=False, stop=True).then_inc(e_y, 1)

                tiles_loop(pe, D4, [(3, e_combT), (4, e_outp), (3, e_hid), (1, e_trans), (1, e_score)])

        @block.vector
        def _(v):
            v.memset(half[:, :], -0.5)
            v.memset(ones_sum, 1.0)
            v.wait_ge(ld_const, N_CONST)
            v.tensor_copy(id16[:, :], idf[:, :])
            v.tensor_copy(idb[:, :], idf[:, :])
            v.tensor_copy(sel0[:, :, :], sel0f[:, :, :])
            v.tensor_copy(sel1[:, :, :], sel1f[:, :, :])
            v.tensor_copy(sel3[:, :, :], sel3f[:, :, :]).then_inc(consts_done, 1)
            v.wait_ge(ld_w0, 48)
            for k in range(3):
                v.tensor_reduce(wabs[:, k], wraw[:, k], AX.X, ALU.add, apply_absolute_value=True).then_inc(q_abs, 1)
            v.wait_ge(q_sum, 1)
            v.tensor_scalar(gam[:, 0:3], bank[2][:, 0:3], 1.0 / (HID * D), 1e-5, ALU.mult, ALU.max).then_inc(q_gam, 1)
            v.wait_ge(q_gam, 1)
            v.reciprocal(rgam[:, 0:3], gam[:, 0:3]).then_inc(q_rg, 1)
            v.wait_ge(q_rg, 1)
            for k in range(3):
                v.tensor_scalar(wq01, wraw[:, k], rgam[:, k:k + 1], BIG, ALU.mult, ALU.add).then_inc(q_r1, 1)
                v.wait_ge(q_r1, k + 1)
                v.tensor_scalar(wraw[:, k], wq01, BIG, 1.0, ALU.subtract, ALU.min).then_inc(q_r2, 1)
                v.wait_ge(q_r2, k + 1)
                if k:
                    v.wait_ge(q_tr, 2 * k)
                v.tensor_scalar(wqb, wraw[:, k], -1.0, None, ALU.max).then_inc(q_bf, 1)

            def pair_evac(i, p, used):
                v.wait_ge(m_a, i + 1)
                v.tensor_copy(wA[:, :, bass.ts(i, P)], bank[2][:, 0:2 * P].rearrange("p (c n) -> p c n", c=2)).then_inc(m_ae, 1)
                v.wait_ge(m_b, i + 1)
                v.tensor_copy(wB[:, i, :], bank[3][:, 0:D]).then_inc(m_be, 1)
            with v.Fori(0, PAIRS1, 1) as i:
                pair_evac(i, 0, True)

            v.wait_ge(ld_x, N_X)
            v.wait_ge(tanh_done, 1)
            v.wait_ge(m_ae, PAIRS1)
            v.wait_ge(m_be, PAIRS1)

            def norm_of(ln, guard):
                def f(t, p, used):
                    if used:
                        guard(t)
                    normalise(v, ln, t, p)
                return f

            def a_max(t, p, used):
                if used:
                    held(v, a_mt, t - 1)
                for j in range(4):
                    b, gp = j // 2, j % 2
                    v.wait_ge(a_p1, 4 * t + j + 1)
                    v.tensor_reduce(mx1[:, p, gp, 8 * b:8 * b + 8], bank[1 + j % 2][:, :].rearrange("p (k n) -> p k n", k=8),
                                    AX.X, ALU.max).then_inc(a_mx, 1)

            def a_final(t, p, used):
                o = bank[6][:, 0:288].rearrange("p (h i) -> p h i", h=32)
                v.wait_ge(a_pv, t + 1)
                v.reciprocal(rec1[:, p], o[:, :, 8:9]).then_inc(a_rec, 1)
                v.wait_ge(a_rec, t + 1)
                v.tensor_tensor(att1[:, p], o[:, :, 0:8], rec1[:, p].broadcast_to([P, 32, 8]), ALU.mult).then_inc(a_att, 1)
                v.wait_ge(a_att, t + 1)
                v.scalar_tensor_tensor(xs[:, t, :], att1[:, p].rearrange("p h i -> p (h i)"), gT[:, 0:1], xs[:, t, :],
                                       ALU.mult, ALU.add).then_inc(a_x, 1)

            tiles_loop(v, D1, [(4, a_final), (0, lambda t, p, u: stats(v, ln1, t, p)),
                               (1, norm_of(ln1, lambda t: held(v, a_qt, t - 1))), (2, a_max)])

            if last_phase >= 2:
                v.wait_ge(a_x, TILES)
                v.wait_ge(q_ev, 6)

                def f_quant(t, p, used):
                    v.wait_ge(ln2.xn, t + 1)
                    v.tensor_reduce(gx[:, p, 0:1], ln2.out[:, p, :], AX.X, ALU.max, apply_absolute_value=True).then_inc(f_ab, 1)
                    v.wait_ge(f_ab, t + 1)
                    v.tensor_scalar(gx[:, p, 1:2], gx[:, p, 0:1], 1e-5, 1.0 / 127.0, ALU.max, ALU.mult).then_inc(f_c1, 1)
                    v.wait_ge(f_c1, t + 1)
                    v.reciprocal(gx[:, p, 2:3], gx[:, p, 1:2]).then_inc(f_c2, 1)
                    v.tensor_scalar(sg[:, p, :], gam[:, 0:2], gx[:, p, 1:2], None, ALU.mult).then_inc(f_sc, 1)
                    v.wait_ge(f_c2, t + 1)
                    if used:
                        held(v, f_tr, t - 1)
                    v.tensor_scalar(xm[:, p, :], ln2.out[:, p, :], gx[:, p, 2:3], MAGIC, ALU.mult, ALU.add).then_inc(f_xm, 1)

                def f_gv(t, p, used):
                    if used:
                        held(v, f_sil, t - 1)
                    v.wait_ge(f_sc, t + 1)
                    for k, (made, done, dst) in enumerate(((f_gp, f_g, gate), (f_vp, f_v, val))):
                        for j in range(2):
                            v.wait_ge(made, 2 * t + j + 1)
                            v.scalar_tensor_tensor(dst[:, p, j * 512:(j + 1) * 512], bank[1 + 2 * k + j][:, :], sg[:, p, k:k + 1],
                                                   bgv[:, k, j * 512:(j + 1) * 512], ALU.mult, ALU.add).then_inc(done, 1)

                def f_hidden(t, p, used):
                    v.wait_ge(f_sil, t + 1)
                    v.wait_ge(f_v, 2 * t + 2)
                    v.tensor_tensor(val[:, p], sil[:, p], val[:, p], ALU.mult).then_inc(f_h, 1)
                    v.wait_ge(f_h, t + 1)
                    v.tensor_reduce(gh[:, p, 0:1], val[:, p], AX.X, ALU.max, apply_absolute_value=True).then_inc(f_ha, 1)
                    v.wait_ge(f_ha, t + 1)
                    v.tensor_scalar(gh[:, p, 1:2], gh[:, p, 0:1], 1e-5, 1.0 / 127.0, ALU.max, ALU.mult).then_inc(f_h1, 1)
                    v.wait_ge(f_h1, t + 1)
                    v.reciprocal(gh[:, p, 2:3], gh[:, p, 1:2]).then_inc(f_h2, 1)
                    v.tensor_scalar(gh[:, p, 3:4], gh[:, p, 1:2], gam[:, 2:3], None, ALU.mult).then_inc(f_c3, 1)
                    v.wait_ge(f_h2, t + 1)
                    if used:
                        held(v, f_ht, t - 1)
                    v.tensor_scalar(hm[:, p], val[:, p], gh[:, p, 2:3], MAGIC, ALU.mult, ALU.add).then_inc(f_hm, 1)

                def f_final(t, p, used):
                    v.wait_ge(f_o, t + 1)
                    v.scalar_tensor_tensor(yb[:, p], bank[6][:, 0:D], gh[:, p, 3:4], bo[:, :], ALU.mult, ALU.add).then_inc(f_y, 1)
                    v.wait_ge(f_y, t + 1)
                    v.scalar_tensor_tensor(xs[:, t, :], yb[:, p], gT[:, 2:3], xs[:, t, :], ALU.mult, ALU.add).then_inc(f_x, 1)

                tiles_loop(v, D2, [(4, f_final), (2, f_gv), (0, lambda t, p, u: stats(v, ln2, t, p)),
                                   (1, norm_of(ln2, lambda t: None)), (1, f_quant), (2, f_hidden)])

            if last_phase >= 3:
                v.wait_ge(f_x, TILES)

                def l_max(t, p, used):
                    if used:
                        held(v, l_mt, t - 1)
                    for j in range(2):
                        v.wait_ge(l_p1, 2 * t + j + 1)
                        v.tensor_reduce(mx3[:, p, 8 * j:8 * j + 8], bank[2][:, :].rearrange("p (k n) -> p k n", k=8),
                                        AX.X, ALU.max).then_inc(l_mx, 1)

                def l_context(t, p, used):
                    if used:
                        held(v, l_o, t - 1)
                    for b in range(2):
                        v.wait_ge(l_pv, 2 * t + b + 1)
                        v.reciprocal(rec3[:, b], bank[6][:, :]).then_inc(l_rec, 1)
                        v.wait_ge(l_rec, 2 * t + b + 1)
                        v.tensor_tensor(cT[:, p, :, 64 * b:64 * b + 64], bank[5][:, :].rearrange("p (k n) -> p k n", k=8),
                                        rec3[:, b].rearrange("p (k n) -> p k n", k=8), ALU.mult).then_inc(l_c, 1)

                def l_final(t, p, used):
                    v.wait_ge(l_o, t + 1)
                    v.scalar_tensor_tensor(xs[:, t, :], bank[7][:, 0:D], gT[:, 1:2], xs[:, t, :], ALU.mult, ALU.add).then_inc(l_x, 1)

                tiles_loop(v, D3, [(5, l_final), (4, l_context), (0, lambda t, p, u: stats(v, ln3, t, p)),
                                   (1, norm_of(ln3, lambda t: held(v, l_tr, t - 1))), (2, l_max)])

            if last_phase >= 4:
                v.wait_ge(l_x, TILES)

                def e_route(t, p, used):
                    v.wait_ge(e_sc, t + 1)
                    v.tensor_tensor(tm4[:, p], bank[1][:, 0:8], gb8[:, 0, :], ALU.add).then_inc(e_s1, 1)
                    v.wait_ge(e_s1, t + 1)
                    if used:
                        held(v, e_ex, t - 1)
                    v.tensor_tensor(sc4[:, p], tm4[:, p], gb8[:, 1, :], ALU.add).then_inc(e_s2, 1)
                    v.wait_ge(e_s2, t + 1)
                    v.tensor_reduce(mxn[:, p], sc4[:, p], AX.X, ALU.max, negate=True).then_inc(e_m, 1)
                    sj = sc4[:, p].unsqueeze(1).broadcast_to([P, 8, 8])
                    se = sc4[:, p].unsqueeze(2).broadcast_to([P, 8, 8])
                    v.tensor_tensor(gt[:, p], sj, se, ALU.is_gt).then_inc(e_g1, 1)
                    v.tensor_tensor(eq[:, p], sj, se, ALU.is_equal).then_inc(e_g2, 1)
                    v.wait_ge(e_g2, t + 1)
                    v.tensor_tensor(eq[:, p], eq[:, p], before[:, :, :], ALU.mult).then_inc(e_g3, 1)
                    v.wait_ge(e_g3, t + 1)
                    v.wait_ge(e_g1, t + 1)
                    v.tensor_tensor(gt[:, p], gt[:, p], eq[:, p], ALU.add).then_inc(e_g4, 1)
                    v.wait_ge(e_g4, t + 1)
                    v.tensor_reduce(rank[:, p], gt[:, p], AX.X, ALU.add).then_inc(e_rk, 1)

                def e_comb(t, p, used):
                    v.wait_ge(e_rk, t + 1)
                    v.wait_ge(e_ex, t + 1)
                    v.scalar_tensor_tensor(es4[:, p], rank[:, p], 1.5, ex4[:, p], ALU.is_lt, ALU.mult).then_inc(e_es, 1)
                    v.wait_ge(e_es, t + 1)
                    v.tensor_reduce(z4[:, p, 0:1], es4[:, p], AX.X, ALU.add).then_inc(e_z, 1)
                    v.wait_ge(e_z, t + 1)
                    v.reciprocal(z4[:, p, 1:2], z4[:, p, 0:1]).then_inc(e_rz, 1)
                    v.wait_ge(e_rz, t + 1)
                    if used:
                        held(v, e_ct, t - 1)
                    v.tensor_scalar(comb[:, p], es4[:, p], z4[:, p, 1:2], None, ALU.mult).then_inc(e_cb, 1)
                    v.wait_ge(e_cb, t + 1)
                    v.tensor_copy(cpart[:, p, 0:8], comb[:, p]).then_inc(e_c1, 1)
                    v.wait_ge(e_c1, t + 1)
                    v.tensor_tensor(cres[:, p, 0], comb[:, p], cpart[:, p, 0:8], ALU.subtract).then_inc(e_c2, 1)
                    v.wait_ge(e_c2, t + 1)
                    v.tensor_copy(cpart[:, p, 8:16], cres[:, p, 0]).then_inc(e_c3, 1)
                    v.wait_ge(e_c3, t + 1)
                    v.tensor_tensor(cres[:, p, 1], cres[:, p, 0], cpart[:, p, 8:16], ALU.subtract).then_inc(e_c4, 1)
                    v.wait_ge(e_c4, t + 1)
                    v.tensor_copy(cpart[:, p, 16:24], cres[:, p, 1]).then_inc(e_c5, 1)

                def e_scale(t, p, used):
                    if used:
                        held(v, e_y, t - 1)
                    for c, (j0, j1) in enumerate(CHUNKS4):
                        v.wait_ge(e_sl, 3 * t + c + 1)
                        v.wait_ge(e_cb2, 3 * t + c + 1)
                        v.tensor_tensor(hs[:, p, j0 * P:j1 * P], sh4[:, p, j0 * P:j1 * P], bank[5 + c % 2][:, 0:(j1 - j0) * P],
                                        ALU.mult).then_inc(e_hs, 1)

                def e_final(t, p, used):
                    v.wait_ge(e_y, t + 1)
                    v.scalar_tensor_tensor(xs[:, t, :], bank[7][:, 0:D], gT[:, 3:4], xs[:, t, :], ALU.mult, ALU.add).then_inc(e_x, 1)

                v.wait_ge(ld_w1, 16)
                tiles_loop(v, D4, [(4, e_final), (3, e_scale), (0, lambda t, p, u: stats(v, ln4, t, p)),
                                   (1, norm_of(ln4, lambda t: held(v, e_tr, t - 1))), (2, e_comb), (1, e_route)])


def constants():
    c = {}
    c["ident"] = np.eye(P, dtype=np.float32)
    r = np.arange(P)
    c["kvmask"] = ((r[:, None] % 64) // 8 == np.arange(8)[None, :]).astype(np.float32)
    c["rowhalf"] = (r[:, None] // 64 == np.arange(2)[None, :]).astype(np.float32)
    sel0 = np.zeros((16, 8, P), np.float32)
    for b in range(2):
        for pair in range(4):
            for k in range(2):
                sel0[8 * b + 2 * pair + k, 4 * b + pair, 64 * k:64 * k + 64] = 1
    c["sel0"] = sel0
    sel1 = np.zeros((16, PAIRS1, P), np.float32)
    for pair in range(PAIRS1):
        for k in range(2):
            sel1[2 * pair + k, pair, 64 * k:64 * k + 64] = 1
    c["sel1"] = sel1
    unit = np.arange(EB * P) // EH
    c["sel3"] = np.tile((unit[None, :] == np.arange(8)[:, None]).astype(np.float32).reshape(8, EB, P), (3, 1, 1))
    c["ones2"] = np.kron(np.eye(2), np.ones((64, 64))).astype(np.float32)
    f = np.float32
    inv = (f(1.0) / np.power(f(10000.0), np.arange(0, CD, 2, dtype=f) / f(CD), dtype=f)).astype(f)
    freqs = np.arange(SEQ, dtype=f)[:, None] * inv[None, :]
    sin = np.repeat(np.sin(freqs), 2, axis=-1).astype(f)
    cos = np.repeat(np.cos(freqs), 2, axis=-1).astype(f)
    sign = np.where(np.arange(CD) < CD // 2, -1, 1).astype(f)
    def diagonal(a):
        return np.kron(np.eye(2, dtype=f), a).reshape(P, 2, 64).astype(f)

    c["cosN"], c["sinN"] = diagonal(cos), diagonal(sin * sign)
    c["cosT"], c["sinT"] = diagonal(cos.T), diagonal((sin * sign).T)
    c["before"] = np.broadcast_to((np.arange(8)[None, :] < np.arange(8)[:, None]).astype(np.float32), (P, 8, 8))
    return c


def kernel(x, ctx_512, g_xattn, g_ffn, L0_ffn_gate_w, L0_ffn_gate_b, L0_ffn_val_w, L0_ffn_val_b, L0_ffn_out_w,
           L0_ffn_out_b, L1_xattn_Wq, L1_xattn_w_kc_q, L1_xattn_w_kc_kv, L1_xattn_W_qr, L1_xattn_W_kr, L1_xattn_Wo,
           L1_ffn_gate_w, L1_ffn_gate_b, L1_ffn_bias, L1_ffn_w1, L1_ffn_b1, L1_ffn_w2, L1_ffn_b2):
    import concourse.bacc as bacc
    from concourse.bass_utils import run_bass_kernel_spmd

    arrays = dict(constants())
    ctx = np.asarray(ctx_512)
    ctxT = ctx.transpose(2, 0, 1)
    arrays.update(
        x=np.asarray(x).reshape(BATCH * SEQ, D),
        ctx=ctx, ctxT=ctxT, ctxTs=np.concatenate([ctxT[32:], ctxT[:32]]),
        g=np.broadcast_to(np.concatenate([np.asarray(g_xattn), np.asarray(g_ffn)])[None, :], (P, 4)),
        gw=np.asarray(L0_ffn_gate_w), vw=np.asarray(L0_ffn_val_w),
        ow=np.asarray(L0_ffn_out_w).reshape(2, P, HID).reshape(2 * P, HID),
        bg=np.asarray(L0_ffn_gate_b)[None, :], bv=np.asarray(L0_ffn_val_b)[None, :], bo=np.asarray(L0_ffn_out_b)[None, :],
        Wq=np.asarray(L1_xattn_Wq).reshape(HEADS1, KD, D), Cq=np.asarray(L1_xattn_w_kc_q),
        Dq=np.asarray(L1_xattn_W_qr), ET=np.asarray(L1_xattn_W_kr).transpose(0, 2, 1),
        Ckv=np.asarray(L1_xattn_w_kc_kv), WoT=np.asarray(L1_xattn_Wo).T.reshape(HEADS1, KD, D),
        gwT=np.asarray(L1_ffn_gate_w).T.reshape(2, P, EXPERTS).transpose(1, 0, 2),
        gb=np.asarray(L1_ffn_gate_b)[None, :], gbias=np.asarray(L1_ffn_bias)[None, :],
        w1T=np.asarray(L1_ffn_w1).reshape(EXPERTS * EH, D).T.reshape(2, P, EXPERTS * EH).transpose(1, 0, 2),
        b1=np.asarray(L1_ffn_b1).reshape(EB, P).T,
        w2T=np.asarray(L1_ffn_w2).transpose(0, 2, 1).reshape(EB, P, D).transpose(1, 0, 2),
        b2=np.asarray(L1_ffn_b2),
    )
    arrays = {f"in_{k}": np.ascontiguousarray(v) for k, v in arrays.items()}
    nc = bacc.Bacc("TRN2", target_bir_lowering=False, num_devices=1)
    d = {k[3:]: nc.dram_tensor(k, v.shape, mybir.dt.from_np(v.dtype), kind="ExternalInput").ap()
         for k, v in arrays.items()}
    out = nc.dram_tensor("out", (BATCH * SEQ, D), F32, kind="ExternalOutput").ap()
    build(nc, d, out, LAST_PHASE)
    got = run_bass_kernel_spmd(nc, [arrays], core_ids=[0])
    return got.results[0]["out"].reshape(BATCH, SEQ, D)


LAST_PHASE = 4
```

```python
from contextlib import ExitStack

import numpy as np

import concourse.bass as bass
from concourse import mybir

ALU = mybir.AluOpType
ACT = mybir.ActivationFunctionType
AX = mybir.AxisListType
F32 = mybir.dt.float32
F16 = mybir.dt.float16
BF16 = mybir.dt.bfloat16

P = 128
BATCH, SEQ, D = 64, 64, 256
TILES = BATCH * SEQ // P
CD = 64
EPS = 1e-5
HID = 1024
HEADS1 = 16
KD, CQ, RR = 128, 192, 64
PAIRS1 = HEADS1 // 2
EXPERTS, EH = 8, 176
EB = EXPERTS * EH // P
ROUND0 = 1536.0
MAGIC = float(2 ** 23 + 0x6600)
S_Q = 2.0 ** 6
S_X = 2.0 ** 8
S_K = 2.0 ** 4
S_A = 2.0 ** 8
S_L = 2.0 ** 6
S_P = 8.0
S_R = 2.0 ** 20
S_C = 2.0 ** 6
S_B = 2.0 ** 6
S_W1 = 2.0 ** 6
S_H = 2.0 ** 6
S_W2 = 2.0 ** 6
BIG = float(1.5 * 2 ** 23)


def tiles_loop(eng, depth, stages):
    def iteration(n, parity, static):
        for lag, stage in stages:
            t = n - lag
            if static and not 0 <= t < TILES:
                continue
            stage(t, (parity - lag) % 2, (not static) or t >= 2)

    first = depth + 2 + depth % 2
    for n in range(first):
        iteration(n, n % 2, True)
    with eng.Fori(first, TILES - 1, 2) as n:
        iteration(n, 0, False)
        iteration(n + 1, 1, False)
    for n in range(TILES, TILES + depth):
        iteration(n, n % 2, True)


def build(nc, d, out, last_phase=4):
    with ExitStack() as ctx:
        def sb(name, shape, dt=F32):
            return ctx.enter_context(nc.sbuf_tensor(name, shape, dt))

        def sem(name):
            return ctx.enter_context(nc.semaphore(name))

        xs = sb("xs", [P, TILES, D])
        ctx2 = sb("ctx2", [P, BATCH, CD])
        khT = sb("khT", [P, BATCH, SEQ], F16)
        klT = sb("klT", [P, BATCH, SEQ], F16)
        gT = sb("gT", [P, 4])
        graw = sb("graw", [P, 4])
        g3s = sb("g3s", [P, 2])
        idf = sb("idf", [P, P])
        id16 = sb("id16", [P, P], F16)
        idb = sb("idb", [P, P], BF16)
        half = sb("half", [P, 1])
        kvmask = sb("kvmask", [P, 8])
        rowhalf = sb("rowhalf", [P, 2])
        lomask = sb("lomask", [P, 2, 8])
        wgv = sb("wgv", [P, 2, 2 * HID], BF16)
        wow = sb("wow", [P, 8, D], BF16)
        gam = sb("gam", [P, 4])
        bgv = sb("bgv", [P, 2, HID])
        bo = sb("bo", [P, D])
        wA = sb("wA", [P, 2, 2, HEADS1 * CD], F16)
        wB = sb("wB", [P, 2, PAIRS1, D], F16)
        cosT = sb("cosT", [P, 2, SEQ])
        sinT = sb("sinT", [P, 2, SEQ])
        cosN = sb("cosN", [P, 2, CD])
        sinN = sb("sinN", [P, 2, CD])
        sel1 = sb("sel1", [16, PAIRS1, P], BF16)
        selr = sb("selr", [48, PAIRS1, P], F16)
        cnt = sb("cnt", [P, PAIRS1, 16], F16)
        w1T = sb("w1T", [P, 2, 2, EXPERTS * EH], F16)
        w2T = sb("w2T", [P, 2, EB, D], F16)
        b1c = sb("b1c", [P, EB])
        gwT = sb("gwT", [P, 2, EXPERTS])
        gw16 = sb("gw16", [P, 2, 2, EXPERTS], F16)
        gb8 = sb("gb8", [P, 2, EXPERTS])
        before = sb("before", [P, 8, 8])
        b2s = sb("b2s", [EXPERTS, D])
        sel3 = sb("sel3", [24, EB, P], BF16)
        ARENA = 17 * 1024 + 256
        arena = sb("arena", [P, ARENA])
        bank = [ctx.enter_context(nc.psum_tensor(f"bank{i}", [P, 512], F32)) for i in range(8)]

        class Arena:
            def __init__(self):
                self.at = 0

            def take(self, shape, dt=F32, rows=P):
                n = int(np.prod(shape))
                words = n if dt == F32 else (n + 1) // 2
                a = arena[0:rows, self.at:self.at + words]
                self.at += words + words % 2
                assert self.at <= ARENA
                if dt != F32:
                    a = a.bitcast(dt)
                names = "abcdef"[:len(shape)]
                if len(shape) > 1:
                    a = a.rearrange(f"p ({' '.join(names)}) -> p {' '.join(names)}",
                                    **dict(zip(names, shape)))
                return a

        class Norm:
            bn, agg, var, rstd, xn = (sem(f"ln_{n}") for n in ("bn", "agg", "var", "rstd", "xn"))

            def __init__(self, ph, mem, scale):
                self.scale = scale
                self.base = ph * TILES
                self.stat, self.mv, self.ve, self.rs = (
                    mem.take([2, 6]), mem.take([2, 2]), mem.take([2, 1]), mem.take([2, 1]))
                self.out = mem.take([2, D])

        passed = sem("passed")

        def held(eng, s, value):
            eng.wait_ge(s, value)
            eng.sem_inc(passed, 1)

        def stats(v, ln, t, p):
            v.bn_stats(ln.stat[:, p, :], xs[:, t, :]).then_inc(ln.bn, 1)
            held(v, ln.bn, ln.base + t + 1)
            v.bn_aggr(ln.mv[:, p, :], ln.stat[:, p, :]).then_inc(ln.agg, 1)
            v.wait_ge(ln.agg, ln.base + t + 1)
            v.tensor_scalar(ln.ve[:, p, :], ln.mv[:, p, 1:2], EPS, ln.scale ** -2, ALU.add, ALU.mult).then_inc(ln.var, 1)

        def rstd(g, ln, t, p):
            g.wait_ge(ln.var, ln.base + t + 1)
            g.tensor_tensor(ln.rs[:, p, :], ln.ve[:, p, :], half[:, :], ALU.pow).then_inc(ln.rstd, 1)

        def normalise(v, ln, t, p):
            v.wait_ge(ln.rstd, ln.base + t + 1)
            dst, src = ln.out[:, p, :], xs[:, t, :]
            if ln is ln1:
                dst = dst.rearrange("n (g k i) -> n k g i", k=8, g=4)
                src = src.rearrange("n (k g i) -> n k g i", k=8, g=4)
            v.tensor_scalar(dst, src, ln.mv[:, p, 0:1], ln.rs[:, p, :], ALU.subtract, ALU.mult).then_inc(ln.xn, 1)

        m0 = Arena()
        kTf = m0.take([BATCH, SEQ])
        sel1f = m0.take([PAIRS1, P], rows=16)
        sel3f = m0.take([EB, P], rows=24)
        selrf = m0.take([PAIRS1, P], rows=48)
        cntf = m0.take([PAIRS1, 16])
        m0b = Arena()
        wq_in = m0b.take([2, 2, D])
        cq_in = m0b.take([2, 2, CQ])
        dq_in = m0b.take([2, 2, 2, RR], rows=96)
        et_in = m0b.take([2, 2, CD], rows=RR)
        ckv_in = m0b.take([2, 2, CD])
        wo_in = m0b.take([2, 2, D])
        ysb = m0b.take([2, 2, D], rows=96)
        zsb = m0b.take([2, D], rows=RR)
        m0c = Arena()
        m0c.at = m0d_at = max(m0.at, m0b.at)
        wraw = m0c.take([3, 8 * D])
        wabs = m0c.take([3, 1])
        wqb = m0c.take([8 * D], BF16)
        rgam = m0c.take([4])
        ones_sum = m0c.take([P])
        m0d = Arena()
        m0d.at = m0d_at
        w1f = m0d.take([2, EXPERTS * EH])
        w2f = m0d.take([EB, D])

        ld_const, ld_x, ld_kT, ld_w0, ld_w1 = (sem(n) for n in ("ld_const", "ld_x", "ld_kT", "ld_w0", "ld_w1"))
        consts_done, tanh_done, g_done = sem("consts_done"), sem("tanh_done"), sem("g_done")
        k_hi, k_lo, w_hi, w_lo, m_ah, m_bh = (sem(n) for n in ("k_hi", "k_lo", "w_hi", "w_lo", "m_ah", "m_bh"))
        q_abs, q_sum, q_gam, q_rg, q_r1, q_r2, q_bf, q_tr, q_ev = (
            sem(f"q_{n}") for n in ("abs", "sum", "gam", "rg", "r1", "r2", "bf", "tr", "ev"))
        m_ld = [sem("m_ld0"), sem("m_ld1")]
        m_y, m_ye, m_z, m_ze, m_a, m_ae, m_b, m_be = (
            sem(f"m_{n}") for n in ("y", "ye", "z", "ze", "a", "ae", "b", "be"))

        const_loads = [
            (graw[:, :], d["g"]), (idf[:, :], d["ident"]), (kvmask[:, :], d["kvmask"]), (rowhalf[:, :], d["rowhalf"]),
            (lomask[:, :, :], d["lomask"]), (sel1f, d["sel1"]), (sel3f, d["sel3"]), (selrf, d["selr"]), (cntf, d["cnt"]),
            (cosT[:, :, :], d["cosT"]), (sinT[:, :, :], d["sinT"]),
            (cosN[:, :, :], d["cosN"]), (sinN[:, :, :], d["sinN"]), (before[:, :, :], d["before"]),
            (bo[:, :], d["bo"].broadcast_to([P, D])), (bgv[:, 0, :], d["bg"].broadcast_to([P, HID])),
            (bgv[:, 1, :], d["bv"].broadcast_to([P, HID])),
            (gb8[:, 0, :], d["gb"].broadcast_to([P, EXPERTS])), (gb8[:, 1, :], d["gbias"].broadcast_to([P, EXPERTS])),
            (b1c[:, :], d["b1"]), (b2s[:, :], d["b2"]), (gwT[:, :, :], d["gwT"]),
        ]
        N_CONST = 16 * len(const_loads)
        N_X = 16 * 3

        m1 = Arena()
        ln1 = Norm(0, m1, S_Q)
        qA = m1.take([2, 2, 4, SEQ], F16)
        qB = m1.take([2, 2, 4, SEQ], F16)
        kA = m1.take([2, 2, 8, SEQ], F16)
        kB = m1.take([2, 2, 8, SEQ], F16)
        mx1 = m1.take([2, 2, 16])
        PT1 = m1.take([2, 4, 512])
        vx = m1.take([2, 8, 18])
        rec1 = m1.take([2, 32, 1])
        att1 = m1.take([2, 32, 8])
        (a_qt, a_qe, a_ql, a_kx, a_kb, a_p1, a_mx, a_mt, a_nm, a_s, a_exp, a_vx, a_pv, a_rec, a_att,
         a_x, a_vz) = (sem(f"a_{n}") for n in (
             "qt", "qe", "ql", "kx", "kb", "p1", "mx", "mt", "nm", "s", "exp", "vx", "pv", "rec", "att",
             "x", "vz"))
        D1 = 4

        m2 = Arena()
        ln2 = Norm(1, m2, 1.0)
        gx = m2.take([2, 4])
        sg = m2.take([2, 2])
        xm = m2.take([2, D])
        xqT = m2.take([2, 2, P], BF16)
        gate = m2.take([2, HID])
        val = m2.take([2, HID])
        sil = m2.take([2, HID])
        hm = m2.take([2, HID])
        gh = m2.take([2, 4])
        hqT = m2.take([2, 8, P], BF16)
        yb = m2.take([2, D])
        (f_ab, f_c1, f_c2, f_c3, f_sc, f_xm, f_tr, f_xe, f_gp, f_vp, f_g, f_v, f_sil, f_h, f_ha, f_h1, f_h2,
         f_hm, f_ht, f_he, f_o, f_y, f_x) = (sem(f"f_{n}") for n in (
             "ab", "c1", "c2", "c3", "sc", "xm", "tr", "xe", "gp", "vp", "g", "v", "sil", "h", "ha", "h1",
             "h2", "hm", "ht", "he", "o", "y", "x"))
        D2 = 4

        m3 = Arena()
        ln3 = Norm(2, m3, S_X)
        xT3 = m3.take([2, 2, 2, P], F16)
        kin = m3.take([2, 2, 2, SEQ])
        kt1 = m3.take([2, 2, 2, SEQ])
        kt2 = m3.take([2, 2, 2, SEQ])
        kbd = m3.take([2, 2, 2, P], F16)
        vt1 = m3.take([2, 2, 2, CD])
        vt2 = m3.take([2, 2, 2, CD])
        vbd = m3.take([2, 2, 2, P], F16)
        qa = m3.take([2, 2, PAIRS1, P], F16)
        mx3 = m3.take([2, HEADS1])
        nm3 = m3.take([2, P], BF16, rows=16)
        PTf = m3.take([2, 512])
        PT3 = m3.take([2, 2, 2, 512], F16)
        rs3 = m3.take([2, P], rows=16)
        rr3 = m3.take([2, P], F16, rows=48)
        rb3 = m3.take([2, 512])
        cf = m3.take([2, 2, 512])
        cT = m3.take([2, 2, PAIRS1, P], F16)
        l_kin = [sem("l_kin0"), sem("l_kin1")]
        (l_tr, l_te, l_tl, l_qa, l_qe, l_ql, l_k1, l_k2, l_k3, l_kb, l_v1, l_v2, l_v3, l_vb, l_p1, l_mx, l_mt,
         l_nm, l_s, l_exp, l_ph, l_pl, l_pv, l_sum, l_rc, l_rh, l_rl, l_rb, l_re, l_c, l_ch, l_cl, l_o, l_x,
         l_z) = (sem(f"l_{n}") for n in (
             "tr", "te", "tl", "qa", "qe", "ql", "k1", "k2", "k3", "kb", "v1", "v2", "v3", "vb", "p1", "mx",
             "mt", "nm", "s", "exp", "ph", "pl", "pv", "sum", "rc", "rh", "rl", "rb", "re", "c", "ch", "cl",
             "o", "x", "z"))
        D3 = 5

        m4 = Arena()
        ln4 = Norm(3, m4, S_X)
        xT4 = m4.take([2, 2, 2, P], F16)
        sc4 = m4.take([2, 8])
        tm4 = m4.take([2, 8])
        gt = m4.take([2, 8, 8])
        eq = m4.take([2, 8, 8])
        rank = m4.take([2, 8])
        half4 = m4.take([2, 8])
        mid4 = m4.take([2, 1])
        dif4 = m4.take([2, 8])
        th4 = m4.take([2, 8])
        es4 = m4.take([2, 8])
        comb = m4.take([2, 8])
        cpart = m4.take([2, 24], BF16)
        cres = m4.take([2, 2, 8])
        cT16 = m4.take([2, P], BF16, rows=24)
        cTf = m4.take([2, P], F32, rows=8)
        hs = m4.take([2, 2, EB * P], F16)
        hf = m4.take([2, EB * P])
        sh4 = m4.take([2, EB * P])
        xo = m4.take([2, D])
        (e_tr, e_te, e_tl, e_hf, e_hh, e_sc, e_s1, e_rt, e_md, e_th, e_rk, e_cc, e_ct, e_cte, e_h, e_sl, e_cb2, e_hs, e_y, e_x, e_out) = (
             sem(f"e_{n}") for n in (
                 "tr", "te", "tl", "hf", "hh", "sc", "s1", "rt", "md", "th", "rk", "cc", "ct", "cte", "h", "sl", "cb2",
                 "hs", "y", "x", "out"))
        D4 = 5
        CHUNKS4 = [(0, 4), (4, 8), (8, EB)]

        block = ctx.enter_context(nc.Block())

        @block.sync
        def _(sp):
            for dst, src in const_loads:
                sp.dma_start(dst, src).then_inc(ld_const, 16)
            for r in range(2):
                sp.dma_start(kTf[64 * r:64 * r + 64], d["ctxT"]).then_inc(ld_kT, 16)
            for i, name in enumerate(("gw", "vw")):
                sp.dma_start(wraw[:, i, :], d[name].rearrange("(c p) i -> p c i", p=P)).then_inc(ld_w0, 16)
            sp.dma_start(wraw[:, 2, :], d["ow"].rearrange("(c p) i -> p c i", p=P)).then_inc(ld_w0, 16)
            sp.dma_start(xs[:, :, :], d["x"].rearrange("(t p) i -> p t i", p=P)).then_inc(ld_x, 16)
            for r in range(2):
                sp.dma_start(ctx2[64 * r:64 * r + 64], d["ctx"].rearrange("b t i -> t b i")).then_inc(ld_x, 16)
            sp.wait_ge(q_ev, 6)
            sp.dma_start(w1f, d["w1T"]).then_inc(ld_w1, 16)
            sp.dma_start(w2f, d["w2T"]).then_inc(ld_w1, 16)

            def pair_weights(i, p, used):
                if used:
                    sp.wait_ge(m_be, i - 1)
                    sp.wait_ge(m_ae, i - 1)
                hs2 = bass.ts(i, 2)
                sp.dma_start(wq_in[:, p], d["Wq"][hs2].rearrange("h k i -> k h i")).then_inc(m_ld[p], 16)
                sp.dma_start(cq_in[:, p], d["Cq"][hs2].rearrange("h k q -> k h q")).then_inc(m_ld[p], 16)
                for h in range(2):
                    sp.dma_start(dq_in[:, p, h], d["Dq"][bass.ts(i, 2)][h].rearrange("(c q) r -> q c r", q=96)).then_inc(m_ld[p], 16)
                sp.dma_start(et_in[:, p], d["ET"][hs2].rearrange("h r i -> r h i")).then_inc(m_ld[p], 16)
                sp.dma_start(ckv_in[:, p], d["Ckv"][hs2].rearrange("h k i -> k h i")).then_inc(m_ld[p], 16)
                sp.dma_start(wo_in[:, p], d["WoT"][hs2].rearrange("h k o -> k h o")).then_inc(m_ld[p], 16)

            sp.wait_ge(k_lo, 1)
            sp.wait_ge(consts_done, 1)
            pair_weights(0, 0, False)
            pair_weights(1, 1, False)
            with sp.Fori(2, PAIRS1 - 1, 2) as i:
                pair_weights(i, 0, True)
                pair_weights(i + 1, 1, True)

            if last_phase >= 3:
                sp.wait_ge(f_x, TILES)

                def context(t, p, used):
                    if used:
                        sp.wait_ge(l_k2, t - 1)
                        sp.wait_ge(l_k1, t - 1)
                    for r in range(2):
                        rows = slice(64 * r, 64 * r + 64)
                        src = d["ctxT"][:, bass.ts(t, 2), :]
                        src2 = d["ctxTs"][:, bass.ts(t, 2), :]
                        sp.dma_start(kin[rows, p, 0], src).then_inc(l_kin[p], 16)
                        sp.dma_start(kin[rows, p, 1], src2).then_inc(l_kin[p], 16)
                tiles_loop(sp, 0, [(0, context)])

            ready = {1: a_x, 2: f_x, 3: l_x, 4: e_x}[last_phase]
            src = xs
            if last_phase < 4:
                for t in range(TILES):
                    sp.wait_ge(ready, t + 1)
                    sp.dma_start(out[bass.ts(t, P), :], src[:, t, :]).then_inc(e_out, 16)
            else:
                def store(t, p, used):
                    sp.wait_ge(e_x, t + 1)
                    sp.dma_start(out[bass.ts(t, P), :], xs[:, t, :]).then_inc(e_out, 16)
                tiles_loop(sp, 0, [(0, store)])
            sp.wait_ge(e_out, 16 * TILES)

        @block.gpsimd
        def _(g):
            g.wait_ge(ld_const, N_CONST)
            g.wait_ge(ld_x, N_X)
            g.wait_ge(consts_done, 1)

            g.wait_ge(m_be, PAIRS1)
            g.wait_ge(m_ae, PAIRS1)
            g.wait_ge(w_lo, 2)
            for p in range(2):
                g.tensor_copy(vx[:, p].rearrange("t n (k i) -> t n k i", k=2)[:, :, :, 8],
                              rowhalf[:, :].unsqueeze(1).broadcast_to([P, 8, 2]))

            def a_keys(t, p, used):
                if used:
                    g.wait_ge(a_s, 4 * t - 4)
                src = khT[:, bass.ts(t, 2), :]
                g.tensor_tensor(kA[:, p], src.unsqueeze(2).broadcast_to([P, 2, 8, SEQ]),
                                kvmask[:, :].unsqueeze(1).unsqueeze(3).broadcast_to([P, 2, 8, SEQ]), ALU.mult).then_inc(a_kx, 1)
                src = klT[:, bass.ts(t, 2), :]
                g.tensor_tensor(kB[:, p], src.unsqueeze(2).broadcast_to([P, 2, 8, SEQ]),
                                lomask[:, :, :].unsqueeze(3).broadcast_to([P, 2, 8, SEQ]), ALU.mult).then_inc(a_kb, 1)

            def a_values(t, p, used):
                if used:
                    held(g, a_pv, t - 1)
                g.tensor_tensor(vx[:, p].rearrange("t n (k i) -> t n k i", k=2)[:, :, :, 0:8],
                                ctx2[:, bass.ts(t, 2), :].rearrange("t b (n k i) -> t (b n) k i", n=4, k=2),
                                rowhalf[:, :].unsqueeze(1).unsqueeze(3).broadcast_to([P, 8, 2, 8]),
                                ALU.mult).then_inc(a_vx, 1)

            tiles_loop(g, D1, [(0, lambda t, p, u: rstd(g, ln1, t, p)), (1, a_keys), (2, a_values)])

            if last_phase >= 2:
                tiles_loop(g, D2, [(0, lambda t, p, u: rstd(g, ln2, t, p))])
            if last_phase >= 3:
                g.wait_ge(f_x, TILES)
                def twice(x, n):
                    return x.unsqueeze(2).broadcast_to([P, 2, 2, n])

                def table(x, n):
                    return x.unsqueeze(1).broadcast_to([P, 2, 2, n])

                def l_keys(t, p, used):
                    g.wait_ge(l_kin[p], 32 * t + (64 - 32 * p))
                    g.tensor_tensor(kt1[:, p], twice(kin[:, p, 0], SEQ), table(cosT[:, :, :], SEQ), ALU.mult).then_inc(l_k1, 1)
                    g.tensor_tensor(kt2[:, p], twice(kin[:, p, 1], SEQ), table(sinT[:, :, :], SEQ), ALU.mult).then_inc(l_k2, 1)
                    g.wait_ge(l_k1, t + 1)
                    g.wait_ge(l_k2, t + 1)
                    g.tensor_tensor(kt1[:, p], kt1[:, p], kt2[:, p], ALU.add).then_inc(l_k3, 1)
                    held(g, l_k3, t + 1)
                    if used:
                        held(g, l_s, 2 * t - 2)
                    flat = kt1[:, p].rearrange("p b r n -> p b (r n)")
                    g.tensor_copy(kbd[:, p, 0], flat).then_inc(l_kb, 1)
                    g.wait_ge(l_kb, 2 * t + 1)
                    g.tensor_tensor(kbd[:, p, 1], flat, kbd[:, p, 0], ALU.subtract).then_inc(l_kb, 1)

                def l_values(t, p, used):
                    src = ctx2[:, bass.ts(t, 2), :]
                    g.tensor_tensor(vt1[:, p], twice(src, CD), table(cosN[:, :, :], CD), ALU.mult).then_inc(l_v1, 1)
                    for h in range(2):
                        lo = slice(32 * h, 32 * h + 32)
                        hi = slice(32 - 32 * h, 64 - 32 * h)
                        last = g.tensor_tensor(vt2[:, p, :, :, lo], twice(src[:, :, hi], 32), table(sinN[:, :, lo], 32), ALU.mult)
                    last.then_inc(l_v2, 1)
                    g.wait_ge(l_v1, t + 1)
                    g.wait_ge(l_v2, t + 1)
                    g.tensor_tensor(vt1[:, p], vt1[:, p], vt2[:, p], ALU.add).then_inc(l_v3, 1)
                    held(g, l_v3, t + 1)
                    if used:
                        held(g, l_pv, 2 * t - 2)
                    flat = vt1[:, p].rearrange("p b r n -> p b (r n)")
                    g.tensor_copy(vbd[:, p, 0], flat).then_inc(l_vb, 1)
                    g.wait_ge(l_vb, 2 * t + 1)
                    g.tensor_tensor(vbd[:, p, 1], flat, vbd[:, p, 0], ALU.subtract).then_inc(l_vb, 1)

                tiles_loop(g, D3, [(0, lambda t, p, u: rstd(g, ln3, t, p)), (3, l_values), (1, l_keys)])
            if last_phase >= 4:
                tiles_loop(g, D4, [(0, lambda t, p, u: rstd(g, ln4, t, p))])

        @block.scalar
        def _(a):
            a.wait_ge(ld_const, N_CONST)
            a.activation(gT[:, :], graw[:, :], ACT.Tanh).then_inc(tanh_done, 1)
            a.wait_ge(ld_kT, 32)
            a.activation(khT[:, :, :], kTf, ACT.Copy, scale=S_K).then_inc(k_hi, 1)
            for j in range(6):
                a.wait_ge(q_tr, j + 1)
                src = bank[j % 2][:, :].bitcast(BF16)
                if j < 4:
                    k, m = j // 2, j % 2
                    dst = wgv[:, m, k * HID:(k + 1) * HID]
                else:
                    m = j - 4
                    dst = wow[:, 4 * m:4 * m + 4, :]
                a.activation(dst, src if j < 4 else src.rearrange("p (c i) -> p c i", c=4), ACT.Copy).then_inc(q_ev, 1)

            def pair_evac(i, p, used):
                for h in range(2):
                    a.wait_ge(m_y, 2 * i + h + 1)
                    a.activation(ysb[:, h, :, :], bank[0][0:96, :].rearrange("q (c i) -> q c i", c=2), ACT.Copy).then_inc(m_ye, 1)
                    a.wait_ge(m_z, 2 * i + h + 1)
                    a.activation(zsb[:, h, :], bank[1][0:RR, 0:D], ACT.Copy).then_inc(m_ze, 1)
                a.wait_ge(m_a, i + 1)
                a.activation(wA[:, 0, :, bass.ts(i, P)], bank[2][:, 0:2 * P].rearrange("p (c n) -> p c n", c=2),
                             ACT.Copy, scale=S_A).then_inc(m_ah, 1)
                a.wait_ge(m_b, i + 1)
                a.activation(wB[:, 0, i, :], bank[3][:, 0:D], ACT.Copy, scale=S_B).then_inc(m_bh, 1)

            with a.Fori(0, PAIRS1, 1) as i:
                pair_evac(i, 0, True)
            a.wait_ge(ld_w1, 32)
            a.activation(w1T[:, 0], w1f, ACT.Copy, scale=S_W1).then_inc(w_hi, 1)
            a.activation(w2T[:, 0], w2f, ACT.Copy, scale=S_W2).then_inc(w_hi, 1)

            a.wait_ge(w_lo, 2)

            def a_nmax(t, p, used):
                a.wait_ge(a_mt, t + 1)
                if used:
                    held(a, a_s, 4 * t - 4)
                a.activation(qB[64:80, p].rearrange("p b g n -> p b (g n)"),
                             bank[3][0:16, 0:2 * P].unsqueeze(1).broadcast_to([16, 2, 2 * P]),
                             ACT.Copy, scale=-1.0 / (S_Q * S_K)).then_inc(a_nm, 1)

            def a_exps(t, p, used):
                if used:
                    held(a, a_pv, t - 1)
                for j in range(4):
                    a.wait_ge(a_s, 4 * t + j + 1)
                    a.activation(PT1[:, p, j], bank[4 + j % 2][:, :], ACT.Exp, scale=8.0 ** -0.5 / (S_Q * S_K)).then_inc(a_exp, 1)

            def a_qevac(t, p, used):
                a.wait_ge(a_qt, t + 1)
                if used:
                    held(a, a_s, 4 * t - 4)
                src = bank[0][0:64, :].rearrange("p (g b n) -> p g b n", g=4, b=2)
                a.activation(qA[0:64, p].rearrange("p b g n -> p g b n"), src, ACT.Copy).then_inc(a_qe, 1)
                a.wait_ge(a_qe, 2 * t + 1)
                a.activation(qB[0:64, p], qA[0:64, p], ACT.Copy).then_inc(a_qe, 1)

            tiles_loop(a, D1, [(3, a_nmax), (3, a_exps), (1, a_qevac)])

            if last_phase >= 2:
                a.wait_ge(a_x, TILES)

                def f_xevac(t, p, used):
                    a.wait_ge(f_tr, t + 1)
                    if used:
                        held(a, f_vp, 2 * t - 2)
                    a.activation(xqT[:, p], bank[0][:, 0:P].bitcast(F16).rearrange("p (c n) -> p c n", c=2),
                                 ACT.Copy, bias=-ROUND0).then_inc(f_xe, 1)

                def f_silu(t, p, used):
                    a.wait_ge(f_g, 2 * t + 2)
                    if used:
                        held(a, f_h, t - 1)
                    a.activation(sil[:, p], gate[:, p], ACT.Silu).then_inc(f_sil, 1)

                def f_hevac(t, p, used):
                    a.wait_ge(f_ht, t + 1)
                    if used:
                        held(a, f_o, t - 1)
                    a.activation(hqT[:, p], bank[5][:, :].bitcast(F16).rearrange("p (c n) -> p c n", c=8),
                                 ACT.Copy, bias=-ROUND0).then_inc(f_he, 1)

                tiles_loop(a, D2, [(3, f_hevac), (2, f_silu), (1, f_xevac)])

            if last_phase >= 3:
                a.wait_ge(f_x, TILES)

                def l_tevac(t, p, used):
                    a.wait_ge(l_tr, t + 1)
                    if used:
                        held(a, l_qa, 2 * t - 2)
                    a.activation(xT3[:, p, 0], bank[0][:, 0:2 * P].rearrange("p (c n) -> p c n", c=2), ACT.Copy).then_inc(l_te, 1)

                def l_qevac(j):
                    def f(t, p, used):
                        if used and j == 0:
                            held(a, l_s, 2 * t - 2)
                        a.wait_ge(l_qa, 2 * t + j + 1)
                        a.activation(qa[:, p, 0, 4 * j:4 * j + 4], bank[1][:, :].rearrange("p (c n) -> p c n", c=4),
                                     ACT.Copy, scale=S_L / (S_X * S_A)).then_inc(l_qe, 1)
                    return f

                def l_nmax(t, p, used):
                    a.wait_ge(l_mt, t + 1)
                    if used:
                        held(a, l_s, 2 * t - 2)
                    a.activation(nm3[:, p], bank[3][0:16, 0:P], ACT.Copy, scale=-1.0, bias=S_P * S_L * S_K).then_inc(l_nm, 1)

                def l_exps(b):
                    def f(t, p, used):
                        a.wait_ge(l_s, 2 * t + b + 1)
                        if used:
                            held(a, l_pl, 2 * t + b - 1)
                        elif t:
                            a.wait_ge(l_pl, 2 * t + b - 1)
                        a.activation(PTf[:, b], bank[4][:, :], ACT.Exp, scale=1.0 / (S_L * S_K)).then_inc(l_exp, 1)
                        if used and b == 0:
                            held(a, l_pv, 2 * t - 2)
                        a.wait_ge(l_exp, 2 * t + b + 1)
                        a.activation(PT3[:, p, 0, b], PTf[:, b], ACT.Copy).then_inc(l_ph, 1)
                    return f

                def l_revac(b):
                    def f(t, p, used):
                        a.wait_ge(l_rb, 2 * t + b + 1)
                        if used:
                            held(a, l_c, 2 * t + b - 1)
                        elif t:
                            a.wait_ge(l_c, 2 * t + b - 1)
                        a.activation(rb3[:, b], bank[6][:, :], ACT.Copy).then_inc(l_re, 1)
                    return f

                def l_chigh(b):
                    def f(t, p, used):
                        if used and b == 0:
                            held(a, l_o, t - 1)
                        a.wait_ge(l_c, 2 * t + b + 1)
                        a.activation(cT[:, p, 0, :, 64 * b:64 * b + 64], cf[:, p, b].rearrange("p (k n) -> p k n", k=8),
                                     ACT.Copy).then_inc(l_ch, 1)
                    return f

                tiles_loop(a, D3, [(2, l_qevac(0)), (3, l_nmax), (3, l_exps(0)), (4, l_revac(0)), (4, l_revac(1)),
                                   (1, l_tevac), (4, l_chigh(0)), (2, l_qevac(1)), (3, l_exps(1)), (4, l_chigh(1))])

            if last_phase >= 4:
                a.wait_ge(l_x, TILES)

                def e_tevac(t, p, used):
                    a.wait_ge(e_tr, t + 1)
                    if used:
                        held(a, e_h, 3 * t - 3)
                    a.activation(xT4[:, p, 0], bank[0][:, 0:2 * P].rearrange("p (c n) -> p c n", c=2), ACT.Copy).then_inc(e_te, 1)

                def e_tanh(t, p, used):
                    a.wait_ge(e_rk, t + 1)
                    if used:
                        held(a, e_cc, 6 * t - 11)
                    a.activation(th4[:, p], dif4[:, p], ACT.Tanh).then_inc(e_th, 1)

                def e_ctev(t, p, used):
                    a.wait_ge(e_ct, t + 1)
                    if used:
                        held(a, e_y, t - 1)
                    a.activation(cT16[:, p], bank[2][0:24, 0:P // 2].bitcast(BF16), ACT.Copy)
                    a.activation(cTf[:, p], bank[2][0:8, P:2 * P], ACT.Copy, scale=S_H * S_W2).then_inc(e_cte, 1)

                def e_silu(c):
                    def f(t, p, used):
                        j0, j1 = CHUNKS4[c]
                        if used and c == 0:
                            held(a, e_hf, 3 * t - 3)
                        a.wait_ge(e_h, 3 * t + c + 1)
                        for j in range(j0, j1):
                            last = a.activation(sh4[:, p, j * P:(j + 1) * P], bank[3 + (p + c) % 2][:, (j - j0) * P:(j - j0 + 1) * P],
                                                ACT.Silu, bias=b1c[:, j:j + 1], scale=1.0 / (S_X * S_W1))
                        last.then_inc(e_sl, 1)
                    return f

                tiles_loop(a, D4, [(2, e_tevac), (3, e_silu(0)), (3, e_ctev), (3, e_silu(1)), (3, e_silu(2)), (2, e_tanh)])

        @block.tensor
        def _(pe):
            pe.wait_ge(ld_const, N_CONST)
            pe.wait_ge(consts_done, 1)
            pe.wait_ge(q_abs, 3)
            pe.matmul(bank[2][:, 0:3], ones_sum, wabs.rearrange("p a b -> p (a b)"), start=True, stop=True).then_inc(q_sum, 1)
            for j in range(6):
                if j >= 2:
                    pe.wait_ge(q_ev, j - 1)
                dst = bank[j % 2][:, :].bitcast(BF16)
                if j < 4:
                    k, m = j // 2, j % 2
                    pe.wait_ge(q_bf, k + 1)
                    for c in range(8):
                        last = pe.transpose(dst[:, c * P:(c + 1) * P], wqb[:, c * D + m * P:c * D + (m + 1) * P], idb[:, :])
                else:
                    m = j - 4
                    pe.wait_ge(q_bf, 3)
                    for c in range(4):
                        for o in range(2):
                            last = pe.transpose(dst[:, c * D + o * P:c * D + (o + 1) * P],
                                                wqb[:, o * HID + (4 * m + c) * P:o * HID + (4 * m + c + 1) * P], idb[:, :])
                last.then_inc(q_tr, 1)

            def pair_products(i, p, used):
                pe.wait_ge(m_ld[p], 56 * i + (112 - 56 * p))
                for h in range(2):
                    if used:
                        held(pe, m_ye, 2 * i + h)
                    elif i + h:
                        pe.wait_ge(m_ye, 2 * i + h)
                    for c in range(2):
                        last = pe.matmul(bank[0][0:96, c * D:(c + 1) * D], cq_in[:, p, h, c * 96:(c + 1) * 96],
                                         wq_in[:, p, h, :], start=True, stop=True)
                    last.then_inc(m_y, 1)
                    held(pe, m_ye, 2 * i + h + 1)
                    for c in range(2):
                        last = pe.matmul(bank[1][0:RR, 0:D], dq_in[:, p, h, c, :], ysb[:, h, c, :], start=(c == 0), stop=(c == 1))
                    last.then_inc(m_z, 1)
                held(pe, m_ze, 2 * i + 2)
                if used:
                    held(pe, m_ae, i)
                elif i:
                    pe.wait_ge(m_ae, i)
                for h in range(2):
                    for m in range(2):
                        last = pe.matmul(bank[2][:, m * P + h * 64:m * P + h * 64 + 64], zsb[:, h, m * P:(m + 1) * P],
                                         et_in[:, p, h, :], start=True, stop=True)
                last.then_inc(m_a, 1)
                if used:
                    held(pe, m_be, i)
                elif i:
                    pe.wait_ge(m_be, i)
                for h in range(2):
                    last = pe.matmul(bank[3][64 * h:64 * h + 64, 0:D], ckv_in[:, p, h, :], wo_in[:, p, h, :], start=True, stop=True)
                last.then_inc(m_b, 1)
            pair_products(0, 0, False)
            pair_products(1, 1, False)
            with pe.Fori(2, PAIRS1 - 1, 2) as i:
                pair_products(i, 0, True)
                pair_products(i + 1, 1, True)

            pe.wait_ge(m_ae, PAIRS1)
            pe.wait_ge(m_be, PAIRS1)

            def a_trans(t, p, used):
                held(pe, ln1.xn, ln1.base + t + 1)
                if used:
                    held(pe, a_qe, 2 * t)
                    held(pe, a_ql, t)
                elif t:
                    pe.wait_ge(a_qe, 2 * t)
                    pe.wait_ge(a_ql, t)
                q = ln1.out[:, p, :].rearrange("n (g c) -> n g c", g=4)
                for g in range(4):
                    last = pe.transpose(bank[0][0:64, g * P:(g + 1) * P], q[:, g], idf[:, :])
                last.then_inc(a_qt, 1)

            def a_pass1(t, p, used):
                held(pe, a_qe, 2 * t + 1)
                held(pe, a_kx, t + 1)
                for j in range(4):
                    b, gp = j // 2, j % 2
                    if used:
                        held(pe, a_mx, 4 * t + j - 1)
                    elif 4 * t + j >= 2:
                        pe.wait_ge(a_mx, 4 * t + j - 1)
                    pe.matmul(bank[1 + j % 2][:, :], qA[0:64, p, b, 2 * gp:2 * gp + 2, :].rearrange("p g n -> p (g n)"),
                              kA[0:64, p, b].rearrange("p k n -> p (k n)"), start=True, stop=True).then_inc(a_p1, 1)

            def a_maxT(t, p, used):
                held(pe, a_mx, 4 * t + 4)
                if used:
                    held(pe, a_nm, t)
                elif t:
                    pe.wait_ge(a_nm, t)
                for gp in range(2):
                    last = pe.transpose(bank[3][0:16, gp * P:(gp + 1) * P], mx1[:, p, gp, :], idf[:, :])
                last.then_inc(a_mt, 1)

            def a_scores(t, p, used):
                held(pe, a_nm, t + 1)
                held(pe, a_ql, t + 1)
                held(pe, a_qe, 2 * t + 2)
                held(pe, a_kb, t + 1)
                for j in range(4):
                    b = j // 2
                    if used:
                        held(pe, a_exp, 4 * t + j - 1)
                    elif 4 * t + j >= 2:
                        pe.wait_ge(a_exp, 4 * t + j - 1)
                    for c in range(2):
                        pair = 2 * (j % 2) + c
                        dst = bank[4 + j % 2][:, c * D:(c + 1) * D]
                        pe.matmul(dst, kA[:, p, b, 2 * pair:2 * pair + 2, :].rearrange("p k n -> p (k n)"),
                                  qA[:, p, b].rearrange("p g n -> p (g n)"), start=True, stop=False)
                        last = pe.matmul(dst, kB[0:80, p, b, 2 * pair:2 * pair + 2, :].rearrange("p k n -> p (k n)"),
                                         qB[0:80, p, b].rearrange("p g n -> p (g n)"), start=False, stop=True)
                    last.then_inc(a_s, 1)

            def a_sums(t, p, used):
                held(pe, a_exp, 4 * t + 4)
                held(pe, a_vx, t + 1)
                if used:
                    held(pe, a_att, t)
                elif t:
                    pe.wait_ge(a_att, t)
                for b in range(2):
                    dst = bank[6][64 * b:64 * b + 64, 0:288].rearrange("p (n k g i) -> p n g k i", n=4, k=2, g=4)
                    for pair in range(4):
                        for g in range(4):
                            col = (pair % 2) * D + g * 64
                            last = pe.matmul(dst[:, pair, g], PT1[:, p, 2 * b + pair // 2, col:col + 64],
                                             vx[:, p, 4 * b + pair, :].rearrange("p (k i) -> p k i", k=2), start=True, stop=True)
                last.then_inc(a_pv, 1)

            tiles_loop(pe, D1, [(3, a_maxT), (4, a_sums), (3, a_scores), (2, a_pass1), (1, a_trans)])

            if last_phase >= 2:
                pe.wait_ge(a_x, TILES)

                def f_trans(t, p, used):
                    held(pe, f_xm, t + 1)
                    if used:
                        held(pe, f_xe, t)
                    elif t:
                        pe.wait_ge(f_xe, t)
                    q = xm[:, p, :].bitcast(F16).rearrange("p (n two) -> p n two", two=2)[:, :, 0]
                    dst = bank[0][:, 0:P].bitcast(F16)
                    for c in range(2):
                        last = pe.transpose(dst[:, c * P:(c + 1) * P], q[:, c * P:(c + 1) * P], id16[:, :])
                    last.then_inc(f_tr, 1)

                def f_prod(t, p, used):
                    held(pe, f_xe, t + 1)
                    for j in range(4):
                        done, made = (f_g, f_gp) if j < 2 else (f_v, f_vp)
                        if used:
                            held(pe, done, 2 * t)
                        elif t:
                            pe.wait_ge(done, 2 * t)
                        for c in range(2):
                            last = pe.matmul(bank[1 + j][:, :], xqT[:, p, c, :], wgv[:, c, j * 512:(j + 1) * 512],
                                             start=(c == 0), stop=(c == 1))
                        last.then_inc(made, 1)

                def f_htrans(t, p, used):
                    held(pe, f_hm, t + 1)
                    if used:
                        held(pe, f_he, t)
                    elif t:
                        pe.wait_ge(f_he, t)
                    q = hm[:, p, :].bitcast(F16).rearrange("p (n two) -> p n two", two=2)[:, :, 0]
                    dst = bank[5][:, :].bitcast(F16)
                    for c in range(8):
                        last = pe.transpose(dst[:, c * P:(c + 1) * P], q[:, c * P:(c + 1) * P], id16[:, :])
                    last.then_inc(f_ht, 1)

                def f_outp(t, p, used):
                    held(pe, f_he, t + 1)
                    if used:
                        held(pe, f_y, t)
                    elif t:
                        pe.wait_ge(f_y, t)
                    for c in range(8):
                        last = pe.matmul(bank[6][:, 0:D], hqT[:, p, c, :], wow[:, c, :], start=(c == 0), stop=(c == 7))
                    last.then_inc(f_o, 1)

                tiles_loop(pe, D2, [(4, f_outp), (3, f_htrans), (2, f_prod), (1, f_trans)])

            if last_phase >= 3:
                pe.wait_ge(f_x, TILES)

                def l_trans(t, p, used):
                    held(pe, ln3.xn, ln3.base + t + 1)
                    if used:
                        held(pe, l_te, t)
                        held(pe, l_tl, t)
                    elif t:
                        pe.wait_ge(l_te, t)
                        pe.wait_ge(l_tl, t)
                    for c in range(2):
                        last = pe.transpose(bank[0][:, c * P:(c + 1) * P], ln3.out[:, p, c * P:(c + 1) * P], idf[:, :])
                    last.then_inc(l_tr, 1)

                def l_query(j):
                    def f(t, p, used):
                        if j == 0:
                            held(pe, l_te, t + 1)
                            held(pe, l_tl, t + 1)
                        for done in (l_qe, l_ql):
                            if used:
                                held(pe, done, 2 * t + j)
                            elif 2 * t + j:
                                pe.wait_ge(done, 2 * t + j)
                        for k in range(4):
                            pair = 4 * j + k
                            for n, (wp, xp, c) in enumerate((wp, xp, c) for wp, xp in ((0, 0), (0, 1), (1, 0)) for c in range(2)):
                                last = pe.matmul(bank[1][:, k * P:(k + 1) * P], wA[:, wp, c, pair * P:(pair + 1) * P],
                                                 xT3[:, p, xp, c, :], start=(n == 0), stop=(n == 5))
                        last.then_inc(l_qa, 1)
                    return f

                def l_pass1(j):
                    def f(t, p, used):
                        held(pe, l_qe, 2 * t + j + 1)
                        if j == 0:
                            held(pe, l_kb, 2 * t + 1)
                        if used:
                            held(pe, l_mx, 2 * t + j)
                        elif 2 * t + j:
                            pe.wait_ge(l_mx, 2 * t + j)
                        for b in range(2):
                            for k in range(4):
                                last = pe.matmul(bank[2][64 * b:64 * b + 64, k * P:(k + 1) * P],
                                                 qa[:, p, 0, 4 * j + k, 64 * b:64 * b + 64], kbd[:, p, 0, b], start=True, stop=True)
                        last.then_inc(l_p1, 1)
                    return f

                def l_maxT(t, p, used):
                    held(pe, l_mx, 2 * t + 2)
                    if used:
                        held(pe, l_nm, t)
                        held(pe, l_rc, t - 1)
                    elif t:
                        pe.wait_ge(l_nm, t)
                    pe.transpose(bank[3][0:16, 0:P], mx3[:, p], idf[:, :]).then_inc(l_mt, 1)

                def l_scores(b):
                    def f(t, p, used):
                        if b == 0:
                            held(pe, l_nm, t + 1)
                            held(pe, l_kb, 2 * t + 2)
                            held(pe, l_ql, 2 * t + 2)
                        if used:
                            held(pe, l_exp, 2 * t + b)
                        elif 2 * t + b:
                            pe.wait_ge(l_exp, 2 * t + b)
                        dst = bank[4][:, :].rearrange("p (k n) -> p k n", k=8)
                        for n, (kp, qp) in enumerate(((0, 0), (0, 1), (1, 0))):
                            pe.matmul(dst, kbd[:, p, kp, b], qa[:, p, qp, :, 64 * b:64 * b + 64], start=(n == 0), stop=False)
                        for k in range(PAIRS1):
                            last = pe.matmul(bank[4][:, 64 * k:64 * k + 64], sel1[:, k, :], nm3[:, p, 64 * b:64 * b + 64],
                                             start=False, stop=(k == PAIRS1 - 1))
                        last.then_inc(l_s, 1)
                    return f

                def l_sums(t, p, used):
                    held(pe, l_ph, 2 * t + 2)
                    held(pe, l_pl, 2 * t + 2)
                    if used and not isinstance(t, int):
                        held(pe, l_nm, t + 2)
                    else:
                        pe.wait_ge(l_nm, min(t + 2, TILES))
                    for b in range(2):
                        for n, (k, pp) in enumerate((k, pp) for k in range(PAIRS1) for pp in range(2)):
                            last = pe.matmul(bank[3][0:16, P + 64 * b:P + 64 * b + 64], cnt[:, k, :], PT3[:, p, pp, b, 64 * k:64 * k + 64],
                                             start=(n == 0), stop=(n == 2 * PAIRS1 - 1))
                    last.then_inc(l_sum, 1)

                def l_recips(b):
                    def f(t, p, used):
                        if b == 0:
                            held(pe, l_rh, t + 1)
                            held(pe, l_rl, t + 1)
                        if used:
                            held(pe, l_re, 2 * t + b)
                        elif 2 * t + b:
                            pe.wait_ge(l_re, 2 * t + b)
                        for k in range(PAIRS1):
                            last = pe.matmul(bank[6][:, 64 * k:64 * k + 64], selr[:, k, :], rr3[:, p, 64 * b:64 * b + 64],
                                             start=True, stop=True)
                        last.then_inc(l_rb, 1)
                    return f

                def l_weighted(b):
                    def f(t, p, used):
                        if b == 0:
                            held(pe, l_vb, 2 * t + 2)
                        if used:
                            held(pe, l_c, 2 * t + b)
                        elif 2 * t + b:
                            pe.wait_ge(l_c, 2 * t + b)
                        for n, (vp, pp) in enumerate(((0, 0), (0, 1), (1, 0))):
                            last = pe.matmul(bank[5][:, :], vbd[:, p, vp, b], PT3[:, p, pp, b], start=(n == 0), stop=(n == 2))
                        last.then_inc(l_pv, 1)
                    return f

                def l_outp(part):
                    def f(t, p, used):
                        if part == 0:
                            held(pe, l_ch, 2 * t + 2)
                            held(pe, l_cl, 2 * t + 2)
                            if used:
                                held(pe, l_x, t)
                            elif t:
                                pe.wait_ge(l_x, t)
                        for k in range(4 * part, 4 * part + 4):
                            for n, (cp, wp) in enumerate(((0, 0), (0, 1), (1, 0))):
                                last = pe.matmul(bank[7][:, 0:D], cT[:, p, cp, k, :], wB[:, wp, k, :],
                                                 start=(k == 0 and n == 0), stop=(k == PAIRS1 - 1 and n == 2))
                        if part == 1:
                            last.then_inc(l_o, 1)
                    return f

                tiles_loop(pe, D3, [(2, l_query(0)), (3, l_maxT), (4, l_sums), (5, l_outp(0)), (3, l_scores(0)), (2, l_pass1(0)),
                                    (5, l_outp(1)), (4, l_recips(0)), (4, l_weighted(0)), (4, l_recips(1)),
                                    (1, l_trans), (2, l_query(1)), (4, l_weighted(1)),
                                    (3, l_scores(1)), (2, l_pass1(1))])

            if last_phase >= 4:
                pe.wait_ge(l_x, TILES)

                def e_trans(t, p, used):
                    held(pe, ln4.xn, ln4.base + t + 1)
                    for done in (e_te, e_tl):
                        if used:
                            held(pe, done, t)
                        elif t:
                            pe.wait_ge(done, t)
                    for c in range(2):
                        last = pe.transpose(bank[0][:, c * P:(c + 1) * P], ln4.out[:, p, c * P:(c + 1) * P], idf[:, :])
                    last.then_inc(e_tr, 1)

                def e_score(t, p, used):
                    held(pe, e_te, t + 1)
                    held(pe, e_tl, t + 1)
                    if used:
                        held(pe, e_s1, t)
                    elif t:
                        pe.wait_ge(e_s1, t)
                    for n, (xp, wp, c) in enumerate((xp, wp, c) for xp, wp in ((0, 0), (0, 1), (1, 0)) for c in range(2)):
                        last = pe.matmul(bank[1][:, 0:8], xT4[:, p, xp, c, :], gw16[:, wp, c, :], start=(n == 0), stop=(n == 5))
                    last.then_inc(e_sc, 1)

                def e_combT(t, p, used):
                    held(pe, e_cc, 6 * t + 6)
                    if used:
                        held(pe, e_cte, t)
                    elif t:
                        pe.wait_ge(e_cte, t)
                    pe.transpose(bank[2][0:24, 0:P // 2].bitcast(BF16), cpart[:, p], idb[:, :])
                    pe.transpose(bank[2][0:8, P:2 * P], comb[:, p], idf[:, :]).then_inc(e_ct, 1)

                def e_hid(c):
                    def f(t, p, used):
                        j0, j1 = CHUNKS4[c]
                        if used:
                            held(pe, e_sl, 3 * t + c - 1)
                        elif 3 * t + c >= 2:
                            pe.wait_ge(e_sl, 3 * t + c - 1)
                        for j in range(j0, j1):
                            for n, (wp, xp, k) in enumerate((wp, xp, k) for wp, xp in ((0, 0), (0, 1), (1, 0)) for k in range(2)):
                                last = pe.matmul(bank[3 + (p + c) % 2][:, (j - j0) * P:(j - j0 + 1) * P], w1T[:, wp, k, j * P:(j + 1) * P],
                                                 xT4[:, p, xp, k, :], start=(n == 0), stop=(n == 5))
                        last.then_inc(e_h, 1)
                    return f

                def e_spread(c):
                    def f(t, p, used):
                        j0, j1 = CHUNKS4[c]
                        if c == 0:
                            held(pe, e_cte, t + 1)
                        if used:
                            held(pe, e_hf, 3 * t + c - 1)
                        elif 3 * t + c >= 2:
                            pe.wait_ge(e_hf, 3 * t + c - 1)
                        for j in range(j0, j1):
                            last = pe.matmul(bank[5 + (p + c) % 2][:, (j - j0) * P:(j - j0 + 1) * P], sel3[:, j, :], cT16[:, p],
                                             start=True, stop=True)
                        last.then_inc(e_cb2, 1)
                    return f

                def e_outp(t, p, used):
                    held(pe, e_hs, t + 1)
                    if used:
                        held(pe, e_x, t)
                    elif t:
                        pe.wait_ge(e_x, t)
                    for n, (j, hp, wp) in enumerate((j, hp, wp) for j in range(EB) for hp, wp in ((0, 0), (0, 1), (1, 0))):
                        pe.matmul(bank[7][:, 0:D], hs[:, p, hp, j * P:(j + 1) * P], w2T[:, wp, j, :], start=(n == 0), stop=False)
                    pe.matmul(bank[7][:, 0:D], cTf[:, p], b2s[:, :], start=False, stop=True).then_inc(e_y, 1)

                tiles_loop(pe, D4, [(2, e_trans), (3, e_hid(0)), (3, e_hid(1)), (3, e_combT), (3, e_spread(0)), (3, e_spread(1)), (2, e_score),
                                    (3, e_hid(2)), (3, e_spread(2)), (4, e_outp)])

        @block.vector
        def _(v):
            v.memset(half[:, :], -0.5)
            v.memset(klT[64:128, :, :], S_Q * S_K)
            v.memset(ones_sum, 1.0)
            v.wait_ge(ld_const, N_CONST)
            v.tensor_tensor(gb8[:, 0, :], gb8[:, 0, :], gb8[:, 1, :], ALU.add)
            v.tensor_copy(id16[:, :], idf[:, :])
            v.tensor_copy(idb[:, :], idf[:, :])
            v.tensor_scalar(gw16[:, 0], gwT[:, :, :], S_W1, None, ALU.mult).then_inc(g_done, 1)
            v.wait_ge(g_done, 1)
            v.scalar_tensor_tensor(gw16[:, 1], gwT[:, :, :], S_W1, gw16[:, 0], ALU.mult, ALU.subtract).then_inc(g_done, 1)
            v.tensor_copy(selr[:, :, :], selrf)
            v.tensor_copy(cnt[:, :, :], cntf)
            v.tensor_copy(sel1[:, :, :], sel1f)
            v.tensor_copy(sel3[:, :, :], sel3f).then_inc(consts_done, 1)
            v.wait_ge(k_hi, 1)
            v.scalar_tensor_tensor(klT[0:64, :, :], kTf[0:64], S_K, khT[0:64, :, :], ALU.mult, ALU.subtract).then_inc(k_lo, 1)
            v.wait_ge(ld_w0, 48)
            for k in range(3):
                v.tensor_reduce(wabs[:, k], wraw[:, k], AX.X, ALU.add, apply_absolute_value=True).then_inc(q_abs, 1)
            v.wait_ge(q_sum, 1)
            v.tensor_scalar(gam[:, 0:3], bank[2][:, 0:3], 1.0 / (HID * D), 1e-5, ALU.mult, ALU.max).then_inc(q_gam, 1)
            v.wait_ge(q_gam, 1)
            v.reciprocal(rgam[:, 0:3], gam[:, 0:3]).then_inc(q_rg, 1)
            v.wait_ge(q_rg, 1)
            for k in range(3):
                v.tensor_scalar(wraw[:, k], wraw[:, k], rgam[:, k:k + 1], BIG, ALU.mult, ALU.add).then_inc(q_r1, 1)
                v.wait_ge(q_r1, k + 1)
                v.tensor_scalar(wraw[:, k], wraw[:, k], BIG, 1.0, ALU.subtract, ALU.min).then_inc(q_r2, 1)
                v.wait_ge(q_r2, k + 1)
                if k:
                    v.wait_ge(q_tr, 2 * k)
                v.tensor_scalar(wqb, wraw[:, k], -1.0, None, ALU.max).then_inc(q_bf, 1)

            def pair_evac(i, p, used):
                v.wait_ge(m_ah, i + 1)
                v.scalar_tensor_tensor(wA[:, 1, :, bass.ts(i, P)], bank[2][:, 0:2 * P].rearrange("p (c n) -> p c n", c=2),
                                       S_A, wA[:, 0, :, bass.ts(i, P)], ALU.mult, ALU.subtract).then_inc(m_ae, 1)
                v.wait_ge(m_bh, i + 1)
                v.scalar_tensor_tensor(wB[:, 1, i, :], bank[3][:, 0:D], S_B, wB[:, 0, i, :], ALU.mult, ALU.subtract).then_inc(m_be, 1)
            with v.Fori(0, PAIRS1, 1) as i:
                pair_evac(i, 0, True)
            v.wait_ge(w_hi, 2)
            v.scalar_tensor_tensor(w1T[:, 1], w1f, S_W1, w1T[:, 0], ALU.mult, ALU.subtract).then_inc(w_lo, 1)
            v.scalar_tensor_tensor(w2T[:, 1], w2f, S_W2, w2T[:, 0], ALU.mult, ALU.subtract).then_inc(w_lo, 1)

            v.wait_ge(ld_x, N_X)
            v.wait_ge(tanh_done, 1)
            v.tensor_scalar(g3s[:, 0:1], gT[:, 1:2], 1.0 / (S_C * S_B), None, ALU.mult).then_inc(g_done, 1)
            v.tensor_scalar(g3s[:, 1:2], gT[:, 3:4], 1.0 / (S_H * S_W2), None, ALU.mult).then_inc(g_done, 1)
            v.wait_ge(m_ae, PAIRS1)
            v.wait_ge(m_be, PAIRS1)
            v.wait_ge(w_lo, 2)

            def norm_of(ln, guard):
                def f(t, p, used):
                    if used:
                        guard(t)
                    normalise(v, ln, t, p)
                return f

            def a_max(t, p, used):
                if used:
                    held(v, a_mt, t - 1)
                for j in range(4):
                    b, gp = j // 2, j % 2
                    v.wait_ge(a_p1, 4 * t + j + 1)
                    v.tensor_reduce(mx1[:, p, gp, 8 * b:8 * b + 8], bank[1 + j % 2][:, :].rearrange("p (k n) -> p k n", k=8),
                                    AX.X, ALU.max).then_inc(a_mx, 1)

            def a_qlow(t, p, used):
                v.wait_ge(a_qe, 2 * t + 1)
                if used:
                    held(v, a_s, 4 * t - 4)
                v.tensor_tensor(qA[64:128, p].rearrange("p b g n -> p g b n"),
                                bank[0][0:64, :].rearrange("p (g b n) -> p g b n", g=4, b=2),
                                qA[0:64, p].rearrange("p b g n -> p g b n"), ALU.subtract).then_inc(a_ql, 1)

            def a_final(t, p, used):
                o = bank[6][:, 0:288].rearrange("p (h i) -> p h i", h=32)
                v.wait_ge(a_pv, t + 1)
                v.reciprocal(rec1[:, p], o[:, :, 8:9]).then_inc(a_rec, 1)
                v.wait_ge(a_rec, t + 1)
                v.tensor_tensor(att1[:, p], o[:, :, 0:8], rec1[:, p].broadcast_to([P, 32, 8]), ALU.mult).then_inc(a_att, 1)
                v.wait_ge(a_att, t + 1)
                v.scalar_tensor_tensor(xs[:, t, :], att1[:, p].rearrange("p h i -> p (h i)"), gT[:, 0:1], xs[:, t, :],
                                       ALU.mult, ALU.add).then_inc(a_x, 1)

            tiles_loop(v, D1, [(4, a_final), (0, lambda t, p, u: stats(v, ln1, t, p)),
                               (1, norm_of(ln1, lambda t: held(v, a_qt, t - 1))), (2, a_max), (1, a_qlow)])

            if last_phase >= 2:
                v.wait_ge(a_x, TILES)
                v.wait_ge(q_ev, 6)

                def f_quant(t, p, used):
                    v.wait_ge(ln2.xn, ln2.base + t + 1)
                    v.tensor_reduce(gx[:, p, 0:1], ln2.out[:, p, :], AX.X, ALU.max, apply_absolute_value=True).then_inc(f_ab, 1)
                    v.wait_ge(f_ab, t + 1)
                    v.tensor_scalar(gx[:, p, 1:2], gx[:, p, 0:1], 1e-5, 1.0 / 127.0, ALU.max, ALU.mult).then_inc(f_c1, 1)
                    v.wait_ge(f_c1, t + 1)
                    v.reciprocal(gx[:, p, 2:3], gx[:, p, 1:2]).then_inc(f_c2, 1)
                    v.tensor_scalar(sg[:, p, :], gam[:, 0:2], gx[:, p, 1:2], None, ALU.mult).then_inc(f_sc, 1)
                    v.wait_ge(f_c2, t + 1)
                    if used:
                        held(v, f_tr, t - 1)
                    v.tensor_scalar(xm[:, p, :], ln2.out[:, p, :], gx[:, p, 2:3], MAGIC, ALU.mult, ALU.add).then_inc(f_xm, 1)

                def f_gv(t, p, used):
                    if used:
                        held(v, f_sil, t - 1)
                    v.wait_ge(f_sc, t + 1)
                    for k, (made, done, dst) in enumerate(((f_gp, f_g, gate), (f_vp, f_v, val))):
                        for j in range(2):
                            v.wait_ge(made, 2 * t + j + 1)
                            v.scalar_tensor_tensor(dst[:, p, j * 512:(j + 1) * 512], bank[1 + 2 * k + j][:, :], sg[:, p, k:k + 1],
                                                   bgv[:, k, j * 512:(j + 1) * 512], ALU.mult, ALU.add).then_inc(done, 1)

                def f_hidden(t, p, used):
                    v.wait_ge(f_sil, t + 1)
                    v.wait_ge(f_v, 2 * t + 2)
                    v.tensor_tensor(val[:, p], sil[:, p], val[:, p], ALU.mult).then_inc(f_h, 1)
                    v.wait_ge(f_h, t + 1)
                    v.tensor_reduce(gh[:, p, 0:1], val[:, p], AX.X, ALU.max, apply_absolute_value=True).then_inc(f_ha, 1)
                    v.wait_ge(f_ha, t + 1)
                    v.tensor_scalar(gh[:, p, 1:2], gh[:, p, 0:1], 1e-5, 1.0 / 127.0, ALU.max, ALU.mult).then_inc(f_h1, 1)
                    v.wait_ge(f_h1, t + 1)
                    v.reciprocal(gh[:, p, 2:3], gh[:, p, 1:2]).then_inc(f_h2, 1)
                    v.tensor_scalar(gh[:, p, 3:4], gh[:, p, 1:2], gam[:, 2:3], None, ALU.mult).then_inc(f_c3, 1)
                    v.wait_ge(f_h2, t + 1)
                    if used:
                        held(v, f_ht, t - 1)
                    v.tensor_scalar(hm[:, p], val[:, p], gh[:, p, 2:3], MAGIC, ALU.mult, ALU.add).then_inc(f_hm, 1)

                def f_final(t, p, used):
                    v.wait_ge(f_o, t + 1)
                    v.scalar_tensor_tensor(yb[:, p], bank[6][:, 0:D], gh[:, p, 3:4], bo[:, :], ALU.mult, ALU.add).then_inc(f_y, 1)
                    v.wait_ge(f_y, t + 1)
                    v.scalar_tensor_tensor(xs[:, t, :], yb[:, p], gT[:, 2:3], xs[:, t, :], ALU.mult, ALU.add).then_inc(f_x, 1)

                tiles_loop(v, D2, [(4, f_final), (2, f_gv), (0, lambda t, p, u: stats(v, ln2, t, p)),
                                   (1, norm_of(ln2, lambda t: None)), (1, f_quant), (2, f_hidden)])

            if last_phase >= 3:
                v.wait_ge(f_x, TILES)
                v.wait_ge(g_done, 4)
                for p in range(2):
                    v.memset(rr3[:, p], 0.0).then_inc(l_z, 1)
                v.wait_ge(l_z, 2)

                def l_max(j):
                    def f(t, p, used):
                        if used and j == 0:
                            held(v, l_mt, t - 1)
                        v.wait_ge(l_p1, 2 * t + j + 1)
                        v.tensor_reduce(mx3[:, p, 8 * j:8 * j + 8], bank[2][:, :].rearrange("p (k n) -> p k n", k=8),
                                        AX.X, ALU.max).then_inc(l_mx, 1)
                    return f

                def l_tlow(t, p, used):
                    v.wait_ge(l_te, t + 1)
                    v.tensor_tensor(xT3[:, p, 1], bank[0][:, 0:2 * P].rearrange("p (c n) -> p c n", c=2), xT3[:, p, 0],
                                    ALU.subtract).then_inc(l_tl, 1)

                def l_qlow(j):
                    def f(t, p, used):
                        v.wait_ge(l_qe, 2 * t + j + 1)
                        v.scalar_tensor_tensor(qa[:, p, 1, 4 * j:4 * j + 4].rearrange("p k n -> p (k n)"), bank[1][:, :],
                                               S_L / (S_X * S_A), qa[:, p, 0, 4 * j:4 * j + 4].rearrange("p k n -> p (k n)"),
                                               ALU.mult, ALU.subtract).then_inc(l_ql, 1)
                    return f

                def l_plow(b):
                    def f(t, p, used):
                        v.wait_ge(l_ph, 2 * t + b + 1)
                        v.tensor_tensor(PT3[:, p, 1, b], PTf[:, b], PT3[:, p, 0, b], ALU.subtract).then_inc(l_pl, 1)
                    return f

                def l_rsum(t, p, used):
                    v.wait_ge(l_sum, t + 1)
                    v.reciprocal(rs3[:, p], bank[3][0:16, P:2 * P]).then_inc(l_rc, 1)
                    v.wait_ge(l_rc, t + 1)
                    if used:
                        held(v, l_rb, 2 * t - 2)
                    v.tensor_scalar(rr3[0:16, p], rs3[:, p], S_R, None, ALU.mult).then_inc(l_rh, 1)
                    v.wait_ge(l_rh, t + 1)
                    v.scalar_tensor_tensor(rr3[32:48, p], rs3[:, p], S_R, rr3[0:16, p], ALU.mult, ALU.subtract).then_inc(l_rl, 1)

                def l_context(b):
                    def f(t, p, used):
                        v.wait_ge(l_re, 2 * t + b + 1)
                        v.wait_ge(l_pv, 2 * t + b + 1)
                        v.scalar_tensor_tensor(cf[:, p, b], bank[5][:, :], S_C / (S_R * S_K), rb3[:, b],
                                               ALU.mult, ALU.mult).then_inc(l_c, 1)
                    return f

                def l_clow(b):
                    def f(t, p, used):
                        v.wait_ge(l_ch, 2 * t + b + 1)
                        half_b = slice(64 * b, 64 * b + 64)
                        v.tensor_tensor(cT[:, p, 1, :, half_b], cf[:, p, b].rearrange("p (k n) -> p k n", k=8),
                                        cT[:, p, 0, :, half_b], ALU.subtract).then_inc(l_cl, 1)
                    return f

                def l_final(t, p, used):
                    v.wait_ge(l_o, t + 1)
                    v.scalar_tensor_tensor(xs[:, t, :], bank[7][:, 0:D], g3s[:, 0:1], xs[:, t, :], ALU.mult, ALU.add).then_inc(l_x, 1)

                tiles_loop(v, D3, [(2, l_qlow(0)), (4, l_rsum), (0, lambda t, p, u: stats(v, ln3, t, p)),
                                   (1, norm_of(ln3, lambda t: held(v, l_tr, t - 1))), (2, l_max(0)), (3, l_plow(0)),
                                   (5, l_final), (4, l_context(0)), (1, l_tlow), (4, l_clow(0)),
                                   (2, l_qlow(1)), (4, l_context(1)), (2, l_max(1)), (3, l_plow(1)), (4, l_clow(1))])

            if last_phase >= 4:
                v.wait_ge(l_x, TILES)

                def e_route(t, p, used):
                    v.wait_ge(e_sc, t + 1)
                    v.scalar_tensor_tensor(sc4[:, p], bank[1][:, 0:8], 1.0 / (S_X * S_W1), gb8[:, 0, :], ALU.mult, ALU.add).then_inc(e_s1, 1)
                    v.wait_ge(e_s1, t + 1)
                    sj = sc4[:, p].unsqueeze(1).broadcast_to([P, 8, 8])
                    se = sc4[:, p].unsqueeze(2).broadcast_to([P, 8, 8])
                    v.tensor_tensor(gt[:, p], sj, se, ALU.is_gt).then_inc(e_rt, 1)
                    v.tensor_tensor(eq[:, p], sj, se, ALU.is_equal).then_inc(e_rt, 1)
                    v.wait_ge(e_rt, 7 * t + 2)
                    v.tensor_tensor(eq[:, p], eq[:, p], before[:, :, :], ALU.mult).then_inc(e_rt, 1)
                    v.wait_ge(e_rt, 7 * t + 3)
                    v.tensor_tensor(gt[:, p], gt[:, p], eq[:, p], ALU.add).then_inc(e_rt, 1)
                    v.wait_ge(e_rt, 7 * t + 4)
                    v.tensor_reduce(rank[:, p], gt[:, p], AX.X, ALU.add).then_inc(e_rt, 1)
                    v.wait_ge(e_rt, 7 * t + 5)
                    v.tensor_scalar(half4[:, p], rank[:, p], 1.5, 0.5, ALU.is_lt, ALU.mult).then_inc(e_rt, 1)
                    v.wait_ge(e_rt, 7 * t + 6)
                    v.tensor_tensor(es4[:, p], half4[:, p], sc4[:, p], ALU.mult).then_inc(e_rt, 1)
                    v.wait_ge(e_rt, 7 * t + 7)
                    v.tensor_reduce(mid4[:, p], es4[:, p], AX.X, ALU.add).then_inc(e_md, 1)
                    v.wait_ge(e_md, t + 1)
                    if used:
                        held(v, e_th, t - 1)
                    v.tensor_scalar(dif4[:, p], sc4[:, p], mid4[:, p], None, ALU.subtract).then_inc(e_rk, 1)

                def e_comb(t, p, used):
                    v.wait_ge(e_th, t + 1)
                    if used:
                        held(v, e_ct, t - 1)
                    v.scalar_tensor_tensor(comb[:, p], th4[:, p], 1.0, half4[:, p], ALU.add, ALU.mult).then_inc(e_cc, 1)
                    v.wait_ge(e_cc, 6 * t + 1)
                    v.tensor_copy(cpart[:, p, 0:8], comb[:, p]).then_inc(e_cc, 1)
                    v.wait_ge(e_cc, 6 * t + 2)
                    v.tensor_tensor(cres[:, p, 0], comb[:, p], cpart[:, p, 0:8], ALU.subtract).then_inc(e_cc, 1)
                    v.wait_ge(e_cc, 6 * t + 3)
                    v.tensor_copy(cpart[:, p, 8:16], cres[:, p, 0]).then_inc(e_cc, 1)
                    v.wait_ge(e_cc, 6 * t + 4)
                    v.tensor_tensor(cres[:, p, 1], cres[:, p, 0], cpart[:, p, 8:16], ALU.subtract).then_inc(e_cc, 1)
                    v.wait_ge(e_cc, 6 * t + 5)
                    v.tensor_copy(cpart[:, p, 16:24], cres[:, p, 1]).then_inc(e_cc, 1)

                def e_tlow(t, p, used):
                    v.wait_ge(e_te, t + 1)
                    v.tensor_tensor(xT4[:, p, 1], bank[0][:, 0:2 * P].rearrange("p (c n) -> p c n", c=2), xT4[:, p, 0],
                                    ALU.subtract).then_inc(e_tl, 1)

                def e_scale(c):
                    def f(t, p, used):
                        j0, j1 = CHUNKS4[c]
                        v.wait_ge(e_sl, 3 * t + c + 1)
                        v.wait_ge(e_cb2, 3 * t + c + 1)
                        v.scalar_tensor_tensor(hf[:, p, j0 * P:j1 * P], sh4[:, p, j0 * P:j1 * P], S_H, bank[5 + (p + c) % 2][:, 0:(j1 - j0) * P],
                                               ALU.mult, ALU.mult).then_inc(e_hf, 1)
                    return f

                def e_split(t, p, used):
                    v.wait_ge(e_hf, 3 * t + 3)
                    if used:
                        held(v, e_y, t - 1)
                    v.tensor_copy(hs[:, p, 0], hf[:, p]).then_inc(e_hh, 1)
                    v.wait_ge(e_hh, t + 1)
                    v.tensor_tensor(hs[:, p, 1], hf[:, p], hs[:, p, 0], ALU.subtract).then_inc(e_hs, 1)

                def e_final(t, p, used):
                    v.wait_ge(e_y, t + 1)
                    v.scalar_tensor_tensor(xs[:, t, :], bank[7][:, 0:D], g3s[:, 1:2], xs[:, t, :], ALU.mult, ALU.add).then_inc(e_x, 1)

                tiles_loop(v, D4, [(5, e_final), (3, e_comb), (0, lambda t, p, u: stats(v, ln4, t, p)),
                                   (1, norm_of(ln4, lambda t: held(v, e_tr, t - 1))), (2, e_tlow), (3, e_scale(0)), (3, e_scale(1)),
                                   (2, e_route), (3, e_scale(2)), (3, e_split)])


def constants():
    c = {}
    c["ident"] = np.eye(P, dtype=np.float32)
    r = np.arange(P)
    c["kvmask"] = ((r[:, None] % 64) // 8 == np.arange(8)[None, :]).astype(np.float32)
    c["rowhalf"] = (r[:, None] // 64 == np.arange(2)[None, :]).astype(np.float32)
    lomask = np.zeros((P, 2, 8), np.float32)
    lomask[:64] = c["kvmask"][:64, None, :]
    for b in range(2):
        for k in range(8):
            lomask[64 + 8 * b + k, b, k] = 1
    c["lomask"] = lomask
    sel1 = np.zeros((16, PAIRS1, P), np.float32)
    for pair in range(PAIRS1):
        for k in range(2):
            sel1[2 * pair + k, pair, 64 * k:64 * k + 64] = 1
    c["sel1"] = sel1
    unit = np.arange(EB * P) // EH
    c["sel3"] = np.tile((unit[None, :] == np.arange(8)[:, None]).astype(np.float32).reshape(8, EB, P), (3, 1, 1))
    c["selr"] = np.concatenate([sel1, np.zeros_like(sel1), sel1])
    cnt = np.zeros((P, PAIRS1, 16), np.float32)
    for pair in range(PAIRS1):
        for k in range(2):
            cnt[64 * k:64 * k + 64, pair, 2 * pair + k] = 1
    c["cnt"] = cnt
    f = np.float32
    inv = (f(1.0) / np.power(f(10000.0), np.arange(0, CD, 2, dtype=f) / f(CD), dtype=f)).astype(f)
    freqs = np.arange(SEQ, dtype=f)[:, None] * inv[None, :]
    sin = np.repeat(np.sin(freqs), 2, axis=-1).astype(f)
    cos = np.repeat(np.cos(freqs), 2, axis=-1).astype(f)
    sign = np.where(np.arange(CD) < CD // 2, -1, 1).astype(f)
    def diagonal(a):
        return (S_K * np.kron(np.eye(2, dtype=f), a)).reshape(P, 2, 64).astype(f)

    c["cosN"], c["sinN"] = diagonal(cos), diagonal(sin * sign)
    c["cosT"], c["sinT"] = diagonal(cos.T), diagonal((sin * sign).T)
    c["before"] = np.broadcast_to((np.arange(8)[None, :] < np.arange(8)[:, None]).astype(np.float32), (P, 8, 8))
    return c


def kernel(x, ctx_512, g_xattn, g_ffn, L0_ffn_gate_w, L0_ffn_gate_b, L0_ffn_val_w, L0_ffn_val_b, L0_ffn_out_w,
           L0_ffn_out_b, L1_xattn_Wq, L1_xattn_w_kc_q, L1_xattn_w_kc_kv, L1_xattn_W_qr, L1_xattn_W_kr, L1_xattn_Wo,
           L1_ffn_gate_w, L1_ffn_gate_b, L1_ffn_bias, L1_ffn_w1, L1_ffn_b1, L1_ffn_w2, L1_ffn_b2):
    import concourse.bacc as bacc
    from concourse.bass_utils import run_bass_kernel_spmd

    arrays = dict(constants())
    ctx = np.asarray(ctx_512)
    ctxT = ctx.transpose(2, 0, 1)
    arrays.update(
        x=np.asarray(x).reshape(BATCH * SEQ, D),
        ctx=ctx, ctxT=ctxT, ctxTs=np.concatenate([ctxT[32:], ctxT[:32]]),
        g=np.broadcast_to(np.concatenate([np.asarray(g_xattn), np.asarray(g_ffn)])[None, :], (P, 4)),
        gw=np.asarray(L0_ffn_gate_w), vw=np.asarray(L0_ffn_val_w),
        ow=np.asarray(L0_ffn_out_w).reshape(2, P, HID).reshape(2 * P, HID),
        bg=np.asarray(L0_ffn_gate_b)[None, :], bv=np.asarray(L0_ffn_val_b)[None, :], bo=np.asarray(L0_ffn_out_b)[None, :],
        Wq=np.asarray(L1_xattn_Wq).reshape(HEADS1, KD, D), Cq=np.asarray(L1_xattn_w_kc_q),
        Dq=np.asarray(L1_xattn_W_qr), ET=np.asarray(L1_xattn_W_kr).transpose(0, 2, 1),
        Ckv=np.asarray(L1_xattn_w_kc_kv), WoT=np.asarray(L1_xattn_Wo).T.reshape(HEADS1, KD, D),
        gwT=np.asarray(L1_ffn_gate_w).T.reshape(2, P, EXPERTS).transpose(1, 0, 2),
        gb=np.asarray(L1_ffn_gate_b)[None, :], gbias=np.asarray(L1_ffn_bias)[None, :],
        w1T=np.asarray(L1_ffn_w1).reshape(EXPERTS * EH, D).T.reshape(2, P, EXPERTS * EH).transpose(1, 0, 2),
        b1=np.asarray(L1_ffn_b1).reshape(EB, P).T,
        w2T=np.asarray(L1_ffn_w2).transpose(0, 2, 1).reshape(EB, P, D).transpose(1, 0, 2),
        b2=np.asarray(L1_ffn_b2),
    )
    arrays = {f"in_{k}": np.ascontiguousarray(v) for k, v in arrays.items()}
    nc = bacc.Bacc("TRN2", target_bir_lowering=False, num_devices=1)
    d = {k[3:]: nc.dram_tensor(k, v.shape, mybir.dt.from_np(v.dtype), kind="ExternalInput").ap()
         for k, v in arrays.items()}
    out = nc.dram_tensor("out", (BATCH * SEQ, D), F32, kind="ExternalOutput").ap()
    build(nc, d, out, LAST_PHASE)
    got = run_bass_kernel_spmd(nc, [arrays], core_ids=[0])
    return got.results[0]["out"].reshape(BATCH, SEQ, D)


LAST_PHASE = 4
```

```python
from contextlib import ExitStack

import numpy as np

import concourse.bass as bass
from concourse import mybir

ALU = mybir.AluOpType
ACT = mybir.ActivationFunctionType
AX = mybir.AxisListType
F32 = mybir.dt.float32
F16 = mybir.dt.float16
BF16 = mybir.dt.bfloat16

P = 128
BATCH, SEQ, D = 64, 64, 256
TILES = BATCH * SEQ // P
CD = 64
EPS = 1e-5
HID = 1024
HEADS1 = 16
KD, CQ, RR = 128, 192, 64
PAIRS1 = HEADS1 // 2
EXPERTS, EH = 8, 176
EB = EXPERTS * EH // P
ROUND0 = 1536.0
MAGIC = float(2 ** 23 + 0x6600)
S_Q = 2.0 ** 6
S_X = 2.0 ** 8
S_K = 2.0 ** 4
S_A = 2.0 ** 8
S_L = 2.0 ** 6
S_P = 8.0
S_R = 2.0 ** 20
S_C = 2.0 ** 6
S_B = 2.0 ** 6
S_W1 = 2.0 ** 6
S_H = 2.0 ** 6
S_W2 = 2.0 ** 6
BIG = float(1.5 * 2 ** 23)


def tiles_loop(eng, depth, stages):
    def iteration(n, parity, static):
        for lag, stage in stages:
            t = n - lag
            if static and not 0 <= t < TILES:
                continue
            stage(t, (parity - lag) % 2, (not static) or t >= 2)

    first = depth + 2 + depth % 2
    for n in range(first):
        iteration(n, n % 2, True)
    with eng.Fori(first, TILES - 1, 2) as n:
        iteration(n, 0, False)
        iteration(n + 1, 1, False)
    for n in range(TILES, TILES + depth):
        iteration(n, n % 2, True)


def build(nc, d, out):
    with ExitStack() as ctx:
        def sb(name, shape, dt=F32):
            return ctx.enter_context(nc.sbuf_tensor(name, shape, dt))

        def sem(name):
            return ctx.enter_context(nc.semaphore(name))

        xs = sb("xs", [P, TILES, D])
        ctx2 = sb("ctx2", [P, BATCH, CD])
        khT = sb("khT", [P, BATCH, SEQ], F16)
        klT = sb("klT", [P, BATCH, SEQ], F16)
        gT = sb("gT", [P, 4])
        graw = sb("graw", [P, 4])
        g3s = sb("g3s", [P, 2])
        idf = sb("idf", [P, P])
        id16 = sb("id16", [P, P], F16)
        idb = sb("idb", [P, P], BF16)
        part = sb("part", [P, 2])
        half = sb("half", [P, 1])
        kvmask = sb("kvmask", [P, 8])
        rowhalf = sb("rowhalf", [P, 2])
        lomask = sb("lomask", [P, 2, 8])
        wgv = sb("wgv", [P, 2, 2 * HID], BF16)
        wow = sb("wow", [P, 8, D], BF16)
        gam = sb("gam", [P, 4])
        bgv = sb("bgv", [P, 2, HID], BF16)
        bo = sb("bo", [P, D])
        wA = sb("wA", [P, 2, 2, HEADS1 * CD], F16)
        wB = sb("wB", [P, 2, PAIRS1, D], F16)
        cosT = sb("cosT", [P, 2, SEQ])
        sinT = sb("sinT", [P, 2, SEQ])
        cosN = sb("cosN", [P, 2, CD])
        sinN = sb("sinN", [P, 2, CD])
        sel1 = sb("sel1", [16, PAIRS1, P], BF16)
        selr = sb("selr", [48, PAIRS1, P], F16)
        cnt = sb("cnt", [P, PAIRS1, 16], F16)
        w1T = sb("w1T", [P, 2, 2, EXPERTS * EH], F16)
        w2T = sb("w2T", [P, 2, EB, D], F16)
        b1c = sb("b1c", [P, EB])
        gwT = sb("gwT", [P, 2, EXPERTS])
        gw16 = sb("gw16", [P, 2, 2, EXPERTS], F16)
        gb8 = sb("gb8", [P, 2, EXPERTS])
        before = sb("before", [P, 8, 8])
        b2s = sb("b2s", [3 * EXPERTS, 3, D], BF16)
        sel3 = sb("sel3", [24, EB, P], BF16)
        ARENA = 18 * 1024
        arena = sb("arena", [P, ARENA])
        bank = [ctx.enter_context(nc.psum_tensor(f"bank{i}", [P, 512], F32)) for i in range(8)]

        class Arena:
            def __init__(self):
                self.at = 0

            def take(self, shape, dt=F32, rows=P):
                n = int(np.prod(shape))
                words = n if dt == F32 else (n + 1) // 2
                a = arena[0:rows, self.at:self.at + words]
                self.at += words + words % 2
                assert self.at <= ARENA
                if dt != F32:
                    a = a.bitcast(dt)
                names = "abcdef"[:len(shape)]
                if len(shape) > 1:
                    a = a.rearrange(f"p ({' '.join(names)}) -> p {' '.join(names)}",
                                    **dict(zip(names, shape)))
                return a

        class Norm:
            bn, agg, var, rstd, shift, xn = (sem(f"ln_{n}") for n in ("bn", "agg", "var", "rstd", "shift", "xn"))

            def __init__(self, ph, mem, scale):
                self.scale = scale
                self.base = ph * TILES
                self.stat, self.mv, self.ve, self.rs, self.sh = (
                    mem.take([2, 6]), mem.take([2, 2]), mem.take([2, 1]), mem.take([2, 1]), mem.take([2, 1]))
                self.out = mem.take([2, D])

        passed = sem("passed")

        def held(eng, s, value):
            eng.wait_ge(s, value)
            eng.sem_inc(passed, 1)

        def stats(v, ln):
            def sums(t, p, used):
                v.bn_stats(ln.stat[:, p, :], xs[:, t, :]).then_inc(ln.bn, 1)

            def moments(t, p, used):
                if used:
                    v.wait_ge(ln.shift, ln.base + t - 1)
                held(v, ln.bn, ln.base + t + 1)
                v.bn_aggr(ln.mv[:, p, :], ln.stat[:, p, :]).then_inc(ln.agg, 1)

            def variance(t, p, used):
                v.wait_ge(ln.agg, ln.base + t + 1)
                v.tensor_scalar(ln.ve[:, p, :], ln.mv[:, p, 1:2], EPS, ln.scale ** -2, ALU.add, ALU.mult).then_inc(ln.var, 1)
            return (0, sums), (0, moments), (0, variance)

        def rstd(g, ln, t, p, used):
            g.wait_ge(ln.var, ln.base + t + 1)
            if used:
                g.wait_ge(ln.xn, ln.base + t - 1)
            g.tensor_tensor(ln.rs[:, p, :], ln.ve[:, p, :], half[:, :], ALU.pow).then_inc(ln.rstd, 1)
            held(g, ln.rstd, ln.base + t + 1)
            g.tensor_scalar(ln.sh[:, p, :], ln.mv[:, p, 0:1], ln.rs[:, p, :], -1.0, ALU.mult, ALU.mult).then_inc(ln.shift, 1)

        def normalise(ln, transposed):
            def f(t, p, used):
                a = nc.scalar
                if used:
                    held(a, transposed, t - 1)
                a.wait_ge(ln.shift, ln.base + t + 1)
                dst, src = ln.out[:, p, :], xs[:, t, :]
                if ln is ln1:
                    dst = dst.rearrange("n (g k i) -> n k g i", k=8, g=4)
                    src = src.rearrange("n (k g i) -> n k g i", k=8, g=4)
                a.activation(dst, src, ACT.Identity, scale=ln.rs[:, p, :], bias=ln.sh[:, p, :]).then_inc(ln.xn, 1)
            return f

        class Staging(Arena):
            def take(self, shape, rows=P):
                n = int(np.prod(shape))
                a = xs[:, :, :].rearrange("p t i -> p (t i)")[0:rows, self.at:self.at + n]
                self.at += n
                assert self.at <= TILES * D
                return a.rearrange("p (a b) -> p a b", a=shape[0])

        m0 = Staging()
        kTf = m0.take([BATCH, SEQ])
        sel1f = m0.take([PAIRS1, P], rows=16)
        sel3f = m0.take([EB, P], rows=24)
        selrf = m0.take([PAIRS1, P], rows=48)
        cntf = m0.take([PAIRS1, 16])
        m0b = Arena()
        wq_in = m0b.take([2, 2, D])
        cq_in = m0b.take([2, 2, CQ])
        dq_in = m0b.take([2, 2, 2, RR], rows=96)
        et_in = m0b.take([2, 2, CD], rows=RR)
        ckv_in = m0b.take([2, 2, CD])
        wo_in = m0b.take([2, 2, D])
        ysb = m0b.take([2, 2, D], rows=96)
        zsb = m0b.take([2, D], rows=RR)
        m0c = Arena()
        m0c.at = m0d_at = m0b.at
        wraw = m0c.take([3, 8 * D])
        wabs = m0c.take([3, 1])
        wqb = m0c.take([8 * D], BF16)
        rgam = m0c.take([4])
        ones_sum = m0c.take([P])
        bgf = m0c.take([2, HID])
        bgh = m0c.take([2, HID], BF16)
        m0d = Arena()
        m0d.at = m0d_at
        w1f = m0d.take([2, EXPERTS * EH])
        w2f = m0d.take([EB, D])
        b2f = m0d.take([D], rows=3 * EXPERTS)

        ld_const, ld_x, ld_kT, ld_w0, ld_w1 = (sem(n) for n in ("ld_const", "ld_x", "ld_kT", "ld_w0", "ld_w1"))
        consts_done, tanh_done, g_done = sem("consts_done"), sem("tanh_done"), sem("g_done")
        k_hi, k_lo, w_hi, w_lo, m_ah, m_bh = (sem(n) for n in ("k_hi", "k_lo", "w_hi", "w_lo", "m_ah", "m_bh"))
        q_abs, q_sum, q_gam, q_rg, q_r1, q_r2, q_bf, q_tr, q_ev, q_bias = (
            sem(f"q_{n}") for n in ("abs", "sum", "gam", "rg", "r1", "r2", "bf", "tr", "ev", "bias"))
        m_ld = [sem("m_ld0"), sem("m_ld1")]
        m_y, m_ye, m_z, m_ze, m_a, m_ae, m_b, m_be = (
            sem(f"m_{n}") for n in ("y", "ye", "z", "ze", "a", "ae", "b", "be"))

        const_loads = [
            (graw[:, :], d["g"]), (idf[:, :], d["ident"]), (kvmask[:, :], d["kvmask"]), (rowhalf[:, :], d["rowhalf"]),
            (lomask[:, :, :], d["lomask"]), (sel1f, d["sel1"]), (sel3f, d["sel3"]), (selrf, d["selr"]), (cntf, d["cnt"]),
            (cosT[:, :, :], d["cosT"]), (sinT[:, :, :], d["sinT"]),
            (cosN[:, :, :], d["cosN"]), (sinN[:, :, :], d["sinN"]), (before[:, :, :], d["before"]),
            (bo[:, :], d["bo"].broadcast_to([P, D])), (bgf[:, 0, :], d["bg"].broadcast_to([P, HID])),
            (bgf[:, 1, :], d["bv"].broadcast_to([P, HID])), (part[:, :], d["part"]),
            (gb8[:, 0, :], d["gb"].broadcast_to([P, EXPERTS])), (gb8[:, 1, :], d["gbias"].broadcast_to([P, EXPERTS])),
            (b1c[:, :], d["b1"]), (gwT[:, :, :], d["gwT"]),
        ]
        N_CONST = 16 * len(const_loads)
        N_X = 16 * 3

        m1 = Arena()
        ln1 = Norm(0, m1, S_Q)
        qA = m1.take([2, 2, 4, SEQ], F16)
        qB = m1.take([2, 2, 4, SEQ], F16)
        kA = m1.take([2, 2, 8, SEQ], F16)
        kB = m1.take([2, 2, 8, SEQ], F16)
        mx1 = m1.take([2, 2, 16])
        PT1 = m1.take([2, 4, 512])
        vx = m1.take([2, 8, 32])
        oT1 = m1.take([2, 4, P])
        rec1 = m1.take([2, 32, 1])
        att1 = m1.take([2, 32, 8])
        (a_qt, a_qe, a_ql, a_kx, a_kb, a_p1, a_mx, a_mt, a_nm, a_s, a_exp, a_vx, a_pv, a_oe, a_o, a_rec, a_att,
         a_x, a_vz) = (sem(f"a_{n}") for n in (
             "qt", "qe", "ql", "kx", "kb", "p1", "mx", "mt", "nm", "s", "exp", "vx", "pv", "oe", "o", "rec", "att",
             "x", "vz"))
        D1 = 5

        m2 = Arena()
        ln2 = Norm(1, m2, 1.0)
        gx = m2.take([2, 4])
        sg = m2.take([2, 2])
        xm = m2.take([2, D])
        xqT = m2.take([2, 2, P], BF16)
        rpart = m2.take([2, 6], BF16)
        rres = m2.take([2, 2])
        rqT = m2.take([2, P], BF16, rows=6)
        val = m2.take([2, HID])
        sil = m2.take([2, HID])
        hm = m2.take([2, HID])
        gh = m2.take([2, 4])
        hqT = m2.take([2, 8, P], BF16)
        xb = m2.take([2, D])
        (f_ab, f_c1, f_c2, f_c3, f_sc, f_xm, f_rq, f_tr, f_xe, f_gp, f_vp, f_sil, f_h, f_ha, f_h1, f_h2,
         f_hm, f_ht, f_he, f_o, f_xb, f_x) = (sem(f"f_{n}") for n in (
             "ab", "c1", "c2", "c3", "sc", "xm", "rq", "tr", "xe", "gp", "vp", "sil", "h", "ha", "h1",
             "h2", "hm", "ht", "he", "o", "xb", "x"))
        D2 = 5

        m3 = Arena()
        ln3 = Norm(2, m3, S_X)
        xT3 = m3.take([2, 2, 2, P], F16)
        kin = m3.take([2, 2, 2, SEQ])
        kt1 = m3.take([2, 2, 2, SEQ])
        kt2 = m3.take([2, 2, 2, SEQ])
        kbd = m3.take([2, 2, 2, P], F16)
        vt1 = m3.take([2, 2, 2, CD])
        vt2 = m3.take([2, 2, 2, CD])
        vbd = m3.take([2, 2, 2, P], F16)
        qa = m3.take([2, 2, PAIRS1, P], F16)
        mx3 = m3.take([2, HEADS1])
        nm3 = m3.take([2, P], BF16, rows=16)
        PTf = m3.take([2, 512])
        PT3 = m3.take([2, 2, 2, 512], F16)
        rs3 = m3.take([2, P], rows=16)
        rr3 = m3.take([2, P], F16, rows=48)
        rb3 = m3.take([2, 512])
        cf = m3.take([2, 2, 512])
        cT = m3.take([2, 2, PAIRS1, P], F16)
        l_kin = [sem("l_kin0"), sem("l_kin1")]
        (l_tr, l_te, l_tl, l_qa, l_qe, l_ql, l_k1, l_k2, l_k3, l_kb, l_v1, l_v2, l_v3, l_vb, l_p1, l_mx, l_mt,
         l_nm, l_s, l_exp, l_ph, l_pl, l_pv, l_sum, l_rc, l_rh, l_rl, l_rb, l_re, l_c, l_ch, l_cl, l_o, l_x,
         l_z) = (sem(f"l_{n}") for n in (
             "tr", "te", "tl", "qa", "qe", "ql", "k1", "k2", "k3", "kb", "v1", "v2", "v3", "vb", "p1", "mx",
             "mt", "nm", "s", "exp", "ph", "pl", "pv", "sum", "rc", "rh", "rl", "rb", "re", "c", "ch", "cl",
             "o", "x", "z"))
        D3 = 5

        m4 = Arena()
        ln4 = Norm(3, m4, S_X)
        xT4 = m4.take([2, 2, 2, P], F16)
        sc4 = m4.take([2, 8])
        gt = m4.take([2, 8, 8])
        eq = m4.take([2, 8, 8])
        rank = m4.take([2, 8])
        half4 = m4.take([2, 8])
        mid4 = m4.take([2, 1])
        dif4 = m4.take([2, 8])
        th4 = m4.take([2, 8])
        es4 = m4.take([2, 8])
        comb = m4.take([2, 8])
        cpart = m4.take([2, 24], BF16)
        cres = m4.take([2, 2, 8])
        cT16 = m4.take([2, P], BF16, rows=24)
        hs = m4.take([2, 2, EB * P], F16)
        hf = m4.take([2, EB * P])
        sh4 = m4.take([2, EB * P])
        xo = m4.take([2, D])
        (e_tr, e_te, e_tl, e_hf, e_hh, e_sc, e_s1, e_rt, e_md, e_th, e_rk, e_cc, e_ct, e_cte, e_h, e_sl, e_cb2, e_hs, e_y, e_x, e_out) = (
             sem(f"e_{n}") for n in (
                 "tr", "te", "tl", "hf", "hh", "sc", "s1", "rt", "md", "th", "rk", "cc", "ct", "cte", "h", "sl", "cb2",
                 "hs", "y", "x", "out"))
        D4 = 5
        CHUNKS4 = [(0, 4), (4, 8), (8, EB)]

        block = ctx.enter_context(nc.Block())

        @block.sync
        def _(sp):
            def pair_weights(i, p, used):
                if used:
                    sp.wait_ge(m_be, i - 1)
                    sp.wait_ge(m_ae, i - 1)
                hs2 = bass.ts(i, 2)
                sp.dma_start(wq_in[:, p], d["Wq"][hs2].rearrange("h k i -> k h i")).then_inc(m_ld[p], 16)
                sp.dma_start(cq_in[:, p], d["Cq"][hs2].rearrange("h k q -> k h q")).then_inc(m_ld[p], 16)
                for h in range(2):
                    sp.dma_start(dq_in[:, p, h], d["Dq"][bass.ts(i, 2)][h].rearrange("(c q) r -> q c r", q=96)).then_inc(m_ld[p], 16)
                sp.dma_start(et_in[:, p], d["ET"][hs2].rearrange("h r i -> r h i")).then_inc(m_ld[p], 16)
                sp.dma_start(ckv_in[:, p], d["Ckv"][hs2].rearrange("h k i -> k h i")).then_inc(m_ld[p], 16)
                sp.dma_start(wo_in[:, p], d["WoT"][hs2].rearrange("h k o -> k h o")).then_inc(m_ld[p], 16)

            for i, name in enumerate(("gw", "vw")):
                sp.dma_start(wraw[:, i, :], d[name].rearrange("(c p) i -> p c i", p=P)).then_inc(ld_w0, 16)
            sp.dma_start(wraw[:, 2, :], d["ow"].rearrange("(c p) i -> p c i", p=P)).then_inc(ld_w0, 16)
            pair_weights(0, 0, False)
            for dst, src in const_loads:
                sp.dma_start(dst, src).then_inc(ld_const, 16)
            for r in range(2):
                sp.dma_start(kTf[64 * r:64 * r + 64], d["ctxT"]).then_inc(ld_kT, 16)
            pair_weights(1, 1, False)
            for r in range(2):
                sp.dma_start(ctx2[64 * r:64 * r + 64], d["ctx"].rearrange("b t i -> t b i")).then_inc(ld_x, 16)
            pair_weights(2, 0, True)
            pair_weights(3, 1, True)
            sp.wait_ge(k_lo, 1)
            sp.wait_ge(consts_done, 1)
            sp.dma_start(xs[:, :, :], d["x"].rearrange("(t p) i -> p t i", p=P)).then_inc(ld_x, 16)
            pair_weights(4, 0, True)
            pair_weights(5, 1, True)
            sp.wait_ge(q_ev, 6)
            sp.dma_start(w1f, d["w1T"]).then_inc(ld_w1, 16)
            sp.dma_start(w2f, d["w2T"]).then_inc(ld_w1, 16)
            sp.dma_start(b2f, d["b2"]).then_inc(ld_w1, 16)
            pair_weights(6, 0, True)
            pair_weights(7, 1, True)

            sp.wait_ge(f_x, TILES)

            def context(t, p, used):
                if used:
                    sp.wait_ge(l_k2, t - 1)
                    sp.wait_ge(l_k1, t - 1)
                for r in range(2):
                    rows = slice(64 * r, 64 * r + 64)
                    src = d["ctxT"][:, bass.ts(t, 2), :]
                    src2 = d["ctxTs"][:, bass.ts(t, 2), :]
                    sp.dma_start(kin[rows, p, 0], src).then_inc(l_kin[p], 16)
                    sp.dma_start(kin[rows, p, 1], src2).then_inc(l_kin[p], 16)
            tiles_loop(sp, 0, [(0, context)])

            def store(t, p, used):
                sp.wait_ge(e_x, t + 1)
                sp.dma_start(out[bass.ts(t, P), :], xs[:, t, :]).then_inc(e_out, 16)
            tiles_loop(sp, 0, [(0, store)])
            sp.wait_ge(e_out, 16 * TILES)

        @block.gpsimd
        def _(g):
            g.wait_ge(ld_const, N_CONST)
            g.wait_ge(q_rg, 1)
            for k in range(2):
                g.tensor_scalar(bgf[:, k], bgf[:, k], rgam[:, k:k + 1], None, ALU.mult).then_inc(q_bias, 1)
            for n in range(2):
                g.wait_ge(q_bias, 2 + 3 * n)
                g.tensor_copy(bgh, bgf).then_inc(q_bias, 1)
                g.wait_ge(q_bias, 3 + 3 * n)
                g.tensor_scalar(bgh, bgh, part[:, n:n + 1], None, ALU.mult).then_inc(q_bias, 1)
                g.wait_ge(q_bias, 4 + 3 * n)
                g.tensor_tensor(bgf, bgf, bgh, ALU.add).then_inc(q_bias, 1)
            g.wait_ge(q_bias, 8)
            g.tensor_copy(bgv[:, :, :], bgf).then_inc(q_bias, 1)

            g.wait_ge(m_be, PAIRS1)
            g.wait_ge(m_ae, PAIRS1)
            g.wait_ge(w_lo, 7)
            g.wait_ge(ld_x, N_X)
            g.wait_ge(consts_done, 1)
            for p in range(2):
                g.memset(vx[:, p], 0.0).then_inc(a_vz, 1)
            g.wait_ge(a_vz, 2)
            for p in range(2):
                g.tensor_copy(vx[:, p].rearrange("t n (k i) -> t n k i", k=2)[:, :, :, 8],
                              rowhalf[:, :].unsqueeze(1).broadcast_to([P, 8, 2])).then_inc(a_vz, 1)
            g.wait_ge(a_vz, 4)

            def a_keys(t, p, used):
                if used:
                    g.wait_ge(a_s, 4 * t - 4)
                src = khT[:, bass.ts(t, 2), :]
                g.tensor_tensor(kA[:, p], src.unsqueeze(2).broadcast_to([P, 2, 8, SEQ]),
                                kvmask[:, :].unsqueeze(1).unsqueeze(3).broadcast_to([P, 2, 8, SEQ]), ALU.mult).then_inc(a_kx, 1)
                src = klT[:, bass.ts(t, 2), :]
                g.tensor_tensor(kB[:, p], src.unsqueeze(2).broadcast_to([P, 2, 8, SEQ]),
                                lomask[:, :, :].unsqueeze(3).broadcast_to([P, 2, 8, SEQ]), ALU.mult).then_inc(a_kb, 1)

            def a_values(t, p, used):
                if used:
                    held(g, a_pv, 4 * t - 4)
                g.tensor_tensor(vx[:, p].rearrange("t n (k i) -> t n k i", k=2)[:, :, :, 0:8],
                                ctx2[:, bass.ts(t, 2), :].rearrange("t b (n k i) -> t (b n) k i", n=4, k=2),
                                rowhalf[:, :].unsqueeze(1).unsqueeze(3).broadcast_to([P, 8, 2, 8]),
                                ALU.mult).then_inc(a_vx, 1)

            tiles_loop(g, D1, [(0, lambda t, p, u: rstd(g, ln1, t, p, u)), (3, a_values), (1, a_keys)])

            g.wait_ge(a_x, TILES)

            def f_rparts(t, p, used):
                r = gx[:, p, 2:3]
                held(g, f_c2, t + 1)
                if used:
                    held(g, f_tr, t - 1)
                g.tensor_copy(rpart[:, p, 0:3], r.broadcast_to([P, 3])).then_inc(f_rq, 1)
                g.wait_ge(f_rq, 5 * t + 1)
                g.tensor_tensor(rres[:, p, 0:1], r, rpart[:, p, 0:1], ALU.subtract).then_inc(f_rq, 1)
                held(g, f_rq, 5 * t + 2)
                g.tensor_copy(rpart[:, p, 3:5], rres[:, p, 0:1].broadcast_to([P, 2])).then_inc(f_rq, 1)
                g.wait_ge(f_rq, 5 * t + 3)
                g.tensor_tensor(rres[:, p, 1:2], rres[:, p, 0:1], rpart[:, p, 3:4], ALU.subtract).then_inc(f_rq, 1)
                held(g, f_rq, 5 * t + 4)
                g.tensor_copy(rpart[:, p, 5:6], rres[:, p, 1:2]).then_inc(f_rq, 1)

            def f_round(t, p, used):
                held(g, f_h2, t + 1)
                if used:
                    held(g, f_ht, t - 1)
                g.tensor_scalar(hm[:, p], val[:, p], gh[:, p, 2:3], MAGIC, ALU.mult, ALU.add).then_inc(f_hm, 1)

            def f_xbias(t, p, used):
                if used:
                    g.wait_ge(f_x, t - 1)
                g.tensor_tensor(xb[:, p], xs[:, t, :], bo[:, :], ALU.add).then_inc(f_xb, 1)

            tiles_loop(g, D2, [(2, f_rparts), (0, lambda t, p, u: rstd(g, ln2, t, p, u)), (4, f_xbias), (3, f_round)])
            g.wait_ge(f_x, TILES)
            def twice(x, n):
                return x.unsqueeze(2).broadcast_to([P, 2, 2, n])

            def table(x, n):
                return x.unsqueeze(1).broadcast_to([P, 2, 2, n])

            def l_keys(t, p, used):
                g.wait_ge(l_kin[p], 32 * t + (64 - 32 * p))
                g.tensor_tensor(kt1[:, p], twice(kin[:, p, 0], SEQ), table(cosT[:, :, :], SEQ), ALU.mult).then_inc(l_k1, 1)
                g.tensor_tensor(kt2[:, p], twice(kin[:, p, 1], SEQ), table(sinT[:, :, :], SEQ), ALU.mult).then_inc(l_k2, 1)
                g.wait_ge(l_k1, t + 1)
                g.wait_ge(l_k2, t + 1)
                g.tensor_tensor(kt1[:, p], kt1[:, p], kt2[:, p], ALU.add).then_inc(l_k3, 1)
                held(g, l_k3, t + 1)
                if used:
                    held(g, l_s, 2 * t - 2)
                flat = kt1[:, p].rearrange("p b r n -> p b (r n)")
                g.tensor_copy(kbd[:, p, 0], flat).then_inc(l_kb, 1)
                g.wait_ge(l_kb, 2 * t + 1)
                g.tensor_tensor(kbd[:, p, 1], flat, kbd[:, p, 0], ALU.subtract).then_inc(l_kb, 1)

            def l_values(t, p, used):
                src = ctx2[:, bass.ts(t, 2), :]
                g.tensor_tensor(vt1[:, p], twice(src, CD), table(cosN[:, :, :], CD), ALU.mult).then_inc(l_v1, 1)
                for h in range(2):
                    lo = slice(32 * h, 32 * h + 32)
                    hi = slice(32 - 32 * h, 64 - 32 * h)
                    last = g.tensor_tensor(vt2[:, p, :, :, lo], twice(src[:, :, hi], 32), table(sinN[:, :, lo], 32), ALU.mult)
                last.then_inc(l_v2, 1)
                g.wait_ge(l_v1, t + 1)
                g.wait_ge(l_v2, t + 1)
                g.tensor_tensor(vt1[:, p], vt1[:, p], vt2[:, p], ALU.add).then_inc(l_v3, 1)
                held(g, l_v3, t + 1)
                if used:
                    held(g, l_pv, 2 * t - 2)
                flat = vt1[:, p].rearrange("p b r n -> p b (r n)")
                g.tensor_copy(vbd[:, p, 0], flat).then_inc(l_vb, 1)
                g.wait_ge(l_vb, 2 * t + 1)
                g.tensor_tensor(vbd[:, p, 1], flat, vbd[:, p, 0], ALU.subtract).then_inc(l_vb, 1)

            tiles_loop(g, D3, [(0, lambda t, p, u: rstd(g, ln3, t, p, u)), (3, l_values), (1, l_keys)])
            tiles_loop(g, D4, [(0, lambda t, p, u: rstd(g, ln4, t, p, u))])

        @block.scalar
        def _(a):
            def ternary_evac(js):
                for j in js:
                    a.wait_ge(q_tr, j + 1)
                    src = bank[6 + j % 2][:, :].bitcast(BF16)
                    if j < 4:
                        k, m = j // 2, j % 2
                        dst = wgv[:, m, k * HID:(k + 1) * HID]
                    else:
                        m = j - 4
                        dst = wow[:, 4 * m:4 * m + 4, :]
                    a.activation(dst, src if j < 4 else src.rearrange("p (c i) -> p c i", c=4), ACT.Copy).then_inc(q_ev, 1)

            def pair_evac(i, p, used):
                def y(h):
                    a.wait_ge(m_y, 2 * i + h + 1)
                    a.activation(ysb[:, h, :, :], bank[4 * h][0:96, :].rearrange("q (c i) -> q c i", c=2), ACT.Copy).then_inc(m_ye, 1)

                def z(h):
                    a.wait_ge(m_z, 2 * i + h + 1)
                    a.activation(zsb[:, h, :], bank[1 + 4 * h][0:RR, 0:D], ACT.Copy).then_inc(m_ze, 1)
                y(0)
                y(1)
                z(0)
                a.wait_ge(m_b, i + 1)
                a.activation(wB[:, 0, i, :], bank[3][:, 0:D], ACT.Copy, scale=S_B).then_inc(m_bh, 1)
                z(1)
                a.wait_ge(m_a, i + 1)
                a.activation(wA[:, 0, :, bass.ts(i, P)], bank[2][:, 0:2 * P].rearrange("p (c n) -> p c n", c=2),
                             ACT.Copy, scale=S_A).then_inc(m_ah, 1)

            pair_evac(0, 0, False)
            a.wait_ge(ld_const, N_CONST)
            a.activation(gT[:, :], graw[:, :], ACT.Tanh).then_inc(tanh_done, 1)
            ternary_evac((0, 1))
            a.wait_ge(ld_kT, 32)
            a.activation(khT[:, :, :], kTf, ACT.Copy, scale=S_K).then_inc(k_hi, 1)
            pair_evac(1, 1, False)
            ternary_evac((2, 3, 4, 5))
            with a.Fori(2, 6, 1) as i:
                pair_evac(i, 0, True)
            a.wait_ge(ld_w1, 48)
            a.activation(w1T[:, 0], w1f, ACT.Copy, scale=S_W1).then_inc(w_hi, 1)
            pair_evac(6, 0, True)
            a.activation(w2T[:, 0], w2f, ACT.Copy, scale=S_W2).then_inc(w_hi, 1)
            pair_evac(7, 1, True)

            a.wait_ge(w_lo, 7)
            a.wait_ge(q_bias, 9)

            def a_nmax(t, p, used):
                a.wait_ge(a_mt, t + 1)
                if used:
                    held(a, a_s, 4 * t - 4)
                a.activation(qB[64:80, p].rearrange("p b g n -> p b (g n)"),
                             bank[3][0:16, 0:2 * P].unsqueeze(1).broadcast_to([16, 2, 2 * P]),
                             ACT.Copy, scale=-1.0 / (S_Q * S_K)).then_inc(a_nm, 1)

            def a_exps(j):
                def f(t, p, used):
                    if used and j == 0:
                        held(a, a_pv, 4 * t - 4)
                    a.wait_ge(a_s, 4 * t + j + 1)
                    a.activation(PT1[:, p, j], bank[4 + j % 2][:, :], ACT.Exp, scale=8.0 ** -0.5 / (S_Q * S_K)).then_inc(a_exp, 1)
                return f

            def a_oevac(t, p, used):
                a.wait_ge(a_pv, 4 * t + 4)
                if used:
                    held(a, a_o, t - 1)
                a.activation(oT1[:, p].rearrange("p g n -> p (g n)"), bank[6][:, :], ACT.Copy).then_inc(a_oe, 1)

            def a_qevac(t, p, used):
                a.wait_ge(a_qt, t + 1)
                if used:
                    held(a, a_s, 4 * t - 4)
                src = bank[0][0:64, :].rearrange("p (g b n) -> p g b n", g=4, b=2)
                a.activation(qA[0:64, p].rearrange("p b g n -> p g b n"), src, ACT.Copy).then_inc(a_qe, 1)
                a.wait_ge(a_qe, 2 * t + 1)
                a.activation(qB[0:64, p], qA[0:64, p], ACT.Copy).then_inc(a_qe, 1)

            tiles_loop(a, D1, [(3, a_nmax), (2, a_qevac), (3, a_exps(0)), (3, a_exps(1)), (4, a_oevac), (1, normalise(ln1, a_qt)),
                               (3, a_exps(2)), (3, a_exps(3))])

            a.wait_ge(a_x, TILES)

            def f_xevac(t, p, used):
                a.wait_ge(f_tr, t + 1)
                if used:
                    held(a, f_vp, 2 * t - 2)
                a.activation(xqT[:, p], bank[0][:, 0:P].bitcast(F16).rearrange("p (c n) -> p c n", c=2),
                             ACT.Copy, bias=-ROUND0)
                a.activation(rqT[:, p], bank[7][0:6, 0:P // 2].bitcast(BF16), ACT.Copy).then_inc(f_xe, 1)

            def f_silu(j):
                def f(t, p, used):
                    if used and j == 0:
                        held(a, f_h, 2 * t - 2)
                    a.wait_ge(f_gp, 2 * t + j + 1)
                    a.activation(sil[:, p, j * 512:(j + 1) * 512], bank[1 + j][:, :], ACT.Silu, scale=sg[:, p, 0:1]).then_inc(f_sil, 1)
                return f

            def f_hevac(t, p, used):
                a.wait_ge(f_ht, t + 1)
                if used:
                    held(a, f_o, t - 1)
                a.activation(hqT[:, p], bank[5][:, :].bitcast(F16).rearrange("p (c n) -> p c n", c=8),
                             ACT.Copy, bias=-ROUND0).then_inc(f_he, 1)

            tiles_loop(a, D2, [(3, f_silu(0)), (3, f_silu(1)), (4, f_hevac), (1, normalise(ln2, f_tr)), (2, f_xevac)])

            a.wait_ge(f_x, TILES)

            def l_tevac(t, p, used):
                a.wait_ge(l_tr, t + 1)
                if used:
                    held(a, l_qa, 2 * t - 2)
                a.activation(xT3[:, p, 0], bank[0][:, 0:2 * P].rearrange("p (c n) -> p c n", c=2), ACT.Copy).then_inc(l_te, 1)

            def l_qevac(j):
                def f(t, p, used):
                    if used and j == 0:
                        held(a, l_s, 2 * t - 2)
                    a.wait_ge(l_qa, 2 * t + j + 1)
                    a.activation(qa[:, p, 0, 4 * j:4 * j + 4], bank[1][:, :].rearrange("p (c n) -> p c n", c=4),
                                 ACT.Copy, scale=S_L / (S_X * S_A)).then_inc(l_qe, 1)
                return f

            def l_nmax(t, p, used):
                a.wait_ge(l_mt, t + 1)
                if used:
                    held(a, l_s, 2 * t - 2)
                a.activation(nm3[:, p], bank[3][0:16, 0:P], ACT.Copy, scale=-1.0, bias=S_P * S_L * S_K).then_inc(l_nm, 1)

            def l_exps(b):
                def f(t, p, used):
                    a.wait_ge(l_s, 2 * t + b + 1)
                    if used:
                        held(a, l_pl, 2 * t + b - 1)
                    elif t:
                        a.wait_ge(l_pl, 2 * t + b - 1)
                    a.activation(PTf[:, b], bank[4][:, :], ACT.Exp, scale=1.0 / (S_L * S_K)).then_inc(l_exp, 1)
                    if used and b == 0:
                        held(a, l_pv, 2 * t - 2)
                    a.wait_ge(l_exp, 2 * t + b + 1)
                    a.activation(PT3[:, p, 0, b], PTf[:, b], ACT.Copy).then_inc(l_ph, 1)
                return f

            def l_revac(b):
                def f(t, p, used):
                    a.wait_ge(l_rb, 2 * t + b + 1)
                    if used:
                        held(a, l_c, 2 * t + b - 1)
                    elif t:
                        a.wait_ge(l_c, 2 * t + b - 1)
                    a.activation(rb3[:, b], bank[6][:, :], ACT.Copy).then_inc(l_re, 1)
                return f

            def l_chigh(b):
                def f(t, p, used):
                    if used and b == 0:
                        held(a, l_o, t - 1)
                    a.wait_ge(l_c, 2 * t + b + 1)
                    a.activation(cT[:, p, 0, :, 64 * b:64 * b + 64], cf[:, p, b].rearrange("p (k n) -> p k n", k=8),
                                 ACT.Copy).then_inc(l_ch, 1)
                return f

            tiles_loop(a, D3, [(2, l_qevac(0)), (3, l_nmax), (1, normalise(ln3, l_tr)), (3, l_exps(0)), (4, l_revac(0)), (4, l_revac(1)),
                               (1, l_tevac), (4, l_chigh(0)), (2, l_qevac(1)), (3, l_exps(1)), (4, l_chigh(1))])

            a.wait_ge(l_x, TILES)

            def e_tevac(t, p, used):
                a.wait_ge(e_tr, t + 1)
                if used:
                    held(a, e_h, 3 * t - 3)
                a.activation(xT4[:, p, 0], bank[0][:, 0:2 * P].rearrange("p (c n) -> p c n", c=2), ACT.Copy).then_inc(e_te, 1)

            def e_tanh(t, p, used):
                a.wait_ge(e_rk, t + 1)
                if used:
                    held(a, e_cc, 6 * t - 11)
                a.activation(th4[:, p], dif4[:, p], ACT.Tanh).then_inc(e_th, 1)

            def e_ctev(t, p, used):
                a.wait_ge(e_ct, t + 1)
                if used:
                    held(a, e_y, t - 1)
                a.activation(cT16[:, p], bank[2][0:24, 0:P // 2].bitcast(BF16), ACT.Copy).then_inc(e_cte, 1)

            def e_silu(c):
                def f(t, p, used):
                    j0, j1 = CHUNKS4[c]
                    if used and c == 0:
                        held(a, e_hf, 3 * t - 3)
                    a.wait_ge(e_h, 3 * t + c + 1)
                    for j in range(j0, j1):
                        last = a.activation(sh4[:, p, j * P:(j + 1) * P], bank[3 + (p + c) % 2][:, (j - j0) * P:(j - j0 + 1) * P],
                                            ACT.Silu, bias=b1c[:, j:j + 1], scale=1.0 / (S_X * S_W1))
                    last.then_inc(e_sl, 1)
                return f

            def e_high(t, p, used):
                a.wait_ge(e_hf, 3 * t + 3)
                if used:
                    held(a, e_y, t - 1)
                a.activation(hs[:, p, 0], hf[:, p], ACT.Copy).then_inc(e_hh, 1)

            tiles_loop(a, D4, [(2, e_tevac), (3, e_silu(0)), (3, e_ctev), (3, e_silu(1)), (1, normalise(ln4, e_tr)),
                               (3, e_silu(2)), (2, e_tanh), (3, e_high)])

        @block.tensor
        def _(pe):
            def ternary_transposes(js):
                for j in js:
                    if j >= 2:
                        pe.wait_ge(q_ev, j - 1)
                    dst = bank[6 + j % 2][:, :].bitcast(BF16)
                    if j < 4:
                        k, m = j // 2, j % 2
                        pe.wait_ge(q_bf, k + 1)
                        for c in range(8):
                            last = pe.transpose(dst[:, c * P:(c + 1) * P], wqb[:, c * D + m * P:c * D + (m + 1) * P], idb[:, :])
                    else:
                        m = j - 4
                        pe.wait_ge(q_bf, 3)
                        for c in range(4):
                            for o in range(2):
                                last = pe.transpose(dst[:, c * D + o * P:c * D + (o + 1) * P],
                                                    wqb[:, o * HID + (4 * m + c) * P:o * HID + (4 * m + c + 1) * P], idb[:, :])
                    last.then_inc(q_tr, 1)

            def pair_products(i, p, used):
                pe.wait_ge(m_ld[p], 56 * i + (112 - 56 * p))
                for h in range(2):
                    for c in range(2):
                        last = pe.matmul(bank[4 * h][0:96, c * D:(c + 1) * D], cq_in[:, p, h, c * 96:(c + 1) * 96],
                                         wq_in[:, p, h, :], start=True, stop=True)
                    last.then_inc(m_y, 1)

                def z(h):
                    held(pe, m_ye, 2 * i + h + 1)
                    for c in range(2):
                        last = pe.matmul(bank[1 + 4 * h][0:RR, 0:D], dq_in[:, p, h, c, :], ysb[:, h, c, :], start=(c == 0), stop=(c == 1))
                    last.then_inc(m_z, 1)
                z(0)
                if used:
                    held(pe, m_be, i)
                elif i:
                    pe.wait_ge(m_be, i)
                for h in range(2):
                    last = pe.matmul(bank[3][64 * h:64 * h + 64, 0:D], ckv_in[:, p, h, :], wo_in[:, p, h, :], start=True, stop=True)
                last.then_inc(m_b, 1)
                z(1)
                held(pe, m_ze, 2 * i + 2)
                if used:
                    held(pe, m_ae, i)
                elif i:
                    pe.wait_ge(m_ae, i)
                for h in range(2):
                    for m in range(2):
                        last = pe.matmul(bank[2][:, m * P + h * 64:m * P + h * 64 + 64], zsb[:, h, m * P:(m + 1) * P],
                                         et_in[:, p, h, :], start=True, stop=True)
                last.then_inc(m_a, 1)

            pair_products(0, 0, False)
            pe.wait_ge(q_abs, 3)
            pe.matmul(bank[6][:, 0:3], ones_sum, wabs.rearrange("p a b -> p (a b)"), start=True, stop=True).then_inc(q_sum, 1)
            pe.wait_ge(ld_const, N_CONST)
            pe.wait_ge(consts_done, 1)
            pe.wait_ge(q_gam, 1)
            ternary_transposes((0, 1))
            pair_products(1, 1, False)
            ternary_transposes((2, 3, 4, 5))
            with pe.Fori(2, PAIRS1 - 1, 2) as i:
                pair_products(i, 0, True)
                pair_products(i + 1, 1, True)

            pe.wait_ge(m_ae, PAIRS1)
            pe.wait_ge(m_be, PAIRS1)

            def a_trans(t, p, used):
                held(pe, ln1.xn, ln1.base + t + 1)
                if used:
                    held(pe, a_qe, 2 * t)
                    held(pe, a_ql, t)
                elif t:
                    pe.wait_ge(a_qe, 2 * t)
                    pe.wait_ge(a_ql, t)
                q = ln1.out[:, p, :].rearrange("n (g c) -> n g c", g=4)
                for g in range(4):
                    last = pe.transpose(bank[0][0:64, g * P:(g + 1) * P], q[:, g], idf[:, :])
                last.then_inc(a_qt, 1)

            def a_pass1(j):
                def f(t, p, used):
                    if j == 0:
                        held(pe, a_qe, 2 * t + 1)
                        held(pe, a_kx, t + 1)
                    b, gp = j // 2, j % 2
                    if used:
                        held(pe, a_mx, 4 * t + j - 1)
                    elif 4 * t + j >= 2:
                        pe.wait_ge(a_mx, 4 * t + j - 1)
                    pe.matmul(bank[1 + j % 2][:, :], qA[0:64, p, b, 2 * gp:2 * gp + 2, :].rearrange("p g n -> p (g n)"),
                              kA[0:64, p, b].rearrange("p k n -> p (k n)"), start=True, stop=True).then_inc(a_p1, 1)
                return f

            def a_maxT(t, p, used):
                held(pe, a_mx, 4 * t + 4)
                if used:
                    held(pe, a_nm, t)
                elif t:
                    pe.wait_ge(a_nm, t)
                for gp in range(2):
                    last = pe.transpose(bank[3][0:16, gp * P:(gp + 1) * P], mx1[:, p, gp, :], idf[:, :])
                last.then_inc(a_mt, 1)

            def a_scores(j):
                def f(t, p, used):
                    if j == 0:
                        held(pe, a_nm, t + 1)
                        held(pe, a_ql, t + 1)
                        held(pe, a_qe, 2 * t + 2)
                        held(pe, a_kb, t + 1)
                    b = j // 2
                    if used:
                        held(pe, a_exp, 4 * t + j - 1)
                    elif 4 * t + j >= 2:
                        pe.wait_ge(a_exp, 4 * t + j - 1)
                    for c in range(2):
                        pair = 2 * (j % 2) + c
                        dst = bank[4 + j % 2][:, c * D:(c + 1) * D]
                        pe.matmul(dst, kA[:, p, b, 2 * pair:2 * pair + 2, :].rearrange("p k n -> p (k n)"),
                                  qA[:, p, b].rearrange("p g n -> p (g n)"), start=True, stop=False)
                        last = pe.matmul(dst, kB[0:80, p, b, 2 * pair:2 * pair + 2, :].rearrange("p k n -> p (k n)"),
                                         qB[0:80, p, b].rearrange("p g n -> p (g n)"), start=False, stop=True)
                    last.then_inc(a_s, 1)
                return f

            def a_weighted(j):
                def f(t, p, used):
                    if j == 0:
                        held(pe, a_exp, 4 * t + 4)
                        held(pe, a_vx, t + 1)
                        if used:
                            held(pe, a_oe, t)
                        elif t:
                            pe.wait_ge(a_oe, t)
                    b = j // 2
                    for c in range(2):
                        pair = 2 * (j % 2) + c
                        dst = bank[6][32 * pair:32 * pair + 32, :].rearrange("p (g b n) -> p g b n", g=4, b=2)
                        last = pe.matmul(dst[:, :, b], vx[:, p, 4 * b + pair, :],
                                         PT1[:, p, j, c * D:(c + 1) * D].rearrange("p (g n) -> p g n", g=4), start=True, stop=True)
                    last.then_inc(a_pv, 1)
                return f

            def a_outT(t, p, used):
                held(pe, a_oe, t + 1)
                if used:
                    held(pe, a_att, t)
                elif t:
                    pe.wait_ge(a_att, t)
                for g in range(4):
                    last = pe.transpose(bank[7][:, g * P:(g + 1) * P], oT1[:, p, g], idf[:, :])
                last.then_inc(a_o, 1)

            tiles_loop(pe, D1, [(2, a_trans), (3, a_maxT), (4, a_weighted(0)), (4, a_weighted(1)), (4, a_weighted(2)),
                                (3, a_scores(0)), (3, a_scores(1)), (2, a_pass1(0)), (4, a_weighted(3)), (2, a_pass1(1)),
                                (3, a_scores(2)), (2, a_pass1(2)), (3, a_scores(3)), (2, a_pass1(3)), (4, a_outT)])

            pe.wait_ge(a_x, TILES)

            def f_trans(t, p, used):
                held(pe, f_xm, t + 1)
                held(pe, f_rq, 5 * t + 5)
                if used:
                    held(pe, f_xe, t)
                elif t:
                    pe.wait_ge(f_xe, t)
                q = xm[:, p, :].bitcast(F16).rearrange("p (n two) -> p n two", two=2)[:, :, 0]
                dst = bank[0][:, 0:P].bitcast(F16)
                for c in range(2):
                    pe.transpose(dst[:, c * P:(c + 1) * P], q[:, c * P:(c + 1) * P], id16[:, :])
                pe.transpose(bank[7][0:6, 0:P // 2].bitcast(BF16), rpart[:, p, :], idb[:, :]).then_inc(f_tr, 1)

            def f_prod(k, j):
                made, done = ((f_gp, f_sil), (f_vp, f_h))[k]

                def f(t, p, used):
                    if k == 0 and j == 0:
                        held(pe, f_xe, t + 1)
                    if used:
                        held(pe, done, 2 * t + j - 1)
                    elif t:
                        pe.wait_ge(done, 2 * t + j - 1)
                    dst = bank[1 + 2 * k + j][:, :]
                    cols = slice(k * HID + j * 512, k * HID + (j + 1) * 512)
                    for c in range(2):
                        pe.matmul(dst, xqT[:, p, c, :], wgv[:, c, cols], start=(c == 0), stop=False)
                    pe.matmul(dst, rqT[:, p], bgv[0:6, k, j * 512:(j + 1) * 512], start=False, stop=True).then_inc(made, 1)
                return f

            def f_htrans(t, p, used):
                held(pe, f_hm, t + 1)
                if used:
                    held(pe, f_he, t)
                elif t:
                    pe.wait_ge(f_he, t)
                q = hm[:, p, :].bitcast(F16).rearrange("p (n two) -> p n two", two=2)[:, :, 0]
                dst = bank[5][:, :].bitcast(F16)
                for c in range(8):
                    last = pe.transpose(dst[:, c * P:(c + 1) * P], q[:, c * P:(c + 1) * P], id16[:, :])
                last.then_inc(f_ht, 1)

            def f_outp(t, p, used):
                held(pe, f_he, t + 1)
                if used:
                    held(pe, f_x, t)
                elif t:
                    pe.wait_ge(f_x, t)
                for c in range(8):
                    last = pe.matmul(bank[6][:, 0:D], hqT[:, p, c, :], wow[:, c, :], start=(c == 0), stop=(c == 7))
                last.then_inc(f_o, 1)

            pe.wait_ge(q_bias, 9)
            tiles_loop(pe, D2, [(3, f_prod(0, 0)), (3, f_prod(0, 1)), (3, f_prod(1, 0)), (3, f_prod(1, 1)), (4, f_htrans),
                                (2, f_trans), (4, f_outp)])

            pe.wait_ge(f_x, TILES)

            def l_trans(t, p, used):
                held(pe, ln3.xn, ln3.base + t + 1)
                if used:
                    held(pe, l_te, t)
                    held(pe, l_tl, t)
                elif t:
                    pe.wait_ge(l_te, t)
                    pe.wait_ge(l_tl, t)
                if not isinstance(t, int) or t >= 3:
                    held(pe, l_rc, t - 2)
                for c in range(2):
                    last = pe.transpose(bank[0][:, c * P:(c + 1) * P], ln3.out[:, p, c * P:(c + 1) * P], idf[:, :])
                last.then_inc(l_tr, 1)

            def l_query(j):
                def f(t, p, used):
                    if j == 0:
                        held(pe, l_te, t + 1)
                        held(pe, l_tl, t + 1)
                    for done in (l_qe, l_ql):
                        if used:
                            held(pe, done, 2 * t + j)
                        elif 2 * t + j:
                            pe.wait_ge(done, 2 * t + j)
                    for k in range(4):
                        pair = 4 * j + k
                        for n, (wp, xp, c) in enumerate((wp, xp, c) for wp, xp in ((0, 0), (0, 1), (1, 0)) for c in range(2)):
                            last = pe.matmul(bank[1][:, k * P:(k + 1) * P], wA[:, wp, c, pair * P:(pair + 1) * P],
                                             xT3[:, p, xp, c, :], start=(n == 0), stop=(n == 5))
                    last.then_inc(l_qa, 1)
                return f

            def l_pass1(j):
                def f(t, p, used):
                    held(pe, l_qe, 2 * t + j + 1)
                    if j == 0:
                        held(pe, l_kb, 2 * t + 1)
                    if used:
                        held(pe, l_mx, 2 * t + j)
                    elif 2 * t + j:
                        pe.wait_ge(l_mx, 2 * t + j)
                    for b in range(2):
                        for k in range(4):
                            last = pe.matmul(bank[2][64 * b:64 * b + 64, k * P:(k + 1) * P],
                                             qa[:, p, 0, 4 * j + k, 64 * b:64 * b + 64], kbd[:, p, 0, b], start=True, stop=True)
                    last.then_inc(l_p1, 1)
                return f

            def l_maxT(t, p, used):
                held(pe, l_mx, 2 * t + 2)
                if used:
                    held(pe, l_nm, t)
                elif t:
                    pe.wait_ge(l_nm, t)
                pe.transpose(bank[3][0:16, 0:P], mx3[:, p], idf[:, :]).then_inc(l_mt, 1)

            def l_scores(b):
                def f(t, p, used):
                    if b == 0:
                        held(pe, l_nm, t + 1)
                        held(pe, l_kb, 2 * t + 2)
                        held(pe, l_ql, 2 * t + 2)
                    if used:
                        held(pe, l_exp, 2 * t + b)
                    elif 2 * t + b:
                        pe.wait_ge(l_exp, 2 * t + b)
                    dst = bank[4][:, :].rearrange("p (k n) -> p k n", k=8)
                    for n, (kp, qp) in enumerate(((0, 0), (0, 1), (1, 0))):
                        pe.matmul(dst, kbd[:, p, kp, b], qa[:, p, qp, :, 64 * b:64 * b + 64], start=(n == 0), stop=False)
                    for k in range(PAIRS1):
                        last = pe.matmul(bank[4][:, 64 * k:64 * k + 64], sel1[:, k, :], nm3[:, p, 64 * b:64 * b + 64],
                                         start=False, stop=(k == PAIRS1 - 1))
                    last.then_inc(l_s, 1)
                return f

            def l_sums(t, p, used):
                held(pe, l_ph, 2 * t + 2)
                held(pe, l_pl, 2 * t + 2)
                for b in range(2):
                    for n, (k, pp) in enumerate((k, pp) for k in range(PAIRS1) for pp in range(2)):
                        last = pe.matmul(bank[0][0:16, D + 64 * b:D + 64 * b + 64], cnt[:, k, :], PT3[:, p, pp, b, 64 * k:64 * k + 64],
                                         start=(n == 0), stop=(n == 2 * PAIRS1 - 1))
                last.then_inc(l_sum, 1)

            def l_recips(b):
                def f(t, p, used):
                    if b == 0:
                        held(pe, l_rh, t + 1)
                        held(pe, l_rl, t + 1)
                    if used:
                        held(pe, l_re, 2 * t + b)
                    elif 2 * t + b:
                        pe.wait_ge(l_re, 2 * t + b)
                    for k in range(PAIRS1):
                        last = pe.matmul(bank[6][:, 64 * k:64 * k + 64], selr[:, k, :], rr3[:, p, 64 * b:64 * b + 64],
                                         start=True, stop=True)
                    last.then_inc(l_rb, 1)
                return f

            def l_weighted(b):
                def f(t, p, used):
                    if b == 0:
                        held(pe, l_vb, 2 * t + 2)
                    if used:
                        held(pe, l_c, 2 * t + b)
                    elif 2 * t + b:
                        pe.wait_ge(l_c, 2 * t + b)
                    for n, (vp, pp) in enumerate(((0, 0), (0, 1), (1, 0))):
                        last = pe.matmul(bank[5][:, :], vbd[:, p, vp, b], PT3[:, p, pp, b], start=(n == 0), stop=(n == 2))
                    last.then_inc(l_pv, 1)
                return f

            def l_outp(part):
                def f(t, p, used):
                    if part == 0:
                        held(pe, l_ch, 2 * t + 2)
                        held(pe, l_cl, 2 * t + 2)
                        if used:
                            held(pe, l_x, t)
                        elif t:
                            pe.wait_ge(l_x, t)
                    for k in range(4 * part, 4 * part + 4):
                        for n, (cp, wp) in enumerate(((0, 0), (0, 1), (1, 0))):
                            last = pe.matmul(bank[7][:, 0:D], cT[:, p, cp, k, :], wB[:, wp, k, :],
                                             start=(k == 0 and n == 0), stop=(k == PAIRS1 - 1 and n == 2))
                    if part == 1:
                        last.then_inc(l_o, 1)
                return f

            tiles_loop(pe, D3, [(2, l_query(0)), (3, l_maxT), (4, l_sums), (5, l_outp(0)), (3, l_scores(0)), (2, l_pass1(0)),
                                (4, l_recips(0)), (5, l_outp(1)), (4, l_weighted(0)), (4, l_recips(1)),
                                (1, l_trans), (2, l_query(1)), (4, l_weighted(1)),
                                (3, l_scores(1)), (2, l_pass1(1))])

            pe.wait_ge(l_x, TILES)

            def e_trans(t, p, used):
                held(pe, ln4.xn, ln4.base + t + 1)
                for done in (e_te, e_tl):
                    if used:
                        held(pe, done, t)
                    elif t:
                        pe.wait_ge(done, t)
                for c in range(2):
                    last = pe.transpose(bank[0][:, c * P:(c + 1) * P], ln4.out[:, p, c * P:(c + 1) * P], idf[:, :])
                last.then_inc(e_tr, 1)

            def e_score(t, p, used):
                held(pe, e_te, t + 1)
                held(pe, e_tl, t + 1)
                if used:
                    held(pe, e_s1, t)
                elif t:
                    pe.wait_ge(e_s1, t)
                for n, (xp, wp, c) in enumerate((xp, wp, c) for xp, wp in ((0, 0), (0, 1), (1, 0)) for c in range(2)):
                    last = pe.matmul(bank[1][:, 0:8], xT4[:, p, xp, c, :], gw16[:, wp, c, :], start=(n == 0), stop=(n == 5))
                last.then_inc(e_sc, 1)

            def e_combT(t, p, used):
                held(pe, e_cc, 6 * t + 6)
                if used:
                    held(pe, e_cte, t)
                elif t:
                    pe.wait_ge(e_cte, t)
                pe.transpose(bank[2][0:24, 0:P // 2].bitcast(BF16), cpart[:, p], idb[:, :]).then_inc(e_ct, 1)

            def e_hid(c):
                def f(t, p, used):
                    j0, j1 = CHUNKS4[c]
                    if used:
                        held(pe, e_sl, 3 * t + c - 1)
                    elif 3 * t + c >= 2:
                        pe.wait_ge(e_sl, 3 * t + c - 1)
                    for j in range(j0, j1):
                        for n, (wp, xp, k) in enumerate((wp, xp, k) for wp, xp in ((0, 0), (0, 1), (1, 0)) for k in range(2)):
                            last = pe.matmul(bank[3 + (p + c) % 2][:, (j - j0) * P:(j - j0 + 1) * P], w1T[:, wp, k, j * P:(j + 1) * P],
                                             xT4[:, p, xp, k, :], start=(n == 0), stop=(n == 5))
                    last.then_inc(e_h, 1)
                return f

            def e_spread(c):
                def f(t, p, used):
                    j0, j1 = CHUNKS4[c]
                    if c == 0:
                        held(pe, e_cte, t + 1)
                    if used:
                        held(pe, e_hf, 3 * t + c - 1)
                    elif 3 * t + c >= 2:
                        pe.wait_ge(e_hf, 3 * t + c - 1)
                    for j in range(j0, j1):
                        last = pe.matmul(bank[5 + (p + c) % 2][:, (j - j0) * P:(j - j0 + 1) * P], sel3[:, j, :], cT16[:, p],
                                         start=True, stop=True)
                    last.then_inc(e_cb2, 1)
                return f

            def e_outp(t, p, used):
                held(pe, e_hs, t + 1)
                if used:
                    held(pe, e_x, t)
                elif t:
                    pe.wait_ge(e_x, t)
                for n, (j, hp, wp) in enumerate((j, hp, wp) for j in range(EB) for hp, wp in ((0, 0), (0, 1), (1, 0))):
                    pe.matmul(bank[7][:, 0:D], hs[:, p, hp, j * P:(j + 1) * P], w2T[:, wp, j, :], start=(n == 0), stop=False)
                for n in range(3):
                    last = pe.matmul(bank[7][:, 0:D], cT16[:, p], b2s[:, n, :], start=False, stop=(n == 2))
                last.then_inc(e_y, 1)

            tiles_loop(pe, D4, [(2, e_trans), (3, e_hid(0)), (3, e_combT), (3, e_hid(1)), (3, e_spread(0)), (3, e_spread(1)),
                                (2, e_score), (3, e_hid(2)), (3, e_spread(2)), (4, e_outp)])

        @block.vector
        def _(v):
            v.memset(half[:, :], -0.5)
            v.memset(klT[64:128, :, :], S_Q * S_K)
            v.memset(ones_sum, 1.0)
            v.wait_ge(ld_w0, 48)
            for k in range(3):
                v.tensor_reduce(wabs[:, k], wraw[:, k], AX.X, ALU.add, apply_absolute_value=True).then_inc(q_abs, 1)
            v.wait_ge(ld_const, N_CONST)
            v.tensor_tensor(gb8[:, 0, :], gb8[:, 0, :], gb8[:, 1, :], ALU.add)
            v.tensor_copy(id16[:, :], idf[:, :])
            v.tensor_copy(idb[:, :], idf[:, :])
            v.tensor_scalar(gw16[:, 0], gwT[:, :, :], S_W1, None, ALU.mult).then_inc(g_done, 1)
            v.wait_ge(g_done, 1)
            v.scalar_tensor_tensor(gw16[:, 1], gwT[:, :, :], S_W1, gw16[:, 0], ALU.mult, ALU.subtract).then_inc(g_done, 1)
            v.tensor_copy(selr[:, :, :], selrf)
            v.tensor_copy(cnt[:, :, :], cntf)
            v.tensor_copy(sel1[:, :, :], sel1f)
            v.tensor_copy(sel3[:, :, :], sel3f).then_inc(consts_done, 1)
            v.wait_ge(q_sum, 1)
            v.tensor_scalar(gam[:, 0:3], bank[6][:, 0:3], 1.0 / (HID * D), 1e-5, ALU.mult, ALU.max).then_inc(q_gam, 1)
            v.wait_ge(q_gam, 1)
            v.reciprocal(rgam[:, 0:3], gam[:, 0:3]).then_inc(q_rg, 1)
            v.wait_ge(q_rg, 1)

            def ternary(k):
                v.tensor_scalar(wraw[:, k], wraw[:, k], rgam[:, k:k + 1], BIG, ALU.mult, ALU.add).then_inc(q_r1, 1)
                v.wait_ge(q_r1, k + 1)
                v.tensor_scalar(wraw[:, k], wraw[:, k], BIG, 1.0, ALU.subtract, ALU.min).then_inc(q_r2, 1)
                v.wait_ge(q_r2, k + 1)
                if k:
                    v.wait_ge(q_tr, 2 * k)
                v.tensor_scalar(wqb, wraw[:, k], -1.0, None, ALU.max).then_inc(q_bf, 1)

            def pair_evac(i, p, used):
                v.wait_ge(m_bh, i + 1)
                v.scalar_tensor_tensor(wB[:, 1, i, :], bank[3][:, 0:D], S_B, wB[:, 0, i, :], ALU.mult, ALU.subtract).then_inc(m_be, 1)
                v.wait_ge(m_ah, i + 1)
                v.scalar_tensor_tensor(wA[:, 1, :, bass.ts(i, P)], bank[2][:, 0:2 * P].rearrange("p (c n) -> p c n", c=2),
                                       S_A, wA[:, 0, :, bass.ts(i, P)], ALU.mult, ALU.subtract).then_inc(m_ae, 1)

            ternary(0)
            pair_evac(0, 0, False)
            v.wait_ge(k_hi, 1)
            v.scalar_tensor_tensor(klT[0:64, :, :], kTf[0:64], S_K, khT[0:64, :, :], ALU.mult, ALU.subtract).then_inc(k_lo, 1)
            ternary(1)
            pair_evac(1, 1, False)
            ternary(2)
            with v.Fori(2, 6, 1) as i:
                pair_evac(i, 0, True)
            pair_evac(6, 0, True)
            v.wait_ge(w_hi, 1)
            v.scalar_tensor_tensor(w1T[:, 1], w1f, S_W1, w1T[:, 0], ALU.mult, ALU.subtract).then_inc(w_lo, 1)
            pair_evac(7, 1, True)
            v.wait_ge(w_hi, 2)
            v.scalar_tensor_tensor(w2T[:, 1], w2f, S_W2, w2T[:, 0], ALU.mult, ALU.subtract).then_inc(w_lo, 1)
            v.wait_ge(ld_w1, 48)
            for n in range(3):
                if n:
                    v.wait_ge(w_lo, 2 + 2 * n)
                v.tensor_scalar(b2s[:, n, :], b2f, S_H * S_W2 if n == 0 else 1.0, None, ALU.mult).then_inc(w_lo, 1)
                if n < 2:
                    v.wait_ge(w_lo, 3 + 2 * n)
                    v.scalar_tensor_tensor(b2f, b2f, S_H * S_W2 if n == 0 else 1.0, b2s[:, n, :],
                                           ALU.mult, ALU.subtract).then_inc(w_lo, 1)

            v.wait_ge(ld_x, N_X)
            v.wait_ge(tanh_done, 1)
            v.tensor_scalar(gam[:, 3:4], gam[:, 2:3], gT[:, 2:3], None, ALU.mult)
            v.tensor_scalar(bo[:, :], bo[:, :], gT[:, 2:3], None, ALU.mult)
            v.tensor_scalar(g3s[:, 0:1], gT[:, 1:2], 1.0 / (S_C * S_B), None, ALU.mult).then_inc(g_done, 1)
            v.tensor_scalar(g3s[:, 1:2], gT[:, 3:4], 1.0 / (S_H * S_W2), None, ALU.mult).then_inc(g_done, 1)
            v.wait_ge(m_ae, PAIRS1)
            v.wait_ge(m_be, PAIRS1)
            v.wait_ge(w_lo, 7)
            v.wait_ge(q_bias, 9)

            def a_max(j):
                def f(t, p, used):
                    if used and j == 0:
                        held(v, a_mt, t - 1)
                    b, gp = j // 2, j % 2
                    v.wait_ge(a_p1, 4 * t + j + 1)
                    v.tensor_reduce(mx1[:, p, gp, 8 * b:8 * b + 8], bank[1 + j % 2][:, :].rearrange("p (k n) -> p k n", k=8),
                                    AX.X, ALU.max).then_inc(a_mx, 1)
                return f

            def a_qlow(t, p, used):
                v.wait_ge(a_qe, 2 * t + 1)
                if used:
                    held(v, a_s, 4 * t - 4)
                v.tensor_tensor(qA[64:128, p].rearrange("p b g n -> p g b n"),
                                bank[0][0:64, :].rearrange("p (g b n) -> p g b n", g=4, b=2),
                                qA[0:64, p].rearrange("p b g n -> p g b n"), ALU.subtract).then_inc(a_ql, 1)

            def a_final(t, p, used):
                o = bank[7][:, :].rearrange("p (g k i) -> p g k i", g=4, k=8)
                rec = rec1[:, p].rearrange("p (g k) o -> p g k o", g=4)
                v.wait_ge(a_o, t + 1)
                v.reciprocal(rec, o[:, :, :, 8:9]).then_inc(a_rec, 1)
                v.wait_ge(a_rec, t + 1)
                att = att1[:, p].rearrange("p (k g) i -> p g k i", g=4)
                v.tensor_tensor(att, o[:, :, :, 0:8], rec.broadcast_to([P, 4, 8, 8]), ALU.mult).then_inc(a_att, 1)
                v.wait_ge(a_att, t + 1)
                v.scalar_tensor_tensor(xs[:, t, :], att1[:, p].rearrange("p h i -> p (h i)"), gT[:, 0:1], xs[:, t, :],
                                       ALU.mult, ALU.add).then_inc(a_x, 1)

            sums, moments, variance = stats(v, ln1)
            tiles_loop(v, D1, [sums, (5, a_final), moments, variance, (2, a_qlow),
                               (2, a_max(0)), (2, a_max(1)), (2, a_max(2)), (2, a_max(3))])

            v.wait_ge(a_x, TILES)
            v.wait_ge(q_ev, 6)

            def f_xmax(t, p, used):
                v.wait_ge(ln2.xn, ln2.base + t + 1)
                v.tensor_reduce(gx[:, p, 0:1], ln2.out[:, p, :], AX.X, ALU.max, apply_absolute_value=True).then_inc(f_ab, 1)

            def f_xclip(t, p, used):
                v.wait_ge(f_ab, t + 1)
                v.tensor_scalar(gx[:, p, 1:2], gx[:, p, 0:1], 1e-5, 1.0 / 127.0, ALU.max, ALU.mult).then_inc(f_c1, 1)

            def f_xscale(t, p, used):
                v.wait_ge(f_c1, t + 1)
                v.reciprocal(gx[:, p, 2:3], gx[:, p, 1:2]).then_inc(f_c2, 1)
                v.tensor_scalar(sg[:, p, :], gam[:, 0:2], gx[:, p, 1:2], None, ALU.mult).then_inc(f_sc, 1)

            def f_xround(t, p, used):
                v.wait_ge(f_c2, t + 1)
                if used:
                    held(v, f_tr, t - 1)
                v.tensor_scalar(xm[:, p, :], ln2.out[:, p, :], gx[:, p, 2:3], MAGIC, ALU.mult, ALU.add).then_inc(f_xm, 1)

            def f_hidden(t, p, used):
                if used:
                    v.wait_ge(f_hm, t - 1)
                for j in range(2):
                    part_j = slice(j * 512, (j + 1) * 512)
                    v.wait_ge(f_sil, 2 * t + j + 1)
                    v.wait_ge(f_vp, 2 * t + j + 1)
                    v.scalar_tensor_tensor(val[:, p, part_j], bank[3 + j][:, :], sg[:, p, 1:2], sil[:, p, part_j],
                                           ALU.mult, ALU.mult).then_inc(f_h, 1)
                v.wait_ge(f_h, 2 * t + 2)
                v.tensor_reduce(gh[:, p, 0:1], val[:, p], AX.X, ALU.max, apply_absolute_value=True).then_inc(f_ha, 1)
                v.wait_ge(f_ha, t + 1)
                v.tensor_scalar(gh[:, p, 1:2], gh[:, p, 0:1], 1e-5, 1.0 / 127.0, ALU.max, ALU.mult).then_inc(f_h1, 1)
                v.wait_ge(f_h1, t + 1)
                v.reciprocal(gh[:, p, 2:3], gh[:, p, 1:2]).then_inc(f_h2, 1)
                v.tensor_scalar(gh[:, p, 3:4], gh[:, p, 1:2], gam[:, 3:4], None, ALU.mult).then_inc(f_c3, 1)

            def f_final(t, p, used):
                v.wait_ge(f_o, t + 1)
                v.wait_ge(f_xb, t + 1)
                v.wait_ge(f_c3, t + 1)
                v.scalar_tensor_tensor(xs[:, t, :], bank[6][:, 0:D], gh[:, p, 3:4], xb[:, p], ALU.mult, ALU.add).then_inc(f_x, 1)

            sums, moments, variance = stats(v, ln2)
            tiles_loop(v, D2, [(2, f_xmax), sums, (2, f_xclip), moments, (2, f_xscale), variance, (2, f_xround),
                               (5, f_final), (3, f_hidden)])

            v.wait_ge(f_x, TILES)
            v.wait_ge(g_done, 4)
            for p in range(2):
                v.memset(rr3[:, p], 0.0).then_inc(l_z, 1)
            v.wait_ge(l_z, 2)

            def l_max(j):
                def f(t, p, used):
                    if used and j == 0:
                        held(v, l_mt, t - 1)
                    v.wait_ge(l_p1, 2 * t + j + 1)
                    v.tensor_reduce(mx3[:, p, 8 * j:8 * j + 8], bank[2][:, :].rearrange("p (k n) -> p k n", k=8),
                                    AX.X, ALU.max).then_inc(l_mx, 1)
                return f

            def l_tlow(t, p, used):
                v.wait_ge(l_te, t + 1)
                v.tensor_tensor(xT3[:, p, 1], bank[0][:, 0:2 * P].rearrange("p (c n) -> p c n", c=2), xT3[:, p, 0],
                                ALU.subtract).then_inc(l_tl, 1)

            def l_qlow(j):
                def f(t, p, used):
                    v.wait_ge(l_qe, 2 * t + j + 1)
                    v.scalar_tensor_tensor(qa[:, p, 1, 4 * j:4 * j + 4].rearrange("p k n -> p (k n)"), bank[1][:, :],
                                           S_L / (S_X * S_A), qa[:, p, 0, 4 * j:4 * j + 4].rearrange("p k n -> p (k n)"),
                                           ALU.mult, ALU.subtract).then_inc(l_ql, 1)
                return f

            def l_plow(b):
                def f(t, p, used):
                    v.wait_ge(l_ph, 2 * t + b + 1)
                    v.tensor_tensor(PT3[:, p, 1, b], PTf[:, b], PT3[:, p, 0, b], ALU.subtract).then_inc(l_pl, 1)
                return f

            def l_rsum(step):
                def f(t, p, used):
                    if step == 0:
                        v.wait_ge(l_sum, t + 1)
                        v.reciprocal(rs3[:, p], bank[0][0:16, D:D + P]).then_inc(l_rc, 1)
                    elif step == 1:
                        v.wait_ge(l_rc, t + 1)
                        if used:
                            held(v, l_rb, 2 * t - 2)
                        v.tensor_scalar(rr3[0:16, p], rs3[:, p], S_R, None, ALU.mult).then_inc(l_rh, 1)
                    else:
                        v.wait_ge(l_rh, t + 1)
                        v.scalar_tensor_tensor(rr3[32:48, p], rs3[:, p], S_R, rr3[0:16, p], ALU.mult, ALU.subtract).then_inc(l_rl, 1)
                return f

            def l_context(b):
                def f(t, p, used):
                    v.wait_ge(l_re, 2 * t + b + 1)
                    v.wait_ge(l_pv, 2 * t + b + 1)
                    v.scalar_tensor_tensor(cf[:, p, b], bank[5][:, :], S_C / (S_R * S_K), rb3[:, b],
                                           ALU.mult, ALU.mult).then_inc(l_c, 1)
                return f

            def l_clow(b):
                def f(t, p, used):
                    v.wait_ge(l_ch, 2 * t + b + 1)
                    half_b = slice(64 * b, 64 * b + 64)
                    v.tensor_tensor(cT[:, p, 1, :, half_b], cf[:, p, b].rearrange("p (k n) -> p k n", k=8),
                                    cT[:, p, 0, :, half_b], ALU.subtract).then_inc(l_cl, 1)
                return f

            def l_final(t, p, used):
                v.wait_ge(l_o, t + 1)
                v.scalar_tensor_tensor(xs[:, t, :], bank[7][:, 0:D], g3s[:, 0:1], xs[:, t, :], ALU.mult, ALU.add).then_inc(l_x, 1)

            sums, moments, variance = stats(v, ln3)
            tiles_loop(v, D3, [(2, l_qlow(0)), (4, l_rsum(0)), sums, (4, l_rsum(1)), moments, (4, l_rsum(2)), variance,
                               (2, l_max(0)), (3, l_plow(0)),
                               (5, l_final), (4, l_context(0)), (1, l_tlow), (4, l_clow(0)),
                               (2, l_qlow(1)), (4, l_context(1)), (2, l_max(1)), (3, l_plow(1)), (4, l_clow(1))])

            v.wait_ge(l_x, TILES)

            def e_route(t, p, used):
                v.wait_ge(e_sc, t + 1)
                v.scalar_tensor_tensor(sc4[:, p], bank[1][:, 0:8], 1.0 / (S_X * S_W1), gb8[:, 0, :], ALU.mult, ALU.add).then_inc(e_s1, 1)
                v.wait_ge(e_s1, t + 1)
                sj = sc4[:, p].unsqueeze(1).broadcast_to([P, 8, 8])
                se = sc4[:, p].unsqueeze(2).broadcast_to([P, 8, 8])
                v.tensor_tensor(gt[:, p], sj, se, ALU.is_gt).then_inc(e_rt, 1)
                v.tensor_tensor(eq[:, p], sj, se, ALU.is_equal).then_inc(e_rt, 1)
                v.wait_ge(e_rt, 7 * t + 2)
                v.tensor_tensor(eq[:, p], eq[:, p], before[:, :, :], ALU.mult).then_inc(e_rt, 1)
                v.wait_ge(e_rt, 7 * t + 3)
                v.tensor_tensor(gt[:, p], gt[:, p], eq[:, p], ALU.add).then_inc(e_rt, 1)
                v.wait_ge(e_rt, 7 * t + 4)
                v.tensor_reduce(rank[:, p], gt[:, p], AX.X, ALU.add).then_inc(e_rt, 1)
                v.wait_ge(e_rt, 7 * t + 5)
                v.tensor_scalar(half4[:, p], rank[:, p], 1.5, 0.5, ALU.is_lt, ALU.mult).then_inc(e_rt, 1)
                v.wait_ge(e_rt, 7 * t + 6)
                v.tensor_tensor(es4[:, p], half4[:, p], sc4[:, p], ALU.mult).then_inc(e_rt, 1)
                v.wait_ge(e_rt, 7 * t + 7)
                v.tensor_reduce(mid4[:, p], es4[:, p], AX.X, ALU.add).then_inc(e_md, 1)
                v.wait_ge(e_md, t + 1)
                if used:
                    held(v, e_th, t - 1)
                v.tensor_scalar(dif4[:, p], sc4[:, p], mid4[:, p], None, ALU.subtract).then_inc(e_rk, 1)

            def e_comb(t, p, used):
                v.wait_ge(e_th, t + 1)
                if used:
                    held(v, e_ct, t - 1)
                v.scalar_tensor_tensor(comb[:, p], th4[:, p], 1.0, half4[:, p], ALU.add, ALU.mult).then_inc(e_cc, 1)
                v.wait_ge(e_cc, 6 * t + 1)
                v.tensor_copy(cpart[:, p, 0:8], comb[:, p]).then_inc(e_cc, 1)
                v.wait_ge(e_cc, 6 * t + 2)
                v.tensor_tensor(cres[:, p, 0], comb[:, p], cpart[:, p, 0:8], ALU.subtract).then_inc(e_cc, 1)
                v.wait_ge(e_cc, 6 * t + 3)
                v.tensor_copy(cpart[:, p, 8:16], cres[:, p, 0]).then_inc(e_cc, 1)
                v.wait_ge(e_cc, 6 * t + 4)
                v.tensor_tensor(cres[:, p, 1], cres[:, p, 0], cpart[:, p, 8:16], ALU.subtract).then_inc(e_cc, 1)
                v.wait_ge(e_cc, 6 * t + 5)
                v.tensor_copy(cpart[:, p, 16:24], cres[:, p, 1]).then_inc(e_cc, 1)

            def e_tlow(t, p, used):
                v.wait_ge(e_te, t + 1)
                v.tensor_tensor(xT4[:, p, 1], bank[0][:, 0:2 * P].rearrange("p (c n) -> p c n", c=2), xT4[:, p, 0],
                                ALU.subtract).then_inc(e_tl, 1)

            def e_scale(c):
                def f(t, p, used):
                    j0, j1 = CHUNKS4[c]
                    v.wait_ge(e_sl, 3 * t + c + 1)
                    v.wait_ge(e_cb2, 3 * t + c + 1)
                    v.scalar_tensor_tensor(hf[:, p, j0 * P:j1 * P], sh4[:, p, j0 * P:j1 * P], S_H, bank[5 + (p + c) % 2][:, 0:(j1 - j0) * P],
                                           ALU.mult, ALU.mult).then_inc(e_hf, 1)
                return f

            def e_low(t, p, used):
                v.wait_ge(e_hh, t + 1)
                if used:
                    held(v, e_y, t - 1)
                v.tensor_tensor(hs[:, p, 1], hf[:, p], hs[:, p, 0], ALU.subtract).then_inc(e_hs, 1)

            def e_final(t, p, used):
                v.wait_ge(e_y, t + 1)
                v.scalar_tensor_tensor(xs[:, t, :], bank[7][:, 0:D], g3s[:, 1:2], xs[:, t, :], ALU.mult, ALU.add).then_inc(e_x, 1)

            sums, moments, variance = stats(v, ln4)
            tiles_loop(v, D4, [(3, e_comb), (4, e_low), sums, (5, e_final), moments, (2, e_tlow), variance,
                               (3, e_scale(0)), (3, e_scale(1)), (2, e_route), (3, e_scale(2))])


def constants():
    c = {}
    c["ident"] = np.eye(P, dtype=np.float32)
    r = np.arange(P)
    c["part"] = np.zeros((P, 2), np.float32)
    c["part"][:6] = [[0, 0], [-1, 0], [-1, -1], [0, 0], [-1, 0], [0, 0]]
    c["kvmask"] = ((r[:, None] % 64) // 8 == np.arange(8)[None, :]).astype(np.float32)
    c["rowhalf"] = (r[:, None] // 64 == np.arange(2)[None, :]).astype(np.float32)
    lomask = np.zeros((P, 2, 8), np.float32)
    lomask[:64] = c["kvmask"][:64, None, :]
    for b in range(2):
        for k in range(8):
            lomask[64 + 8 * b + k, b, k] = 1
    c["lomask"] = lomask
    sel1 = np.zeros((16, PAIRS1, P), np.float32)
    for pair in range(PAIRS1):
        for k in range(2):
            sel1[2 * pair + k, pair, 64 * k:64 * k + 64] = 1
    c["sel1"] = sel1
    unit = np.arange(EB * P) // EH
    c["sel3"] = np.tile((unit[None, :] == np.arange(8)[:, None]).astype(np.float32).reshape(8, EB, P), (3, 1, 1))
    c["selr"] = np.concatenate([sel1, np.zeros_like(sel1), sel1])
    cnt = np.zeros((P, PAIRS1, 16), np.float32)
    for pair in range(PAIRS1):
        for k in range(2):
            cnt[64 * k:64 * k + 64, pair, 2 * pair + k] = 1
    c["cnt"] = cnt
    f = np.float32
    inv = (f(1.0) / np.power(f(10000.0), np.arange(0, CD, 2, dtype=f) / f(CD), dtype=f)).astype(f)
    freqs = np.arange(SEQ, dtype=f)[:, None] * inv[None, :]
    sin = np.repeat(np.sin(freqs), 2, axis=-1).astype(f)
    cos = np.repeat(np.cos(freqs), 2, axis=-1).astype(f)
    sign = np.where(np.arange(CD) < CD // 2, -1, 1).astype(f)
    def diagonal(a):
        return (S_K * np.kron(np.eye(2, dtype=f), a)).reshape(P, 2, 64).astype(f)

    c["cosN"], c["sinN"] = diagonal(cos), diagonal(sin * sign)
    c["cosT"], c["sinT"] = diagonal(cos.T), diagonal((sin * sign).T)
    c["before"] = np.broadcast_to((np.arange(8)[None, :] < np.arange(8)[:, None]).astype(np.float32), (P, 8, 8))
    return c


def kernel(x, ctx_512, g_xattn, g_ffn, L0_ffn_gate_w, L0_ffn_gate_b, L0_ffn_val_w, L0_ffn_val_b, L0_ffn_out_w,
           L0_ffn_out_b, L1_xattn_Wq, L1_xattn_w_kc_q, L1_xattn_w_kc_kv, L1_xattn_W_qr, L1_xattn_W_kr, L1_xattn_Wo,
           L1_ffn_gate_w, L1_ffn_gate_b, L1_ffn_bias, L1_ffn_w1, L1_ffn_b1, L1_ffn_w2, L1_ffn_b2):
    import concourse.bacc as bacc
    from concourse.bass_utils import run_bass_kernel_spmd

    arrays = dict(constants())
    ctx = np.asarray(ctx_512)
    ctxT = ctx.transpose(2, 0, 1)
    arrays.update(
        x=np.asarray(x).reshape(BATCH * SEQ, D),
        ctx=ctx, ctxT=ctxT, ctxTs=np.concatenate([ctxT[32:], ctxT[:32]]),
        g=np.broadcast_to(np.concatenate([np.asarray(g_xattn), np.asarray(g_ffn)])[None, :], (P, 4)),
        gw=np.asarray(L0_ffn_gate_w), vw=np.asarray(L0_ffn_val_w),
        ow=np.asarray(L0_ffn_out_w).reshape(2, P, HID).reshape(2 * P, HID),
        bg=np.asarray(L0_ffn_gate_b)[None, :], bv=np.asarray(L0_ffn_val_b)[None, :], bo=np.asarray(L0_ffn_out_b)[None, :],
        Wq=np.asarray(L1_xattn_Wq).reshape(HEADS1, KD, D), Cq=np.asarray(L1_xattn_w_kc_q),
        Dq=np.asarray(L1_xattn_W_qr), ET=np.asarray(L1_xattn_W_kr).transpose(0, 2, 1),
        Ckv=np.asarray(L1_xattn_w_kc_kv), WoT=np.asarray(L1_xattn_Wo).T.reshape(HEADS1, KD, D),
        gwT=np.asarray(L1_ffn_gate_w).T.reshape(2, P, EXPERTS).transpose(1, 0, 2),
        gb=np.asarray(L1_ffn_gate_b)[None, :], gbias=np.asarray(L1_ffn_bias)[None, :],
        w1T=np.asarray(L1_ffn_w1).reshape(EXPERTS * EH, D).T.reshape(2, P, EXPERTS * EH).transpose(1, 0, 2),
        b1=np.asarray(L1_ffn_b1).reshape(EB, P).T,
        w2T=np.asarray(L1_ffn_w2).transpose(0, 2, 1).reshape(EB, P, D).transpose(1, 0, 2),
        b2=np.tile(np.asarray(L1_ffn_b2), (3, 1)),
    )
    arrays = {f"in_{k}": np.ascontiguousarray(v) for k, v in arrays.items()}
    nc = bacc.Bacc("TRN2", target_bir_lowering=False, num_devices=1)
    d = {k[3:]: nc.dram_tensor(k, v.shape, mybir.dt.from_np(v.dtype), kind="ExternalInput").ap()
         for k, v in arrays.items()}
    out = nc.dram_tensor("out", (BATCH * SEQ, D), F32, kind="ExternalOutput").ap()
    build(nc, d, out)
    got = run_bass_kernel_spmd(nc, [arrays], core_ids=[0])
    return got.results[0]["out"].reshape(BATCH, SEQ, D)
```
